# Optimizing a Trainium2 kernel written in Bass

```python
import numpy as np
import jax
import jax.numpy as jnp

def _softmax(x, axis=-1):
    return jax.nn.softmax(x, axis=axis)

def _gelu(x):
    return jax.nn.gelu(x, approximate=True)

def _silu(x):
    return jax.nn.silu(x)

def _sigmoid(x):
    return jax.nn.sigmoid(x)

def _layernorm(x, axis=-1, eps=1e-05):
    m = jnp.mean(x, axis=axis, keepdims=True)
    v = jnp.var(x, axis=axis, keepdims=True)
    return (x - m) / jnp.sqrt(v + eps)

def _scatter_add(tgt, idx, src, axis=0):
    return tgt.at[idx].add(src)

def _segment_sum(src, seg, n):
    return jax.ops.segment_sum(src, seg, n)
kernel_name = 'mk_conv_preact_d4_conv_nchw32_r2_423868'

def setup_inputs(seed: int=0):
    np.random.seed(seed)
    _w = jnp.asarray

    def _rec_inputs():
        import jax
        import jax.numpy as jnp
        _gk = jax.random.key(seed)
        x = -0.0003929 + 0.9999 * jax.random.normal(jax.random.fold_in(_gk, 1), (8, 32, 128, 128), jnp.float32)
        return x
    x = _rec_inputs()

    def _L0_conv_setup():
        import jax, jax.numpy as jnp
        import numpy as np
        B, C_IN, C_OUT, H, W = (8, 32, 32, 128, 128)
        M1H, M2H = (32, 32)
        WSCALE = 0.02
        key = jax.random.key(seed)
        ks = jax.random.split(key, 6)
        wshape = (C_IN, C_OUT, M1H, M2H)
        return {'x': jax.random.normal(ks[0], (B, C_IN, H, W), jnp.float32), 'w1r': jax.random.normal(ks[1], wshape, jnp.float32) * WSCALE, 'w1i': jax.random.normal(ks[2], wshape, jnp.float32) * WSCALE, 'w2r': jax.random.normal(ks[3], wshape, jnp.float32) * WSCALE, 'w2i': jax.random.normal(ks[4], wshape, jnp.float32) * WSCALE, 'bias': jax.random.normal(ks[5], (1, C_OUT, 1, 1), jnp.float32)}
    _L0_conv_all = _L0_conv_setup()
    _L0_conv_in = {k: v for k, v in _L0_conv_all.items() if k in ('w1r', 'w1i', 'w2r', 'w2i', 'bias')}
    del _L0_conv_all

    def _L1_conv_setup():
        import jax, jax.numpy as jnp
        import numpy as np
        from jax import lax
        BN_EPS = 1e-05
        key = jax.random.key(seed)
        k1, k2, k3, k4 = jax.random.split(key, 4)
        B, C_in, C_out, T, N, K = (16, 32, 32, 128, 128, 3)
        x = jax.random.normal(k1, (B, C_in, T, N), dtype=jnp.float32)
        A = jax.random.uniform(k2, (N, N), dtype=jnp.float32)
        conv_w = jax.random.normal(k3, (C_out, C_in, K, 1), dtype=jnp.float32) * (1.0 / np.sqrt(C_in * K))
        conv_b = jax.random.normal(k4, (C_out,), dtype=jnp.float32) * 0.01
        gamma = jnp.ones((C_out,), dtype=jnp.float32)
        beta = jnp.zeros((C_out,), dtype=jnp.float32)
        return {'x': x, 'A': A, 'conv_w': conv_w, 'conv_b': conv_b, 'gamma': gamma, 'beta': beta}
    _L1_conv_all = _L1_conv_setup()
    _L1_conv_in = {k: v for k, v in _L1_conv_all.items() if k in ('A', 'conv_w', 'conv_b', 'gamma', 'beta')}
    del _L1_conv_all

    def _L2_conv_setup():
        import jax, jax.numpy as jnp
        import numpy as np
        from jax import lax
        B, C, O, K, H, W = (4, 32, 32, 9, 128, 128)
        EPS = 1e-05

        def conv2d(x, w, b=None, stride=1, padding=1, groups=1):
            out = lax.conv_general_dilated(x, w, (stride, stride), [(padding, padding)] * 2, dimension_numbers=('NCHW', 'OIHW', 'NCHW'), feature_group_count=groups)
            if b is not None:
                out = out + b[None, :, None, None]
            return out

        def batchnorm(x, g, b):
            mean = jnp.mean(x, axis=(0, 2, 3), keepdims=True)
            var = jnp.var(x, axis=(0, 2, 3), keepdims=True)
            return (x - mean) * lax.rsqrt(var + EPS) * g[None, :, None, None] + b[None, :, None, None]

        def grid_sample_zeros(img, ix, iy):
            Bi, Ci, Hi, Wi = img.shape
            x0 = jnp.floor(ix)
            y0 = jnp.floor(iy)
            x1 = x0 + 1.0
            y1 = y0 + 1.0
            wx1 = ix - x0
            wx0 = 1.0 - wx1
            wy1 = iy - y0
            wy0 = 1.0 - wy1
            imgf = img.reshape(Bi, Ci, Hi * Wi)

            def corner(xc, yc, w):
                valid = (xc >= 0) & (xc <= Wi - 1) & (yc >= 0) & (yc <= Hi - 1)
                xi = jnp.clip(xc, 0, Wi - 1).astype(jnp.int32)
                yi = jnp.clip(yc, 0, Hi - 1).astype(jnp.int32)
                idx = yi * Wi + xi
                vals = jax.vmap(lambda im, id_: im[:, id_])(imgf, idx)
                return vals * (w * valid.astype(w.dtype))[:, None]
            return corner(x0, y0, wx0 * wy0) + corner(x1, y0, wx1 * wy0) + corner(x0, y1, wx0 * wy1) + corner(x1, y1, wx1 * wy1)

        def dsc_axis(x, offset, weight, axis):
            Bi, Ci, Hi, Wi = x.shape
            off = jnp.transpose(offset, (0, 2, 3, 1))
            hb = jnp.arange(Hi, dtype=x.dtype)[None, :, None, None]
            wb = jnp.arange(Wi, dtype=x.dtype)[None, None, :, None]
            if axis == 'x':
                ix = wb + off
                iy = jnp.broadcast_to(hb, off.shape)
            else:
                iy = hb + off
                ix = jnp.broadcast_to(wb, off.shape)
            s = grid_sample_zeros(x, ix, iy)
            return jnp.einsum('bchwk,ock->bohw', s, weight)

        def offset_branch(x, dw_w, dw_b, bn_g, bn_b, pw_w, pw_b):
            h = conv2d(x, dw_w, dw_b, padding=1, groups=x.shape[1])
            h = jax.nn.relu(batchnorm(h, bn_g, bn_b))
            return conv2d(h, pw_w, pw_b, padding=0)
        key = jax.random.key(seed)
        ks = jax.random.split(key, 16)
        n = lambda k, sh, s: jax.random.normal(k, sh, dtype=jnp.float32) * s
        d = {}
        d['x'] = n(ks[0], (B, C, H, W), 1.0)
        d['conv_w'] = n(ks[1], (O, C, 3, 3), (2.0 / (C * 9)) ** 0.5)
        d['conv_b'] = jnp.zeros((O,), jnp.float32)
        d['offx_dw_w'] = n(ks[2], (C, 1, 3, 3), 0.3)
        d['offx_dw_b'] = jnp.zeros((C,), jnp.float32)
        d['offx_bn_g'] = jnp.ones((C,), jnp.float32)
        d['offx_bn_b'] = jnp.zeros((C,), jnp.float32)
        d['offx_pw_w'] = n(ks[3], (K, C, 1, 1), 0.1)
        d['offx_pw_b'] = n(ks[4], (K,), 0.1)
        d['offy_dw_w'] = n(ks[5], (C, 1, 3, 3), 0.3)
        d['offy_dw_b'] = jnp.zeros((C,), jnp.float32)
        d['offy_bn_g'] = jnp.ones((C,), jnp.float32)
        d['offy_bn_b'] = jnp.zeros((C,), jnp.float32)
        d['offy_pw_w'] = n(ks[6], (K, C, 1, 1), 0.1)
        d['offy_pw_b'] = n(ks[7], (K,), 0.1)
        d['dscx_w'] = n(ks[8], (O, C, K), (2.0 / (C * K)) ** 0.5)
        d['dscy_w'] = n(ks[9], (O, C, K), (2.0 / (C * K)) ** 0.5)
        d['fus_w'] = n(ks[10], (O, 3 * O, 1, 1), (2.0 / (3 * O)) ** 0.5)
        d['fus_bn_g'] = jnp.ones((O,), jnp.float32)
        d['fus_bn_b'] = jnp.zeros((O,), jnp.float32)
        return d
    _L2_conv_all = _L2_conv_setup()
    _L2_conv_in = {k: v for k, v in _L2_conv_all.items() if k in ('conv_w', 'conv_b', 'offx_dw_w', 'offx_dw_b', 'offx_bn_g', 'offx_bn_b', 'offx_pw_w', 'offx_pw_b', 'offy_dw_w', 'offy_dw_b', 'offy_bn_g', 'offy_bn_b', 'offy_pw_w', 'offy_pw_b', 'dscx_w', 'dscy_w', 'fus_w', 'fus_bn_g', 'fus_bn_b')}
    del _L2_conv_all

    def _L3_conv_setup():
        import math
        import jax, jax.numpy as jnp
        import numpy as np
        K = 3
        ROTATIONS = np.array([i * math.pi / 4.0 for i in range(8)], dtype=np.float32)
        SCALES = np.array([1.0, 1.25, 1.25 ** 2, 1.25 ** 3], dtype=np.float32)

        def _spatial_kernel(freq_weight):
            cw = freq_weight[..., 0] + 1j * freq_weight[..., 1]
            return jnp.fft.irfft2(cw, s=(K, K), axes=(-2, -1))

        def _transform_kernel(kernel, cos_t, sin_t):
            k = K
            coords = (2.0 * jnp.arange(k, dtype=kernel.dtype) + 1.0) / k - 1.0
            gy_out, gx_out = jnp.meshgrid(coords, coords, indexing='ij')
            gx = cos_t * gx_out - sin_t * gy_out
            gy = sin_t * gx_out + cos_t * gy_out
            ix = ((gx + 1.0) * k - 1.0) * 0.5
            iy = ((gy + 1.0) * k - 1.0) * 0.5
            x0 = jnp.floor(ix).astype(jnp.int32)
            y0 = jnp.floor(iy).astype(jnp.int32)
            x1, y1 = (x0 + 1, y0 + 1)
            wx1 = ix - x0.astype(kernel.dtype)
            wy1 = iy - y0.astype(kernel.dtype)
            wx0, wy0 = (1.0 - wx1, 1.0 - wy1)

            def tap(yy, xx):
                valid = (xx >= 0) & (xx < k) & (yy >= 0) & (yy < k)
                v = kernel[..., jnp.clip(yy, 0, k - 1), jnp.clip(xx, 0, k - 1)]
                return jnp.where(valid, v, jnp.zeros((), kernel.dtype))
            return tap(y0, x0) * (wy0 * wx0) + tap(y0, x1) * (wy0 * wx1) + tap(y1, x0) * (wy1 * wx0) + tap(y1, x1) * (wy1 * wx1)

        def _equivariant_kernel(freq_weight):
            base = _spatial_kernel(freq_weight)
            th = jnp.asarray(ROTATIONS)[:, None]
            sc = jnp.asarray(SCALES)[None, :]
            cos_t = (jnp.cos(th) * sc).reshape(-1)
            sin_t = (jnp.sin(th) * sc).reshape(-1)
            kernels = jax.vmap(lambda c, s: _transform_kernel(base, c, s))(cos_t, sin_t)
            return kernels.mean(axis=0)
        key = jax.random.key(seed)
        k1, k2 = jax.random.split(key)
        x = jax.random.normal(k1, (8, 32, 256, 256), dtype=jnp.float32)
        freq_weight = jax.random.normal(k2, (32, 32, K, K // 2 + 1, 2), dtype=jnp.float32) * 0.02
        return {'x': x, 'freq_weight': freq_weight}
    _L3_conv_all = _L3_conv_setup()
    _L3_conv_in = {k: v for k, v in _L3_conv_all.items() if k in ('freq_weight',)}
    del _L3_conv_all
    return {'x': x, 'L0_conv_w1r': _L0_conv_in['w1r'], 'L0_conv_w1i': _L0_conv_in['w1i'], 'L0_conv_w2r': _L0_conv_in['w2r'], 'L0_conv_w2i': _L0_conv_in['w2i'], 'L0_conv_bias': _L0_conv_in['bias'], 'L1_conv_A': _L1_conv_in['A'], 'L1_conv_conv_w': _L1_conv_in['conv_w'], 'L1_conv_conv_b': _L1_conv_in['conv_b'], 'L1_conv_gamma': _L1_conv_in['gamma'], 'L1_conv_beta': _L1_conv_in['beta'], 'L2_conv_conv_w': _L2_conv_in['conv_w'], 'L2_conv_conv_b': _L2_conv_in['conv_b'], 'L2_conv_offx_dw_w': _L2_conv_in['offx_dw_w'], 'L2_conv_offx_dw_b': _L2_conv_in['offx_dw_b'], 'L2_conv_offx_bn_g': _L2_conv_in['offx_bn_g'], 'L2_conv_offx_bn_b': _L2_conv_in['offx_bn_b'], 'L2_conv_offx_pw_w': _L2_conv_in['offx_pw_w'], 'L2_conv_offx_pw_b': _L2_conv_in['offx_pw_b'], 'L2_conv_offy_dw_w': _L2_conv_in['offy_dw_w'], 'L2_conv_offy_dw_b': _L2_conv_in['offy_dw_b'], 'L2_conv_offy_bn_g': _L2_conv_in['offy_bn_g'], 'L2_conv_offy_bn_b': _L2_conv_in['offy_bn_b'], 'L2_conv_offy_pw_w': _L2_conv_in['offy_pw_w'], 'L2_conv_offy_pw_b': _L2_conv_in['offy_pw_b'], 'L2_conv_dscx_w': _L2_conv_in['dscx_w'], 'L2_conv_dscy_w': _L2_conv_in['dscy_w'], 'L2_conv_fus_w': _L2_conv_in['fus_w'], 'L2_conv_fus_bn_g': _L2_conv_in['fus_bn_g'], 'L2_conv_fus_bn_b': _L2_conv_in['fus_bn_b'], 'L3_conv_freq_weight': _L3_conv_in['freq_weight']}

def reference(x, L0_conv_w1r, L0_conv_w1i, L0_conv_w2r, L0_conv_w2i, L0_conv_bias, L1_conv_A, L1_conv_conv_w, L1_conv_conv_b, L1_conv_gamma, L1_conv_beta, L2_conv_conv_w, L2_conv_conv_b, L2_conv_offx_dw_w, L2_conv_offx_dw_b, L2_conv_offx_bn_g, L2_conv_offx_bn_b, L2_conv_offx_pw_w, L2_conv_offx_pw_b, L2_conv_offy_dw_w, L2_conv_offy_dw_b, L2_conv_offy_bn_g, L2_conv_offy_bn_b, L2_conv_offy_pw_w, L2_conv_offy_pw_b, L2_conv_dscx_w, L2_conv_dscy_w, L2_conv_fus_w, L2_conv_fus_bn_g, L2_conv_fus_bn_b, L3_conv_freq_weight):
    import jax
    import jax.numpy as jnp

    def _L0_conv_ref(x, w1r, w1i, w2r, w2i, bias):
        import jax, jax.numpy as jnp
        import numpy as np
        B, C_IN, C_OUT, H, W = (8, 32, 32, 128, 128)
        M1H, M2H = (32, 32)
        WSCALE = 0.02
        w1 = w1r + 1j * w1i
        w2 = w2r + 1j * w2i
        b, c, h, w = x.shape
        x_ft = jnp.fft.rfft2(x)
        out_lo = jnp.einsum('bixy,ioxy->boxy', x_ft[:, :, :M1H, :M2H], w1)
        out_hi = jnp.einsum('bixy,ioxy->boxy', x_ft[:, :, -M1H:, :M2H], w2)
        out_ft = jnp.zeros((b, w1.shape[1], h, w // 2 + 1), jnp.complex64)
        out_ft = out_ft.at[:, :, :M1H, :M2H].set(out_lo)
        out_ft = out_ft.at[:, :, -M1H:, :M2H].set(out_hi)
        out = jnp.fft.irfft2(out_ft, s=(h, w))
        return out + bias

    def _L1_conv_ref(x, A, conv_w, conv_b, gamma, beta):
        import jax, jax.numpy as jnp
        import numpy as np
        from jax import lax
        BN_EPS = 1e-05
        K = conv_w.shape[2]
        pad = (K - 1) // 2
        y = lax.conv_general_dilated(x, conv_w, window_strides=(1, 1), padding=((pad, pad), (0, 0)), dimension_numbers=('NCHW', 'OIHW', 'NCHW'))
        y = jax.nn.relu(y + conv_b[None, :, None, None])
        y = jnp.einsum('bctn,nm->bctm', y, A)
        mean = jnp.mean(y, axis=(0, 2, 3), keepdims=True)
        var = jnp.var(y, axis=(0, 2, 3), keepdims=True)
        y = (y - mean) * lax.rsqrt(var + BN_EPS)
        y = y * gamma[None, :, None, None] + beta[None, :, None, None]
        return jax.nn.relu(y)

    def _L2_conv_ref(x, conv_w, conv_b, offx_dw_w, offx_dw_b, offx_bn_g, offx_bn_b, offx_pw_w, offx_pw_b, offy_dw_w, offy_dw_b, offy_bn_g, offy_bn_b, offy_pw_w, offy_pw_b, dscx_w, dscy_w, fus_w, fus_bn_g, fus_bn_b):
        import jax, jax.numpy as jnp
        import numpy as np
        from jax import lax
        B, C, O, K, H, W = (4, 32, 32, 9, 128, 128)
        EPS = 1e-05

        def conv2d(x, w, b=None, stride=1, padding=1, groups=1):
            out = lax.conv_general_dilated(x, w, (stride, stride), [(padding, padding)] * 2, dimension_numbers=('NCHW', 'OIHW', 'NCHW'), feature_group_count=groups)
            if b is not None:
                out = out + b[None, :, None, None]
            return out

        def batchnorm(x, g, b):
            mean = jnp.mean(x, axis=(0, 2, 3), keepdims=True)
            var = jnp.var(x, axis=(0, 2, 3), keepdims=True)
            return (x - mean) * lax.rsqrt(var + EPS) * g[None, :, None, None] + b[None, :, None, None]

        def grid_sample_zeros(img, ix, iy):
            Bi, Ci, Hi, Wi = img.shape
            x0 = jnp.floor(ix)
            y0 = jnp.floor(iy)
            x1 = x0 + 1.0
            y1 = y0 + 1.0
            wx1 = ix - x0
            wx0 = 1.0 - wx1
            wy1 = iy - y0
            wy0 = 1.0 - wy1
            imgf = img.reshape(Bi, Ci, Hi * Wi)

            def corner(xc, yc, w):
                valid = (xc >= 0) & (xc <= Wi - 1) & (yc >= 0) & (yc <= Hi - 1)
                xi = jnp.clip(xc, 0, Wi - 1).astype(jnp.int32)
                yi = jnp.clip(yc, 0, Hi - 1).astype(jnp.int32)
                idx = yi * Wi + xi
                vals = jax.vmap(lambda im, id_: im[:, id_])(imgf, idx)
                return vals * (w * valid.astype(w.dtype))[:, None]
            return corner(x0, y0, wx0 * wy0) + corner(x1, y0, wx1 * wy0) + corner(x0, y1, wx0 * wy1) + corner(x1, y1, wx1 * wy1)

        def dsc_axis(x, offset, weight, axis):
            Bi, Ci, Hi, Wi = x.shape
            off = jnp.transpose(offset, (0, 2, 3, 1))
            hb = jnp.arange(Hi, dtype=x.dtype)[None, :, None, None]
            wb = jnp.arange(Wi, dtype=x.dtype)[None, None, :, None]
            if axis == 'x':
                ix = wb + off
                iy = jnp.broadcast_to(hb, off.shape)
            else:
                iy = hb + off
                ix = jnp.broadcast_to(wb, off.shape)
            s = grid_sample_zeros(x, ix, iy)
            return jnp.einsum('bchwk,ock->bohw', s, weight)

        def offset_branch(x, dw_w, dw_b, bn_g, bn_b, pw_w, pw_b):
            h = conv2d(x, dw_w, dw_b, padding=1, groups=x.shape[1])
            h = jax.nn.relu(batchnorm(h, bn_g, bn_b))
            return conv2d(h, pw_w, pw_b, padding=0)
        out_standard = conv2d(x, conv_w, conv_b, padding=1)
        offset_x = offset_branch(x, offx_dw_w, offx_dw_b, offx_bn_g, offx_bn_b, offx_pw_w, offx_pw_b)
        offset_y = offset_branch(x, offy_dw_w, offy_dw_b, offy_bn_g, offy_bn_b, offy_pw_w, offy_pw_b)
        out_x = dsc_axis(x, offset_x, dscx_w, 'x')
        out_y = dsc_axis(x, offset_y, dscy_w, 'y')
        out = jnp.concatenate([out_standard, out_x, out_y], axis=1)
        out = conv2d(out, fus_w, None, padding=0)
        return jax.nn.relu(batchnorm(out, fus_bn_g, fus_bn_b))

    def _L3_conv_ref(x, freq_weight):
        import math
        import jax, jax.numpy as jnp
        import numpy as np
        K = 3
        ROTATIONS = np.array([i * math.pi / 4.0 for i in range(8)], dtype=np.float32)
        SCALES = np.array([1.0, 1.25, 1.25 ** 2, 1.25 ** 3], dtype=np.float32)

        def _spatial_kernel(freq_weight):
            cw = freq_weight[..., 0] + 1j * freq_weight[..., 1]
            return jnp.fft.irfft2(cw, s=(K, K), axes=(-2, -1))

        def _transform_kernel(kernel, cos_t, sin_t):
            k = K
            coords = (2.0 * jnp.arange(k, dtype=kernel.dtype) + 1.0) / k - 1.0
            gy_out, gx_out = jnp.meshgrid(coords, coords, indexing='ij')
            gx = cos_t * gx_out - sin_t * gy_out
            gy = sin_t * gx_out + cos_t * gy_out
            ix = ((gx + 1.0) * k - 1.0) * 0.5
            iy = ((gy + 1.0) * k - 1.0) * 0.5
            x0 = jnp.floor(ix).astype(jnp.int32)
            y0 = jnp.floor(iy).astype(jnp.int32)
            x1, y1 = (x0 + 1, y0 + 1)
            wx1 = ix - x0.astype(kernel.dtype)
            wy1 = iy - y0.astype(kernel.dtype)
            wx0, wy0 = (1.0 - wx1, 1.0 - wy1)

            def tap(yy, xx):
                valid = (xx >= 0) & (xx < k) & (yy >= 0) & (yy < k)
                v = kernel[..., jnp.clip(yy, 0, k - 1), jnp.clip(xx, 0, k - 1)]
                return jnp.where(valid, v, jnp.zeros((), kernel.dtype))
            return tap(y0, x0) * (wy0 * wx0) + tap(y0, x1) * (wy0 * wx1) + tap(y1, x0) * (wy1 * wx0) + tap(y1, x1) * (wy1 * wx1)

        def _equivariant_kernel(freq_weight):
            base = _spatial_kernel(freq_weight)
            th = jnp.asarray(ROTATIONS)[:, None]
            sc = jnp.asarray(SCALES)[None, :]
            cos_t = (jnp.cos(th) * sc).reshape(-1)
            sin_t = (jnp.sin(th) * sc).reshape(-1)
            kernels = jax.vmap(lambda c, s: _transform_kernel(base, c, s))(cos_t, sin_t)
            return kernels.mean(axis=0)
        kern = _equivariant_kernel(freq_weight)
        pad = K // 2
        return jax.lax.conv_general_dilated(x, kern, window_strides=(1, 1), padding=[(pad, pad), (pad, pad)], dimension_numbers=('NCHW', 'OIHW', 'NCHW'))

    def _gn(v, G=16, eps=1e-05):
        B_, C_, H_, W_ = v.shape
        g = v.reshape(B_, G, C_ // G, H_, W_)
        m = jnp.mean(g, axis=(2, 3, 4), keepdims=True)
        s = jnp.var(g, axis=(2, 3, 4), keepdims=True)
        return ((g - m) / jnp.sqrt(s + eps)).reshape(v.shape)

    def _ln_c(v, eps=1e-06):
        m = jnp.mean(v, axis=1, keepdims=True)
        s = jnp.var(v, axis=1, keepdims=True)
        return (v - m) / jnp.sqrt(s + eps)

    def _ln_t(v, eps=1e-05):
        m = jnp.mean(v, axis=-1, keepdims=True)
        s = jnp.var(v, axis=-1, keepdims=True)
        return (v - m) / jnp.sqrt(s + eps)

    def _to_tokens(v):
        B_, C_, H_, W_ = v.shape
        return v.reshape(B_, C_, H_ * W_).transpose(0, 2, 1)

    def _from_tokens(t, like):
        B_, C_, H_, W_ = like.shape
        return t.transpose(0, 2, 1).reshape(B_, C_, H_, W_)
    x = x + _L0_conv_ref(_gn(x), L0_conv_w1r, L0_conv_w1i, L0_conv_w2r, L0_conv_w2i, L0_conv_bias)
    x = x + _L1_conv_ref(_gn(x), L1_conv_A, L1_conv_conv_w, L1_conv_conv_b, L1_conv_gamma, L1_conv_beta)
    x = x + _L2_conv_ref(_gn(x), L2_conv_conv_w, L2_conv_conv_b, L2_conv_offx_dw_w, L2_conv_offx_dw_b, L2_conv_offx_bn_g, L2_conv_offx_bn_b, L2_conv_offx_pw_w, L2_conv_offx_pw_b, L2_conv_offy_dw_w, L2_conv_offy_dw_b, L2_conv_offy_bn_g, L2_conv_offy_bn_b, L2_conv_offy_pw_w, L2_conv_offy_pw_b, L2_conv_dscx_w, L2_conv_dscy_w, L2_conv_fus_w, L2_conv_fus_bn_g, L2_conv_fus_bn_b)
    x = x + _L3_conv_ref(_gn(x), L3_conv_freq_weight)
    return x

_drawn_inputs = setup_inputs


def setup_inputs(seed=0):
    import zlib

    import numpy as np

    out = dict(_drawn_inputs(seed))
    spreads = {'L1_conv_gamma': (1.0, 0.2),
     'L1_conv_beta': (0.0, 0.1),
     'L2_conv_conv_b': (0.0, 0.8),
     'L2_conv_offx_dw_b': (0.0, 0.8),
     'L2_conv_offx_bn_g': (1.0, 0.6),
     'L2_conv_offx_bn_b': (0.0, 0.753),
     'L2_conv_offy_dw_b': (0.0, 0.8),
     'L2_conv_offy_bn_g': (1.0, 0.6),
     'L2_conv_offy_bn_b': (0.0, 0.442),
     'L2_conv_fus_bn_g': (1.0, 0.2),
     'L2_conv_fus_bn_b': (0.0, 0.1)}
    factors = {'L1_conv_conv_b': 8.0}
    for name, (base, spread) in spreads.items():
        noise = np.random.default_rng([zlib.crc32(name.encode()), seed]).standard_normal(out[name].shape)
        drawn = base * np.exp(spread * noise) if base else spread * noise
        out[name] = jnp.asarray(drawn.astype(out[name].dtype))
    for name, factor in factors.items():
        out[name] = (out[name] * factor).astype(out[name].dtype)
    return out
```

```python
from contextlib import ExitStack

import numpy as np

import concourse.bass as bass
from concourse import mybir

F32 = mybir.dt.float32
BF16 = mybir.dt.bfloat16
ALU = mybir.AluOpType
ACT = mybir.ActivationFunctionType

B, C, H, W = 8, 32, 128, 128
P = 128
PX = H * W
G = 16
M1, M2 = 32, 32
KX = 2 * M1
K9 = 9
EPS = 1e-5


class Chain:

    def __init__(self, eng, sem, base=0):
        self.eng, self.sem, self.base, self.n = eng, sem, base, 0

    def done(self, ins):
        ins.then_inc(self.sem, 1)
        self.n += 1

    def sync(self):
        self.eng.wait_ge(self.sem, self.base + self.n)


def alone(eng, passed):
    eng.sem_inc(passed, 1)


def one(ap, i):
    dims = "abcdefg"[:len(ap.shape)]
    left = " ".join(dims)
    right = "(" + " ".join(dims[:2]) + ") " + " ".join(dims[2:])
    return ap[(bass.ds(i, 1),) + (slice(None),) * (len(dims) - 1)].rearrange(f"{left} -> {right}")


class Stage:

    def __init__(self, nc, sems, name):
        self.nc, self.sems, self.name, self.ctx = nc, sems, name, ExitStack()

    def __enter__(self):
        return self

    def __exit__(self, *e):
        self.ctx.close()

    def sb(self, name, shape, dt=F32):
        return self.ctx.enter_context(self.nc.sbuf_tensor(f"{self.name}_{name}", shape, dt))

    def ps(self, name, shape):
        return self.ctx.enter_context(self.nc.psum_tensor(f"{self.name}_{name}", shape, F32))

    def sem(self, name):
        return self.sems.enter_context(self.nc.semaphore(f"{self.name}_{name}"))

    def block(self):
        return self.nc.Block()



def spectral_forward(nc, sems, x, consts, F):
    with Stage(nc, sems, "fw") as s:
        X = s.sb("x", [P, 2, C, W])
        rows = s.sb("rows", [P, KX * 3, C])
        dh = s.sb("dh", [P, KX * 3])
        dwp = s.sb("dwp", [P, 2 * M2])
        dwq = s.sb("dwq", [P, 2 * M2])
        avg = s.sb("avg", [P, P])
        st = s.sb("st", [P, G, 6])
        ag = s.sb("ag", [P, G, 2])
        mean = s.sb("mean", [P, G])
        dev = s.sb("dev", [P, G])
        rstd = s.sb("rstd", [P, G])
        ps_s = s.ps("s", [P, 512])
        ps_r = [s.ps(f"r{k}", [P, 512]) for k in range(2)]
        ps_f = [s.ps(f"f{k}", [P, 512]) for k in range(2)]
        c_in, passed = s.sem("c_in"), s.sem("passed")
        x_in = [s.sem(f"x_in{k}") for k in range(2)]
        stats, sums, rooted, normed = s.sem("stats"), s.sem("sums"), s.sem("rooted"), s.sem("normed")
        r_full, r_read, f_full, f_read, r_used = (s.sem(n) for n in ("r_full", "r_read", "f_full", "f_read", "r_used"))
        NR, NF = C // 2, KX // 2 // 8

        with s.block() as block:
            @block.sync
            def _(sp):
                for t, a in ((dh, "dft_h"), (dwp, "dft_wp"), (dwq, "dft_wq"), (avg, "avg")):
                    sp.dma_start(t[:], consts[a]).then_inc(c_in, 16)
                for k in range(2):
                    for c in range(0, C, 8):
                        sp.dma_start(X[:, k, c:c + 8], x[k].rearrange("c h w -> h c w")[:, c:c + 8]).then_inc(x_in[k], 16)
                with sp.Fori(1, B // 2) as i:
                    for k in range(2):
                        sp.wait_ge(r_full, (2 * i + k - 1) * NR)
                        alone(sp, passed)
                        for c in range(0, C, 8):
                            sp.dma_start(X[:, k, c:c + 8], one(x, 2 * i + k).rearrange("c h w -> h c w")[:, c:c + 8]).then_inc(x_in[k], 16)

            @block.vector
            def _(v):
                with v.Fori(0, B // 2) as i:
                    ch = Chain(v, stats, i * (2 * 38))
                    for k in range(2):
                        n = 2 * i + k
                        v.wait_ge(x_in[k], 64 * (i + 1))
                        for g in range(G):
                            ch.done(v.bn_stats(st[:, g], X[:, k, 2 * g:2 * g + 2, :].rearrange("p a w -> p (a w)")))
                        ch.sync()
                        alone(v, passed)
                        for g in range(G):
                            ch.done(v.bn_aggr(ag[:, g], st[:, g]))
                        ch.sync()
                        v.wait_ge(sums, 2 * n + 1)
                        ch.done(v.tensor_copy(mean[:], ps_s[:, 0:G]))
                        ch.sync()
                        ch.done(v.tensor_tensor(dev[:], ag[:, :, 0], mean[:], ALU.subtract))
                        ch.sync()
                        ch.done(v.tensor_tensor(dev[:], dev[:], dev[:], ALU.mult))
                        ch.sync()
                        ch.done(v.tensor_tensor(dev[:], dev[:], ag[:, :, 1], ALU.add))
                        v.wait_ge(sums, 2 * n + 2)
                        ch.done(v.tensor_scalar(rstd[:], ps_s[:, G:2 * G], EPS, None, ALU.add))
                        ch.sync()
                        v.wait_ge(rooted, n + 1)
                        ch.done(v.reciprocal(rstd[:], rstd[:]))
                        ch.sync()
                        for g in range(G):
                            xg = X[:, k, 2 * g:2 * g + 2, :]
                            v.tensor_scalar(xg, xg, mean[:, g:g + 1], rstd[:, g:g + 1],
                                            ALU.subtract, ALU.mult).then_inc(normed, 1)
                    assert ch.n == 2 * 38

            @block.tensor
            def _(pe):
                pe.wait_ge(c_in, 64)
                with pe.Fori(0, B // 2) as i:
                    for k in range(2):
                        n = 2 * i + k
                        pe.wait_ge(stats, 38 * n + 32)
                        pe.matmul(ps_s[:, 0:G], avg[:], ag[:, :, 0], start=True, stop=True).then_inc(sums, 1)
                        pe.wait_ge(stats, 38 * n + 36)
                        pe.matmul(ps_s[:, G:2 * G], avg[:], dev[:], start=True, stop=True).then_inc(sums, 1)
                        for c in range(C):
                            j = c // 2
                            if c % 2 == 0:
                                pe.wait_ge(normed, G * n + j + 1)
                                pe.wait_ge(r_read, NR * n + j + 1)
                            mm = pe.matmul(ps_r[j % 2][:, (c % 2) * KX * 3:(c % 2 + 1) * KX * 3],
                                           X[:, k, c, :], dh[:], start=True, stop=True)
                            if c % 2:
                                mm.then_inc(r_full, 1)
                        for j in range(NF):
                            if j == 0:
                                pe.wait_ge(r_read, NR * (n + 1) + 2)
                            pe.wait_ge(f_read, NF * n + j + 1)
                            for q in range(8):
                                for half in range(2):
                                    kx = (8 * j + q) + M1 * half
                                    out = ps_f[j % 2][64 * half:64 * half + 64, 64 * q:64 * q + 64]
                                    pe.matmul(out, rows[:, 3 * kx + 1:3 * kx + 3, :], dwp[:], start=True, stop=False)
                                    mm = pe.matmul(out, rows[:, 3 * kx:3 * kx + 2, :], dwq[:], start=False, stop=True)
                            mm.then_inc(f_full, 1)

            @block.scalar
            def _(a):
                a.sem_inc(r_read, 2)
                a.sem_inc(f_read, 2)
                with a.Fori(0, B) as n:
                    a.wait_ge(stats, 38 * n + 37)
                    a.activation(rstd[:], rstd[:], ACT.Sqrt).then_inc(rooted, 1)
                    for j in range(NR):
                        a.wait_ge(r_full, NR * n + j + 1)
                        if j == 0:
                            a.wait_ge(f_full, NF * n)
                        a.activation(rows[:, :, 2 * j:2 * j + 2].rearrange("p k c -> p c k"),
                                     ps_r[j % 2][:, 0:2 * KX * 3].rearrange("p (c k) -> p c k", c=2),
                                     ACT.Copy).then_inc(r_read, 1)
                    for j in range(NF):
                        a.wait_ge(f_full, NF * n + j + 1)
                        for r in range(2):
                            ins = a.activation(
                                F[:, 8 * M2 * j:8 * M2 * (j + 1), r, bass.ds(n, 1)].rearrange("p (k y) b -> p k (y b)", k=8),
                                ps_f[j % 2][:].rearrange("p (k r y) -> p k r y", k=8, r=2)[:, :, r, :],
                                ACT.Copy)
                        ins.then_inc(f_read, 1)

def spectral_mix(nc, sems, w, F, spec):
    NP = M1 // 2
    CH = 4
    with Stage(nc, sems, "mx") as s:
        WT = s.sb("w", [P, 2, C, CH * M2])
        FC = s.sb("fc", [P, 2, CH * M2, 2 * B])
        out = s.sb("out", [P, 2, 2, M2, B])
        ps = [s.ps(f"m{k}", [P, 512]) for k in range(2)]
        w_in = [s.sem(f"w_in{k}") for k in range(2)]
        passed, f_in, full, read, sent = s.sem("passed"), s.sem("f_in"), s.sem("full"), s.sem("read"), [s.sem(f"sent{k}") for k in range(2)]
        with s.block() as block:
            @block.sync
            def _(sp):
                def load(n, k):
                    for q in range(4):
                        for x in range(2):
                            src = w[q].rearrange("c o (n x) y -> n c o (x y)", x=CH)
                            sp.dma_start(WT[32 * q:32 * q + 32, k, 16 * x:16 * x + 16],
                                         one(src, n)[:, 16 * x:16 * x + 16]).then_inc(w_in[k], 16)
                for k in range(2):
                    load(k, k)
                with sp.Fori(1, M1 // CH // 2) as i:
                    for k in range(2):
                        sp.wait_ge(full, (2 * i + k - 1) * (CH // 2))
                        alone(sp, passed)
                        load(2 * i + k, k)

            @block.gpsimd
            def _(g):
                for k in range(2):
                    g.tensor_copy(FC[:, k], F[:, k * CH * M2:(k + 1) * CH * M2].rearrange("p m r b -> p m (r b)")).then_inc(f_in, 1)
                with g.Fori(1, M1 // CH // 2) as i:
                    for k in range(2):
                        g.wait_ge(full, (2 * i + k - 1) * (CH // 2))
                        alone(g, passed)
                        g.tensor_copy(FC[:, k], F[:, bass.ds((2 * i + k) * (CH * M2), CH * M2)].rearrange("p m r b -> p m (r b)")).then_inc(f_in, 1)

            @block.tensor
            def _(pe):
                pe.sem_inc(read, 2)
                with pe.Fori(0, M1 // CH // 2) as i:
                    for k in range(2):
                        pe.wait_ge(w_in[k], 128 * (i + 1))
                        pe.wait_ge(f_in, 2 * i + k + 1)
                        for j in range(CH // 2):
                            n = (2 * i + k) * (CH // 2) + j
                            pe.wait_ge(read, n + 1)
                            alone(pe, passed)
                            for par in range(2):
                                for ky in range(M2):
                                    m = (2 * j + par) * M2 + ky
                                    for half in range(2):
                                        r = slice(64 * half, 64 * half + 64)
                                        o = 64 * par + 32 * half
                                        mm = pe.matmul(ps[j % 2][o:o + 32, 16 * ky:16 * ky + 16], WT[r, k, :, m],
                                                       FC[r, k, m, :], start=True, stop=True,
                                                       tile_position=(64 * half, o))
                            mm.then_inc(full, 1)

            @block.vector
            def _(v):
                with v.Fori(0, NP // 2) as i:
                    for k in range(2):
                        n = 2 * i + k
                        v.wait_ge(full, n + 1)
                        v.wait_ge(sent[k], 16 * i)
                        for r in range(2):
                            ins = v.tensor_copy(out[:, k, r], ps[k][:].rearrange("p (y r b) -> p y r b", r=2, b=B)[:, :, r, :])
                        ins.then_inc(read, 1)

            @block.scalar
            def _(a):
                with a.Fori(0, NP // 2) as i:
                    for k in range(2):
                        a.wait_ge(read, 2 * i + k + 3)
                        a.dma_start(one(spec, 2 * i + k), out[:, k].rearrange("p r y b -> p (r y b)")).then_inc(sent[k], 16)
                for k in range(2):
                    a.wait_ge(sent[k], 16 * (NP // 2))


def spectral_inverse(nc, sems, x, spec, consts, bias, x1, gstat):
    OC = 4
    with Stage(nc, sems, "iv") as s:
        Gk = s.sb("g", [P, 2, OC, M2, B])
        X = s.sb("x", [P, 2, B, OC, W])
        Z = s.sb("z", [P, 2, 4, H])
        er, ei, ew = (s.sb(n, [P, P]) for n in ("er", "ei", "ew"))
        avg = s.sb("avg", [P, P])
        bs = s.sb("bs", [P, C])
        NG = 2 * B
        st = s.sb("st", [P, NG, 6])
        ag = s.sb("ag", [P, NG, 2])
        mean, dev = s.sb("mean", [P, NG]), s.sb("dev", [P, NG])
        res = s.sb("res", [P, 2, 2, B])
        ps_z = [s.ps(f"z{k}", [P, 512]) for k in range(2)]
        ps_y = [s.ps(f"y{k}", [P, 512]) for k in range(4)]
        ps_s = s.ps("s", [P, 512])
        c_in, passed = s.sem("c_in"), s.sem("passed")
        in_ = [s.sem(f"in{k}") for k in range(2)]
        z_full, z_done, y_full, y_done, stats, sums, rooted, r_sent = (
            s.sem(n) for n in ("z_full", "z_done", "y_full", "y_done", "stats", "sums", "rooted", "r_sent"))
        sent = [s.sem(f"sent{k}") for k in range(2)]
        NZ = B * OC // 8
        CHN = 2 * NG + 7

        with s.block() as block:
            @block.sync
            def _(sp):
                for t, a in ((er, "inv_hr"), (ei, "inv_hi"), (ew, "inv_w"), (avg, "avg")):
                    sp.dma_start(t[:], consts[a]).then_inc(c_in, 16)
                sp.dma_start(bs[:], bias.partition_broadcast(P)).then_inc(c_in, 16)

                def load(n, k):
                    src = spec.rearrange("j (par hl n o) f -> n par hl j o f", par=2, hl=2, o=OC)
                    for ri in range(2):
                        for hl in range(2):
                            for par in range(2):
                                p0 = 64 * ri + 32 * hl + 16 * par
                                sp.dma_start(Gk[p0:p0 + 16, k].rearrange("p o y b -> p o (y b)"),
                                             one(src, n)[par, hl, :, :, ri * M2 * B:(ri + 1) * M2 * B]).then_inc(in_[k], 16)
                    xs = x.rearrange("b (n o) h w -> n h b o w", o=OC)
                    for b in range(B):
                        sp.dma_start(X[:, k, b], one(xs, n)[:, b]).then_inc(in_[k], 16)
                for k in range(2):
                    load(k, k)
                with sp.Fori(1, C // OC // 2) as i:
                    for k in range(2):
                        sp.wait_ge(sent[k], 16 * B * i)
                        alone(sp, passed)
                        sp.wait_ge(stats, CHN * (2 * i + k - 1))
                        alone(sp, passed)
                        load(2 * i + k, k)

            @block.tensor
            def _(pe):
                pe.wait_ge(c_in, 80)
                pe.sem_inc(z_done, 2)
                pe.sem_inc(y_done, 4)
                with pe.Fori(0, C // OC // 2) as i:
                    for k in range(2):
                        n = 2 * i + k
                        pe.wait_ge(in_[k], 256 * (i + 1))

                        def over_h(j):
                            pe.wait_ge(z_done, NZ * n + j + 1)
                            for m in range(8):
                                b, o = divmod(8 * j + m, OC)
                                for r, e in enumerate((er, ei)):
                                    p0 = 64 * (m % 2) + 32 * r
                                    mm = pe.matmul(ps_z[j % 2][p0:p0 + 32, 128 * (m // 2):128 * (m // 2) + 128],
                                                   Gk[:, k, o, :, b], e[:], start=True, stop=True)
                            mm.then_inc(z_full, 1)

                        def over_w(j):
                            pe.wait_ge(z_done, NZ * n + j + 3)
                            pe.wait_ge(y_done, 2 * NZ * n + 2 * j + 2)
                            for m in range(8):
                                h = slice(64 * (m % 2), 64 * (m % 2) + 64)
                                q = 128 * (m // 2)
                                mm = pe.matmul(ps_y[(2 * j + m % 2) % 4][:, q:q + 128], Z[h, j % 2, m // 2, :],
                                               ew[h, :], start=True, stop=True)
                                if m >= 6:
                                    mm.then_inc(y_full, 1)
                        over_h(0)
                        for j in range(NZ):
                            if j + 1 < NZ:
                                over_h(j + 1)
                            over_w(j)
                        pe.wait_ge(stats, CHN * n + 2 * NG)
                        pe.matmul(ps_s[:, 0:NG], avg[:], ag[:, :, 0], start=True, stop=True).then_inc(sums, 1)
                        pe.wait_ge(stats, CHN * n + 2 * NG + 4)
                        pe.matmul(ps_s[:, NG:2 * NG], avg[:], dev[:], start=True, stop=True).then_inc(sums, 1)

            @block.scalar
            def _(a):
                with a.Fori(0, C // OC) as n:
                    for j in range(NZ):
                        a.wait_ge(z_full, NZ * n + j + 1)
                        if j >= 2:
                            a.wait_ge(y_full, 2 * (NZ * n + j - 1))
                        a.activation(Z[:, j % 2].rearrange("p m h -> p (m h)"), ps_z[j % 2][:], ACT.Copy).then_inc(z_done, 1)
                    a.wait_ge(stats, CHN * (n + 1) - 1)
                    a.activation(res[:, :, 1], res[:, :, 1], ACT.Sqrt).then_inc(rooted, 1)

            @block.vector
            def _(v):
                v.wait_ge(c_in, 80)
                with v.Fori(0, C // OC // 2) as i:
                    ch = Chain(v, stats, i * (2 * CHN))
                    for k in range(2):
                        n = 2 * i + k
                        v.wait_ge(in_[k], 256 * (i + 1))
                        for y in range(2 * NZ):
                            v.wait_ge(y_full, 2 * NZ * n + y + 1)
                            for q in range(4):
                                o = y % 2 + 2 * (q % 2)
                                xo = X[:, k, 2 * (y // 2) + q // 2, o, :]
                                ins = v.scalar_tensor_tensor(out=xo, in0=ps_y[y % 4][:, 128 * q:128 * q + 128],
                                                             scalar=bs[:, bass.ds(n * OC + o, 1)],
                                                             in1=xo, op0=ALU.add, op1=ALU.add)
                            ins.then_inc(y_done, 1)
                        v.wait_ge(y_done, 2 * NZ * (n + 1) + 4)
                        for g in range(NG):
                            ch.done(v.bn_stats(st[:, g], X[:, k, g // 2, 2 * (g % 2):2 * (g % 2) + 2, :].rearrange("p o w -> p (o w)")))
                        ch.sync()
                        alone(v, passed)
                        for g in range(NG):
                            ch.done(v.bn_aggr(ag[:, g], st[:, g]))
                        ch.sync()
                        v.wait_ge(sums, 2 * n + 1)
                        ch.done(v.tensor_copy(mean[:], ps_s[:, 0:NG]))
                        ch.sync()
                        ch.done(v.tensor_tensor(dev[:], ag[:, :, 0], mean[:], ALU.subtract))
                        ch.sync()
                        ch.done(v.tensor_tensor(dev[:], dev[:], dev[:], ALU.mult))
                        ch.sync()
                        ch.done(v.tensor_tensor(dev[:], dev[:], ag[:, :, 1], ALU.add))
                        ch.sync()
                        v.wait_ge(r_sent, 16 * n)
                        ch.done(v.tensor_copy(res[:, :, 0], mean[:].rearrange("p (b q) -> p q b", q=2)))
                        v.wait_ge(sums, 2 * n + 2)
                        ch.done(v.tensor_scalar(res[:, :, 1], ps_s[:, NG:2 * NG].rearrange("p (b q) -> p q b", q=2), EPS, None, ALU.add))
                        v.wait_ge(rooted, n + 1)
                        ch.done(v.reciprocal(res[:, :, 1], res[:, :, 1]))
                    assert ch.n == 2 * CHN

            @block.gpsimd
            def _(g):
                with g.Fori(0, C // OC // 2) as i:
                    for k in range(2):
                        n = 2 * i + k
                        g.wait_ge(y_done, 2 * NZ * (n + 1) + 4)
                        alone(g, passed)
                        for b in range(B):
                            g.dma_start(one(x1.rearrange("b (n o) h w -> n h b o w", o=OC), n)[:, b], X[:, k, b]).then_inc(sent[k], 16)
                        g.wait_ge(stats, CHN * (n + 1))
                        alone(g, passed)
                        g.dma_start(one(gstat, n), res[0:1].rearrange("p q t b -> p (q t b)")).then_inc(r_sent, 16)
                for k in range(2):
                    g.wait_ge(sent[k], 16 * B * (C // OC // 2))
                g.wait_ge(r_sent, 16 * (C // OC))


def norm_coefficients(nc, sems, name, st, parts, share, gb, out):
    n = st.shape[1]
    with Stage(nc, sems, name) as s:
        ag = s.sb("ag", [parts, 2])
        dev = s.sb("dev", [parts, 1])
        cs = s.sb("cs", [parts, 3])
        ps = s.ps("ps", [P, 512])
        steps, sums, rooted = s.sem("steps"), s.sem("sums"), s.sem("rooted")
        with s.block() as block:
            @block.vector
            def _(v):
                ch = Chain(v, steps)
                ch.done(v.bn_aggr(ag[:], st[0:parts].rearrange("p n s -> p (n s)")))
                v.wait_ge(sums, 1)
                ch.done(v.tensor_copy(cs[:, 0:1], ps[0:parts, 0:1]))
                ch.sync()
                ch.done(v.tensor_tensor(dev[:], ag[:, 0:1], cs[:, 0:1], ALU.subtract))
                ch.sync()
                ch.done(v.tensor_tensor(dev[:], dev[:], dev[:], ALU.mult))
                ch.sync()
                ch.done(v.tensor_tensor(dev[:], dev[:], ag[:, 1:2], ALU.add))
                v.wait_ge(sums, 2)
                ch.done(v.tensor_scalar(cs[:, 1:2], ps[0:parts, 1:2], EPS, None, ALU.add))
                v.wait_ge(rooted, 1)
                ch.done(v.reciprocal(cs[:, 1:2], cs[:, 1:2]))
                ch.sync()
                ch.done(v.tensor_tensor(out[:, 0:1], cs[:, 1:2], gb[:, 0:1], ALU.mult))
                ch.sync()
                ch.done(v.tensor_tensor(cs[:, 2:3], cs[:, 0:1], out[:, 0:1], ALU.mult))
                ch.sync()
                v.tensor_tensor(out[:, 1:2], gb[:, 1:2], cs[:, 2:3], ALU.subtract)

            @block.tensor
            def _(pe):
                pe.wait_ge(steps, 1)
                pe.matmul(ps[0:parts, 0:1], share, ag[:, 0:1], start=True, stop=True).then_inc(sums, 1)
                pe.wait_ge(steps, 5)
                pe.matmul(ps[0:parts, 1:2], share, dev[:], start=True, stop=True).then_inc(sums, 1)

            @block.scalar
            def _(a):
                a.wait_ge(steps, 6)
                a.activation(cs[:, 1:2], cs[:, 1:2], ACT.Sqrt).then_inc(rooted, 1)


RC = 16
NCH = H // RC


def load_taps(sp, X, k, src, j, got, pad=0):
    for d in range(3):
        lo, hi = j * RC + d - 1, j * RC + d - 1 + RC
        a, b = max(lo, 0), min(hi, H)
        sp.dma_start(X[32 * d:32 * d + 32, k, a - lo:b - lo, pad:pad + W], src[:, a:b, :]).then_inc(got, 16)


def graph_conv(nc, sems, x1, gstat, wt, wts, y1, st):
    with Stage(nc, sems, "gc") as s:
        X = s.sb("x", [97, 2, RC, W])
        Y = s.sb("y", [P, 2, 512])
        O = s.sb("o", [P, 2, 512])
        GS = s.sb("gs", [96, 2, B])
        cw = s.sb("cw", [97, C])
        A = s.sb("A", [P, P])
        ps_c = [s.ps(f"c{k}", [P, 512]) for k in range(2)]
        ps_a = [s.ps(f"a{k}", [P, 512]) for k in range(2)]
        c_in, g_in, passed = s.sem("c_in"), s.sem("g_in"), s.sem("passed")
        x_in = [s.sem(f"x_in{k}") for k in range(2)]
        set_, normed, edged, conv, y_done, prod, o_done, counted = (
            s.sem(n) for n in ("set", "normed", "edged", "conv", "y_done", "prod", "o_done", "counted"))
        sent = [s.sem(f"sent{k}") for k in range(2)]

        with s.block() as block:
            @block.sync
            def _(sp):
                sp.dma_start(cw[:], wts["l1_w"]).then_inc(c_in, 16)
                sp.dma_start(A[:], wts["l1_A"]).then_inc(c_in, 16)
                for d in range(3):
                    for e in range(2):
                        sp.dma_start(GS[32 * d + e:32 * d + 32:2].rearrange("p t b -> p (t b)"),
                                     gstat.rearrange("n a (q t) -> (n a q) t", q=2)).then_inc(g_in, 16)
                sp.wait_ge(set_, 1)
                with sp.Fori(0, B) as b:
                    for j in range(NCH):
                        k = j % 2
                        sp.wait_ge(conv, b * NCH + j + 1)
                        alone(sp, passed)
                        load_taps(sp, X, k, one(x1, b), j, x_in[k])

            @block.gpsimd
            def _(g):
                g.memset(X[:], 0.0).then_inc(set_, 1)
                g.wait_ge(set_, 1)
                g.memset(X[96:97], 1.0).then_inc(set_, 1)
                with g.Fori(0, B) as b:
                    for j in range(NCH):
                        g.wait_ge(o_done, b * NCH + j + 3)
                        alone(g, passed)
                        g.dma_start(one(y1, b)[:, j], O[:, j % 2]).then_inc(sent[j % 2], 16)
                for k in range(2):
                    g.wait_ge(sent[k], 16 * B * NCH // 2)

            @block.vector
            def _(v):
                v.wait_ge(g_in, 96)
                v.sem_inc(counted, 2)
                with v.Fori(0, B) as b:
                    for j in range(NCH + 1):
                        if j < NCH:
                            k = j % 2
                            v.wait_ge(x_in[k], 48 * (b * (NCH // 2) + j // 2 + 1))
                            xk = X[0:96, k].rearrange("p r w -> p (r w)")
                            v.tensor_scalar(xk, xk, GS[:, 0, bass.ds(b, 1)], GS[:, 1, bass.ds(b, 1)],
                                            ALU.subtract, ALU.mult).then_inc(normed, 1)
                            if j in (0, NCH - 1):
                                v.wait_ge(normed, b * NCH + j + 1)
                                edge = X[0:32, k, 0, :] if j == 0 else X[64:96, k, RC - 1, :]
                                v.memset(edge, 0.0).then_inc(edged, 1)
                        if j:
                            v.wait_ge(o_done, b * NCH + j + 2)
                            v.bn_stats(st[:, bass.ds(b * NCH + j - 1, 1), :].rearrange("p a s -> p (a s)"),
                                       O[:, (j - 1) % 2]).then_inc(counted, 1)

            @block.tensor
            def _(pe):
                pe.wait_ge(c_in, 32)
                pe.wait_ge(set_, 2)
                pe.sem_inc(conv, 2)
                pe.sem_inc(prod, 2)
                with pe.Fori(0, B) as b:
                    for j in range(NCH + 1):
                        n = b * NCH + j
                        if j < NCH:
                            k = j % 2
                            pe.wait_ge(normed, n + 1)
                            if j == 0:
                                pe.wait_ge(edged, 2 * b + 1)
                            if j == NCH - 1:
                                pe.wait_ge(edged, 2 * b + 2)
                            pe.wait_ge(y_done, n + 1)
                            for r in range(RC):
                                mm = pe.matmul(ps_c[k][:, 32 * r:32 * r + 32], X[:, k, r, :], cw[:], start=True, stop=True)
                            mm.then_inc(conv, 1)
                        if j:
                            k = (j - 1) % 2
                            pe.wait_ge(y_done, n + 2)
                            pe.wait_ge(o_done, n)
                            for q in range(4):
                                mm = pe.matmul(ps_a[k][:, 128 * q:128 * q + 128], Y[:, k, 128 * q:128 * q + 128], A[:],
                                               start=True, stop=True)
                            mm.then_inc(prod, 1)

            @block.scalar
            def _(a):
                a.sem_inc(y_done, 2)
                a.sem_inc(o_done, 2)
                with a.Fori(0, B) as b:
                    for j in range(NCH + 1):
                        n = b * NCH + j
                        if j < NCH:
                            a.wait_ge(conv, n + 3)
                            a.wait_ge(prod, n + 1)
                            a.activation(Y[:, j % 2], ps_c[j % 2][:], ACT.Relu).then_inc(y_done, 1)
                        if j:
                            k = (j - 1) % 2
                            a.wait_ge(prod, n + 2)
                            a.wait_ge(sent[k], 16 * (b * (NCH // 2) + (j - 1) // 2))
                            a.wait_ge(counted, n)
                            a.activation(O[:, k], ps_a[k][:], ACT.Copy).then_inc(o_done, 1)


def residual_norm(nc, sems, name, y, coef, x, x_out, pair, GS):
    N = PX // 4
    with Stage(nc, sems, name) as s:
        Y = s.sb("y", [P, 2, N])
        X = s.sb("x", [P, 2, N])
        st = s.sb("st", [P, 8, 6])
        ag = s.sb("ag", [P, 2])
        dev = s.sb("dev", [P, 1])
        pr = s.sb("pr", [P, P])
        ps = s.ps("ps", [P, 512])
        c_in, passed = s.sem("c_in"), s.sem("passed")
        got = [s.sem(f"in{k}") for k in range(2)]
        sent = [s.sem(f"sent{k}") for k in range(2)]
        act, steps, sums, rooted = s.sem("act"), s.sem("steps"), s.sem("sums"), s.sem("rooted")
        ST = 1 + 8 + 1 + 1 + 1 + 1 + 1 + 1 + 1
        with s.block() as block:
            @block.sync
            def _(sp):
                sp.dma_start(pr[:], pair).then_inc(c_in, 16)
                with sp.Fori(0, B // 2) as i:
                    for k in range(2):
                        sp.wait_ge(sent[k], 64 * i)
                        alone(sp, passed)
                        sp.wait_ge(steps, ST * (2 * i + k) + k)
                        alone(sp, passed)
                        sp.dma_start(Y[:, k], one(y, 2 * i + k)).then_inc(got[k], 16)
                        for q in range(4):
                            r = slice(32 * q, 32 * q + 32)
                            xv = X[r, k].rearrange("p (h w) -> p h w", w=W)
                            sp.dma_start(xv, one(x, 2 * i + k)[q]).then_inc(got[k], 16)

            @block.scalar
            def _(a):
                with a.Fori(0, B // 2) as i:
                    for k in range(2):
                        n = 2 * i + k
                        a.wait_ge(got[k], 80 * (i + 1))
                        a.activation(Y[:, k], Y[:, k], ACT.Relu, bias=coef[:, 1:2], scale=coef[:, 0:1]).then_inc(act, 1)
                        a.wait_ge(steps, ST * n + ST - 1 + 2)
                        alone(a, passed)
                        gv = GS[:, 1, bass.ds(n, 1)]
                        a.activation(gv, gv, ACT.Sqrt).then_inc(rooted, 1)

            @block.vector
            def _(v):
                v.sem_inc(steps, 2)
                with v.Fori(0, B // 2) as i:
                    ch = Chain(v, steps, i * (2 * ST) + 2)
                    for k in range(2):
                        n = 2 * i + k
                        v.wait_ge(act, n + 1)
                        ch.done(v.tensor_tensor(X[:, k], X[:, k], Y[:, k], ALU.add))
                        ch.sync()
                        for q in range(8):
                            ch.done(v.bn_stats(st[:, q], X[:, k, 512 * q:512 * q + 512]))
                        ch.sync()
                        alone(v, passed)
                        ch.done(v.bn_aggr(ag[:], st[:].rearrange("p q s -> p (q s)")))
                        v.wait_ge(sums, 2 * n + 1)
                        ch.done(v.tensor_copy(GS[:, 0, bass.ds(n, 1)], ps[:, 0:1]))
                        ch.sync()
                        ch.done(v.tensor_tensor(dev[:], ag[:, 0:1], GS[:, 0, bass.ds(n, 1)], ALU.subtract))
                        ch.sync()
                        ch.done(v.tensor_tensor(dev[:], dev[:], dev[:], ALU.mult))
                        ch.sync()
                        ch.done(v.tensor_tensor(dev[:], dev[:], ag[:, 1:2], ALU.add))
                        v.wait_ge(sums, 2 * n + 2)
                        ch.done(v.tensor_scalar(GS[:, 1, bass.ds(n, 1)], ps[:, 1:2], EPS, None, ALU.add))
                        v.wait_ge(rooted, n + 1)
                        alone(v, passed)
                        ch.done(v.reciprocal(GS[:, 1, bass.ds(n, 1)], GS[:, 1, bass.ds(n, 1)]))
                    assert ch.n == 2 * ST

            @block.tensor
            def _(pe):
                pe.wait_ge(c_in, 16)
                with pe.Fori(0, B) as n:
                    pe.wait_ge(steps, ST * n + 2 + 10)
                    pe.matmul(ps[:, 0:1], pr[:], ag[:, 0:1], start=True, stop=True).then_inc(sums, 1)
                    pe.wait_ge(steps, ST * n + 2 + 14)
                    pe.matmul(ps[:, 1:2], pr[:], dev[:], start=True, stop=True).then_inc(sums, 1)

            @block.gpsimd
            def _(g):
                with g.Fori(0, B // 2) as i:
                    for k in range(2):
                        g.wait_ge(steps, ST * (2 * i + k) + 3)
                        alone(g, passed)
                        for q in range(4):
                            r = slice(32 * q, 32 * q + 32)
                            xv = X[r, k].rearrange("p (h w) -> p h w", w=W)
                            g.dma_start(one(x_out, 2 * i + k)[q], xv).then_inc(sent[k], 16)
                for k in range(2):
                    g.wait_ge(sent[k], 64 * (B // 2))


def depth_conv(nc, sems, x2, GS, LF, fb, hs, st):
    with Stage(nc, sems, "dc") as s:
        X = s.sb("x", [96, 2, RC, W + 2])
        O = s.sb("o", [96, 2, RC * W])
        ps = [s.ps(f"c{k}", [P, 512]) for k in range(4)]
        set_, passed = s.sem("set"), s.sem("passed")
        x_in = [s.sem(f"x_in{k}") for k in range(2)]
        sent = [s.sem(f"sent{k}") for k in range(2)]
        normed, edged, conv, o_done, counted = (s.sem(n) for n in ("normed", "edged", "conv", "o_done", "counted"))
        Q = RC // 4
        with s.block() as block:
            @block.sync
            def _(sp):
                sp.wait_ge(set_, 1)
                with sp.Fori(0, B) as b:
                    for j in range(NCH):
                        sp.wait_ge(conv, Q * (b * NCH + j + 1))
                        alone(sp, passed)
                        load_taps(sp, X, j % 2, one(x2, b), j, x_in[j % 2], pad=1)

            @block.gpsimd
            def _(g):
                g.memset(X[:], 0.0).then_inc(set_, 1)
                with g.Fori(0, B) as b:
                    for j in range(NCH):
                        k = j % 2
                        g.wait_ge(o_done, Q * (b * NCH + j + 1) + 4)
                        alone(g, passed)
                        g.dma_start(one(hs, b)[:, j * RC * W:(j + 1) * RC * W], O[:, k]).then_inc(sent[k], 16)
                for k in range(2):
                    g.wait_ge(sent[k], 16 * B * NCH // 2)

            @block.vector
            def _(v):
                with v.Fori(0, B) as b:
                    for j in range(NCH + 1):
                        if j < NCH:
                            k = j % 2
                            v.wait_ge(x_in[k], 48 * (b * (NCH // 2) + j // 2 + 1))
                            xk = X[0:96, k, :, 1:W + 1]
                            v.tensor_scalar(xk, xk, GS[0:96, 0, bass.ds(b, 1)], GS[0:96, 1, bass.ds(b, 1)],
                                            ALU.subtract, ALU.mult).then_inc(normed, 1)
                            if j in (0, NCH - 1):
                                v.wait_ge(normed, b * NCH + j + 1)
                                edge = X[0:32, k, 0, :] if j == 0 else X[64:96, k, RC - 1, :]
                                v.memset(edge, 0.0).then_inc(edged, 1)
                        if j:
                            for q in range(Q):
                                m = b * (NCH * Q) + (j - 1) * Q + q
                                v.wait_ge(o_done, m + 5)
                                v.bn_stats(st[:, bass.ds(m, 1), :].rearrange("p a s -> p (a s)"),
                                           O[0:64, (j - 1) % 2, 512 * q:512 * q + 512]).then_inc(counted, 1)

            @block.tensor
            def _(pe):
                pe.sem_inc(conv, 2 * Q)
                with pe.Fori(0, B) as b:
                    for j in range(NCH):
                        k = j % 2
                        n = b * NCH + j
                        pe.wait_ge(normed, n + 1)
                        if j == 0:
                            pe.wait_ge(edged, 2 * b + 1)
                        if j == NCH - 1:
                            pe.wait_ge(edged, 2 * b + 2)
                        for q in range(Q):
                            pe.wait_ge(o_done, Q * n + q + 1)
                            alone(pe, passed)
                            for d in range(3):
                                mm = pe.matmul(ps[q][0:96, :], LF[:, d, :], X[:, k, 4 * q:4 * q + 4, d:d + W],
                                               start=(d == 0), stop=(d == 2))
                            mm.then_inc(conv, 1)

            @block.scalar
            def _(a):
                a.sem_inc(o_done, 4)
                with a.Fori(0, B) as b:
                    for j in range(NCH):
                        k = j % 2
                        n = b * NCH + j
                        a.wait_ge(sent[k], 16 * (b * (NCH // 2) + j // 2))
                        if j >= 2:
                            a.wait_ge(counted, Q * (n - 1))
                        for q in range(Q):
                            a.wait_ge(conv, Q * n + q + 1 + 2 * Q)
                            a.activation(O[:, k, 512 * q:512 * q + 512], ps[q][0:96, :], ACT.Identity,
                                         bias=fb[:, 0:1]).then_inc(o_done, 1)


def last_conv(nc, sems, x3, GS, LW, out):
    R2 = RC // 2
    with Stage(nc, sems, "lc") as s:
        X = s.sb("x", [P, 2, R2, W + 2])
        R = s.sb("r", [64, 2, R2, W])
        shift = s.sb("shift", [P, B])
        negated = s.sem("negated")
        ps = [s.ps(f"c{k}", [P, 512]) for k in range(4)]
        set_, passed = s.sem("set"), s.sem("passed")
        x_in = [s.sem(f"x_in{k}") for k in range(2)]
        r_in = [s.sem(f"r_in{k}") for k in range(2)]
        sent = [s.sem(f"sent{k}") for k in range(2)]
        normed, edged, conv, added = (s.sem(n) for n in ("normed", "edged", "conv", "added"))
        Q = R2 // 4
        with s.block() as block:
            @block.sync
            def _(sp):
                sp.wait_ge(set_, 1)
                with sp.Fori(0, B) as b:
                    for j in range(NCH):
                        k = j % 2
                        sp.wait_ge(conv, Q * (b * NCH + j + 1))
                        alone(sp, passed)
                        sp.wait_ge(sent[k], 32 * (b * (NCH // 2) + j // 2))
                        alone(sp, passed)
                        img = one(x3, b)
                        for d in range(4):
                            r0 = j * RC + d - 1
                            a = 1 if r0 < 0 else 0
                            e = R2 - 1 if r0 + 2 * (R2 - 1) >= H else R2
                            sp.dma_start(X[32 * d:32 * d + 32, k, a:e, 1:W + 1],
                                         img[:, r0 + 2 * a:r0 + 2 * (e - 1) + 1:2, :]).then_inc(x_in[k], 16)
                        for p in range(2):
                            sp.dma_start(R[32 * p:32 * p + 32, k], img[:, j * RC + p:(j + 1) * RC:2, :]).then_inc(r_in[k], 16)

            @block.gpsimd
            def _(g):
                g.memset(X[:], 0.0).then_inc(set_, 1)
                with g.Fori(0, B) as b:
                    for j in range(NCH):
                        k = j % 2
                        g.wait_ge(added, Q * (b * NCH + j + 1) + 4)
                        alone(g, passed)
                        for p in range(2):
                            g.dma_start(one(out, b)[:, j * RC + p:(j + 1) * RC:2, :], R[32 * p:32 * p + 32, k]).then_inc(sent[k], 16)
                for k in range(2):
                    g.wait_ge(sent[k], 32 * B * NCH // 2)

            @block.scalar
            def _(a):
                with a.Fori(0, B) as b:
                    for j in range(NCH):
                        k = j % 2
                        a.wait_ge(negated, 1)
                        a.wait_ge(x_in[k], 64 * (b * (NCH // 2) + j // 2 + 1))
                        alone(a, passed)
                        xk = X[:, k, :, 1:W + 1]
                        a.activation(xk, xk, ACT.Identity, bias=shift[:, bass.ds(b, 1)],
                                     scale=GS[:, 1, bass.ds(b, 1)]).then_inc(normed, 1)

            @block.vector
            def _(v):
                v.sem_inc(added, 4)
                v.scalar_tensor_tensor(out=shift[:], in0=GS[:, 0, :], scalar=-1.0, in1=GS[:, 1, :],
                                       op0=ALU.mult, op1=ALU.mult).then_inc(negated, 1)
                with v.Fori(0, B) as b:
                    for j in range(NCH + 1):
                        if j in (0, NCH - 1):
                            v.wait_ge(normed, b * NCH + j + 1)
                            edge = X[0:32, j % 2, 0, :] if j == 0 else X[96:128, j % 2, R2 - 1, :]
                            v.memset(edge, 0.0).then_inc(edged, 1)
                        if j:
                            k = (j - 1) % 2
                            n = b * NCH + j - 1
                            v.wait_ge(r_in[k], 32 * (b * (NCH // 2) + (j - 1) // 2 + 1))
                            for q in range(Q):
                                v.wait_ge(conv, Q * n + q + 1 + 2 * Q)
                                rq = R[:, k, 4 * q:4 * q + 4, :].rearrange("p r w -> p (r w)")
                                v.tensor_tensor(rq, ps[2 * k + q][0:64, :], rq, ALU.add).then_inc(added, 1)

            @block.tensor
            def _(pe):
                pe.sem_inc(conv, 2 * Q)
                with pe.Fori(0, B) as b:
                    for j in range(NCH):
                        k = j % 2
                        n = b * NCH + j
                        pe.wait_ge(normed, n + 1)
                        if j == 0:
                            pe.wait_ge(edged, 2 * b + 1)
                        if j == NCH - 1:
                            pe.wait_ge(edged, 2 * b + 2)
                        for q in range(Q):
                            pe.wait_ge(added, Q * n + q + 1)
                            alone(pe, passed)
                            for d in range(3):
                                mm = pe.matmul(ps[2 * k + q][0:64, :], LW[:, d, :], X[:, k, 4 * q:4 * q + 4, d:d + W],
                                               start=(d == 0), stop=(d == 2))
                            mm.then_inc(conv, 1)


def load_weights(nc, sems, d, wt):
    with Stage(nc, sems, "wt") as s:
        dsc = s.sb("dsc", [C, 2, K9, 4 * C])
        fus = s.sb("fus", [C, 3, C])
        cw = s.sb("cw", [C, 3, 96])
        cb = s.sb("cb", [C, 1])
        fz = s.sb("fz", [C, 96])
        dwv = s.sb("dwv", [96, 2, 3])
        idm = s.sb("idm", [96, C])
        b96 = s.sb("b96", [96, 1])
        fT = s.sb("fT", [12, C, P])
        cm = s.sb("cm", [12, 9])
        sel = s.sb("sel", [97, 2 * K9, P])
        ps = [s.ps(f"p{k}", [P, 512]) for k in range(5)]
        c_in, made, zeroed = s.sem("c_in"), s.sem("made"), s.sem("zeroed")
        loads = [(dsc[:].rearrange("m a k c -> m (a k c)"), d["dsc"]), (fus[:].rearrange("m g o -> m (g o)"), d["fusT"]),
                 (cw[:].rearrange("m x c -> m (x c)"), d["convw"]), (cb[:], d["conv_b"]), (fz[:, 64:96], d["fusT"][:, 0:C]),
                 (dwv[:].rearrange("p a x -> p (a x)"), d["dw"]), (idm[:], d["idm"]), (b96[:], d["b96"]),
                 (fT[:].rearrange("f o i -> f (o i)"), d["freqT"]), (cm[:], d["freq_to_taps"]),
                 (sel[:].rearrange("r k p -> r (k p)"), d["select"]),
                 (wt["grid"][:].rearrange("p j n -> p (j n)"), d["grid"]), (wt["pw"][:], d["pw"]), (wt["pb"][:], d["pb"]),
                 (wt["share"][:], d["share"]), (wt["gb1"][:], d["gb1"]), (wt["gbo"][:], d["gbo"]), (wt["gbf"][:], d["gbf"]),
                 (wt["eye"][:], d["eye"])]
        with s.block() as block:
            @block.sync
            def _(sp):
                for dst, src in loads:
                    sp.dma_start(dst, src).then_inc(c_in, 16)

            @block.gpsimd
            def _(g):
                g.memset(fz[:, 0:64], 0.0).then_inc(zeroed, 1)
                g.memset(wt["L3"][:], 0.0).then_inc(zeroed, 1)

            @block.tensor
            def _(pe):
                pe.wait_ge(c_in, 16 * len(loads))
                pe.wait_ge(zeroed, 2)
                for a in range(2):
                    for k in range(K9):
                        mm = pe.matmul(ps[a][:, 32 * k:32 * k + 32], dsc[:, a, k, :], fus[:, 2 - a, :], start=True, stop=True)
                for x in range(3):
                    mm = pe.matmul(ps[2][0:96, 32 * x:32 * x + 32], cw[:, x, :], fus[:, 0, :], start=True, stop=True)
                pe.matmul(ps[3][0:96, 0:1], fz[:], cb[:], start=True, stop=True)
                for o in range(C):
                    mm = pe.matmul(ps[4][:, 9 * o:9 * o + 9], fT[:, o, :], cm[:], start=True, stop=True)
                mm.then_inc(made, 1)

            @block.vector
            def _(v):
                v.wait_ge(made, 1)
                for a in range(2):
                    v.tensor_scalar(wt["Z"][:, a, :], ps[a][:, 0:32 * K9], -1.0, None, ALU.mult)
                v.tensor_copy(wt["L2"][:, :, 64:96], ps[2][0:96, 0:96].rearrange("p (x o) -> p x o", x=3))
                for x in range(3):
                    for a in range(2):
                        v.tensor_scalar(wt["L2"][:, x, 32 * a:32 * a + 32], idm[:], dwv[:, a, x:x + 1], None, ALU.mult)
                v.tensor_tensor(wt["b2"][:], ps[3][0:96, 0:1], b96[:], ALU.add)
                for q in range(4):
                    for t in range(2):
                        if 0 <= q - t <= 2:
                            dy = q - t
                            src = ps[4][32 * q:32 * q + 32, 0:288].rearrange("i (o y x) -> i y x o", y=3, x=3)[:, dy]
                            v.tensor_copy(wt["L3"][32 * q:32 * q + 32, :, 32 * t:32 * t + 32], src)

            @block.scalar
            def _(a):
                a.wait_ge(c_in, 16 * len(loads))
                a.activation(wt["sel"][:], sel[:], ACT.Copy)


LINES = 32
PAIRS = [(0, 1), (2, 3), (4, 5), (6, 7), (8,)]


def deformable(nc, sems, b_views, coef, GS, wt, uy, st):
    x2, hs, u = b_views
    with Stage(nc, sems, "df") as s:
        XI = s.sb("xi", [P, 2, H // 4 * W])
        IX = s.sb("ix", [97, PX], BF16)
        HI = s.sb("hi", [64, 2, RC * W])
        t_ix, t_r, t_r2 = (s.sb(n, [P, 512]) for n in ("t_ix", "t_r", "t_r2"))
        parts = s.sb("parts", [P, 2, 3, 512], BF16)
        XS = s.sb("xs", [P, 2, P])
        Zs = s.sb("zs", [P, 2, 4, 32 * K9])
        NT = 5
        T = s.sb("t", [P, NT, 1024])
        YB = s.sb("yb", [H, C, W])
        U = s.sb("u", [P, LINES, W])
        XO = s.sb("xo", [P, 2, P])
        ps_d = [s.ps(f"d{k}", [P, 1024]) for k in range(2)]
        ps_z = [s.ps(f"z{k}", [P, 512]) for k in range(2)]
        ps_o = [s.ps(f"o{k}", [P, 512]) for k in range(2)]
        passed, ones = s.sem("passed"), s.sem("ones")
        h_in, p_out = ([s.sem(f"{n}{k}") for k in range(2)] for n in ("h_in", "p_out"))
        i_in = [s.sem("iy_in"), s.sem("ix_in")]
        u_in, uy_out, uy_in, u_out = (s.sem(n) for n in ("u_in", "uy_out", "uy_in", "u_out"))
        relu, off, split = s.sem("relu"), s.sem("off"), s.sem("split")
        normed, line_in = s.sem("normed"), s.sem("line_in")
        z_full, z_read = s.sem("z_full"), s.sem("z_read")
        d_full, d_read = s.sem("d_full"), s.sem("d_read")
        hat, t_used = s.sem("hat"), s.sem("t_used")
        o_read = s.sem("o_read")
        turned, u_added = s.sem("turned"), s.sem("u_added")
        summed, counted = s.sem("summed"), s.sem("counted")
        S = 2 * LINES
        L = len(PAIRS)
        CHN = 6

        with s.block() as block:
            @block.sync
            def _(sp):
                sp.wait_ge(ones, 1)
                with sp.Fori(0, B) as b:
                    x2b = one(x2, b)
                    for j in range(NCH):
                        k = j % 2
                        sp.wait_ge(off, b * NCH + j + 1)
                        alone(sp, passed)
                        sp.dma_start(HI[:, k], one(hs, b)[0:64, j * RC * W:(j + 1) * RC * W]).then_inc(h_in[k], 16)
                    sp.wait_ge(line_in, b * S)
                    alone(sp, passed)
                    for q in range(4):
                        r = slice(32 * q, 32 * q + 32)
                        sp.dma_start(XI[r, 0].rearrange("c (h w) -> c h w", w=32), x2b[:, :, 32 * q:32 * q + 32]).then_inc(i_in[0], 16)
                    for q in range(4):
                        r = slice(32 * q, 32 * q + 32)
                        sp.dma_start(XI[r, 1].rearrange("c (h w) -> c h w", w=W), x2b[:, 32 * q:32 * q + 32, :]).then_inc(i_in[1], 16)
                    sp.wait_ge(u_out, b * 64)
                    alone(sp, passed)
                    sp.wait_ge(counted, b * 8)
                    alone(sp, passed)
                    for q in range(4):
                        r = slice(32 * q, 32 * q + 32)
                        sp.dma_start(U[r], one(hs, b)[64:96].rearrange("o (h w) -> o h w", w=W)[:, 32 * q:32 * q + 32, :]).then_inc(u_in, 16)
                    sp.wait_ge(o_read, b * S + LINES + 2)
                    alone(sp, passed)
                    for q in range(4):
                        sp.dma_start(one(uy, b).rearrange("o h w -> h o w")[:, 8 * q:8 * q + 8], YB[:, 8 * q:8 * q + 8]).then_inc(uy_out, 16)
                    sp.wait_ge(uy_out, b * 64 + 64)
                    alone(sp, passed)
                    for q in range(4):
                        r = slice(32 * q, 32 * q + 32)
                        sp.dma_start(YB[r], one(uy, b)[:, 32 * q:32 * q + 32, :]).then_inc(uy_in, 16)
                    sp.wait_ge(summed, b + 1)
                    alone(sp, passed)
                    for q in range(4):
                        r = slice(32 * q, 32 * q + 32)
                        sp.dma_start(one(u, b)[q], U[r]).then_inc(u_out, 16)
                sp.wait_ge(u_out, B * 64)

            @block.gpsimd
            def _(g):
                g.memset(IX[96:97], 1.0).then_inc(ones, 1)
                with g.Fori(0, B) as b:
                    g.wait_ge(d_full, b * (S * L))
                    alone(g, passed)
                    for j in range(NCH):
                        k = j % 2
                        g.wait_ge(split, CHN * (b * NCH + j + 3))
                        alone(g, passed)
                        for part in range(3):
                            for q in range(4):
                                px = j * RC * W + 512 * q
                                g.dma_start(IX[32 * part:32 * part + 32, px:px + 512],
                                            parts[32 * q:32 * q + 32, k, part, :]).then_inc(p_out[k], 16)
                    for a in range(2):
                        g.wait_ge(normed, 2 * b + a + 1)
                        alone(g, passed)
                        img = XI[:, a].rearrange("p (h w) -> p h w", w=(32, W)[a])
                        with g.Fori(0, LINES // 2) as i:
                            for k in range(2):
                                n = b * S + a * LINES + 2 * i + k
                                g.wait_ge(z_full, 4 * n + 4)
                                alone(g, passed)
                                line = img[:, :, bass.ds(2 * i + k, 1)] if a == 0 else img[:, bass.ds(2 * i + k, 1), :]
                                g.tensor_copy(XS[:, k, :], line.rearrange("p h w -> p (h w)")).then_inc(line_in, 1)

            @block.scalar
            def _(act):
                act.sem_inc(d_read, 2)
                with act.Fori(0, B) as b:
                    for j in range(NCH):
                        k = j % 2
                        act.wait_ge(h_in[k], 16 * (b * (NCH // 2) + j // 2 + 1))
                        act.activation(HI[:, k], HI[:, k], ACT.Relu, bias=coef[0:64, 1:2], scale=coef[0:64, 0:1]).then_inc(relu, 1)
                    with act.Fori(0, LINES) as i:
                        for k in range(2):
                            for e, pts in enumerate(PAIRS):
                                m = (b * S + 2 * i + k) * L + e
                                w = 512 * len(pts)
                                act.wait_ge(d_full, m + 1)
                                act.wait_ge(t_used, m + 1)
                                act.activation(T[:, e, 0:w], ps_d[(k * L + e) % 2][:, 0:w], ACT.Abs).then_inc(d_read, 1)

            @block.vector
            def _(v):
                v.sem_inc(z_read, 2)
                v.sem_inc(o_read, 2)
                v.sem_inc(u_added, 2)
                v.sem_inc(split, 2 * CHN)

                def read_z(n, k, q):
                    v.wait_ge(z_full, 4 * n + q + 9)
                    if q == 0:
                        v.wait_ge(t_used, 5 * n)
                    v.tensor_copy(Zs[:, k, q], ps_z[q % 2][:, 0:32 * K9]).then_inc(z_read, 1)

                def read_o(a, n, j, k):
                    v.wait_ge(t_used, 5 * n + 10)
                    if a == 0:
                        v.tensor_copy(YB[:].rearrange("h o (q w) -> h q o w", q=4)[:, :, :, bass.ds(j, 1)].rearrange("h q o w -> h q (o w)"),
                                      ps_o[k][:, 0:P].rearrange("h (q o) -> h q o", q=4)).then_inc(o_read, 1)
                    else:
                        v.tensor_copy(XO[:, k], ps_o[k][:, 0:P]).then_inc(o_read, 1)

                def add_turned(b, j, k):
                    v.wait_ge(turned, b * LINES + j + 1)
                    uj = U[:, bass.ds(j, 1), :].rearrange("p j w -> p (j w)")
                    v.tensor_tensor(uj, ps_o[k][:, P:2 * P], uj, ALU.add).then_inc(u_added, 1)

                def two_steps(b, a, i, first, last):
                    for k in range(2):
                        j = 2 * i + k
                        n = b * S + a * LINES + j
                        ahead = not (a == 1 and last and k == 1)
                        behind = not (first and k == 0)
                        for e, pts in enumerate(PAIRS):
                            w = 512 * len(pts)
                            v.wait_ge(d_read, n * L + e + 3)
                            v.tensor_scalar(T[:, e, 0:w], T[:, e, 0:w], 1.0, 1.0, ALU.min, ALU.subtract).then_inc(hat, 1)
                            if e == 0 and behind:
                                read_o(a, n - 1, j - 1, 1 - k)
                            if e >= 1 and ahead:
                                read_z(n + 1, 1 - k, e - 1)
                            if e == 3 and behind and a == 1:
                                add_turned(b, j - 1, 1 - k)

                with v.Fori(0, B) as b:
                    for j in range(NCH):
                        k = j % 2
                        m = b * NCH + j
                        ch = Chain(v, split, CHN * (m + 2))
                        v.wait_ge(off, m + 3)
                        v.wait_ge(p_out[k], 192 * (b * (NCH // 2) + j // 2))
                        ch.done(v.scalar_tensor_tensor(out=t_ix[:], in0=ps_d[k][:, 0:512], scalar=wt["pb"][:, 0:1],
                                                       in1=wt["grid"][:, j, :], op0=ALU.add, op1=ALU.add))
                        ch.sync()
                        ch.done(v.tensor_copy(parts[:, k, 0], t_ix[:]))
                        ch.sync()
                        ch.done(v.tensor_tensor(t_r[:], t_ix[:], parts[:, k, 0], ALU.subtract))
                        ch.sync()
                        ch.done(v.tensor_copy(parts[:, k, 1], t_r[:]))
                        ch.sync()
                        ch.done(v.tensor_tensor(t_r2[:], t_r[:], parts[:, k, 1], ALU.subtract))
                        ch.sync()
                        ch.done(v.tensor_copy(parts[:, k, 2], t_r2[:]))
                        assert ch.n == CHN
                    for a in range(2):
                        v.wait_ge(i_in[a], 64 * (b + 1))
                        v.tensor_scalar(XI[:, a], XI[:, a], GS[:, 0, bass.ds(b, 1)], GS[:, 1, bass.ds(b, 1)],
                                        ALU.subtract, ALU.mult).then_inc(normed, 1)
                    for q in range(4):
                        read_z(b * S, 0, q)
                    for a in range(2):
                        two_steps(b, a, 0, True, False)
                        with v.Fori(1, LINES // 2 - 1) as i:
                            two_steps(b, a, i, False, False)
                        two_steps(b, a, LINES // 2 - 1, False, True)
                        read_o(a, b * S + a * LINES + LINES - 1, LINES - 1, 1)
                        if a == 0:
                            v.wait_ge(u_in, 64 * (b + 1))
                    add_turned(b, LINES - 1, 1)
                    v.wait_ge(uy_in, 64 * (b + 1))
                    v.wait_ge(u_added, (b + 1) * LINES + 2)
                    v.tensor_tensor(U[:].rearrange("p j w -> p (j w)"), U[:].rearrange("p j w -> p (j w)"),
                                    YB[:].rearrange("p j w -> p (j w)"), ALU.add).then_inc(summed, 1)
                    v.wait_ge(summed, b + 1)
                    for q in range(8):
                        v.bn_stats(st[:, bass.ds(b * 8 + q, 1), :].rearrange("p a s -> p (a s)"),
                                   U[:].rearrange("p j w -> p (j w)")[:, 512 * q:512 * q + 512]).then_inc(counted, 1)

            @block.tensor
            def _(pe):
                pe.sem_inc(off, 2)
                pe.sem_inc(z_full, 8)
                pe.sem_inc(t_used, L)
                pe.wait_ge(ones, 1)

                def spread(a, n, j, k, e):
                    pe.wait_ge(d_read, n * L + e + 1)
                    if a == 0:
                        ix = IX[:].rearrange("r (h q w) -> r q h w", q=4, w=32)[:, :, :, bass.ds(j, 1)].rearrange("r q h w -> r q (h w)")
                    else:
                        ix = IX[:].rearrange("r (q h w) -> r q h w", q=4, w=W)[:, :, bass.ds(j, 1), :].rearrange("r q h w -> r q (h w)")
                    for x, pt in enumerate(PAIRS[e]):
                        mm = pe.matmul(ps_d[(k * L + e) % 2][:, 512 * x:512 * x + 512], wt["sel"][:, K9 * a + pt, :], ix,
                                       start=True, stop=True)
                    mm.then_inc(d_full, 1)

                def make_z(a, n, k, q):
                    r = slice(32 * q, 32 * q + 32)
                    if q == 0:
                        pe.wait_ge(line_in, n + 1)
                    pe.wait_ge(z_read, 4 * n + q + 1)
                    alone(pe, passed)
                    pe.matmul(ps_z[q % 2][:, 0:32 * K9], XS[r, k, :], wt["Z"][r, a, :], start=True, stop=True,
                              tile_position=(32 * q, 0)).then_inc(z_full, 1)

                def apply(a, b, n, j, k, e):
                    pe.wait_ge(hat, n * L + e + 1)
                    if e == 0:
                        pe.wait_ge(z_read, 4 * n + 6)
                        pe.wait_ge(o_read, n + 1)
                        if a == 1:
                            pe.wait_ge(u_added, b * LINES + j + 1)
                    for x, pt in enumerate(PAIRS[e]):
                        for q in range(4):
                            c = 512 * x + 128 * q
                            mm = pe.matmul(ps_o[k][:, 32 * q:32 * q + 32], T[:, e, c:c + 128], Zs[:, k, q, 32 * pt:32 * pt + 32],
                                           start=(pt == 0 and q == 0), stop=(pt == K9 - 1), skip_group_check=True)
                    mm.then_inc(t_used, 1)

                def turn(n, k):
                    pe.wait_ge(o_read, n + 3)
                    alone(pe, passed)
                    pe.transpose(ps_o[k][:, P:2 * P], XO[:, k], wt["eye"][:]).then_inc(turned, 1)

                def two_steps(b, a, i, first, last):
                    for k in range(2):
                        j = 2 * i + k
                        n = b * S + a * LINES + j
                        nxt = (1, 0) if a == 0 and last and k == 1 else None if last and k == 1 else (a, j + 1)
                        for e in range(L):
                            if e + 2 < L:
                                spread(a, n, j, k, e + 2)
                            elif nxt:
                                spread(nxt[0], n + 1, nxt[1], 1 - k, e + 2 - L)
                            apply(a, b, n, j, k, e)
                            if e < 4 and nxt:
                                make_z(nxt[0], n + 1, 1 - k, e)
                            if a == 1 and e == 1 and not (first and k == 0):
                                turn(n - 1, 1 - k)

                with pe.Fori(0, B) as b:
                    pe.wait_ge(d_read, b * (S * L) + 2)
                    for j in range(NCH):
                        k = j % 2
                        m = b * NCH + j
                        pe.wait_ge(relu, m + 1)
                        pe.wait_ge(split, CHN * (m + 1))
                        alone(pe, passed)
                        for q in range(4):
                            mm = pe.matmul(ps_d[k][32 * q:32 * q + 32, 0:512], wt["pw"][:], HI[:, k, 512 * q:512 * q + 512],
                                           start=True, stop=True)
                        mm.then_inc(off, 1)
                    for q in range(4):
                        make_z(0, b * S, 0, q)
                    for k in range(2):
                        pe.wait_ge(p_out[k], 192 * (NCH // 2) * (b + 1))
                    pe.wait_ge(split, CHN * NCH * (b + 1) + 2 * CHN)
                    for e in range(2):
                        spread(0, b * S, 0, 0, e)
                    for a in range(2):
                        two_steps(b, a, 0, True, False)
                        with pe.Fori(1, LINES // 2 - 1) as i:
                            two_steps(b, a, i, False, False)
                        two_steps(b, a, LINES // 2 - 1, False, True)
                    turn(b * S + 2 * LINES - 1, 1)


def dft_constants():
    two_pi = 2 * np.pi
    kx = np.concatenate([np.arange(M1), np.arange(H - M1, H)])
    h = np.arange(H)
    ang = two_pi * ((h[:, None] * kx[None]) % H) / H
    dft_h = np.stack([-np.sin(ang), np.cos(ang), np.sin(ang)], 2).reshape(H, -1)
    aw = two_pi * ((np.arange(W)[:, None] * np.arange(M2)[None]) % W) / W
    dft_wp = np.concatenate([np.cos(aw), -np.sin(aw)], 1)
    dft_wq = np.concatenate([np.sin(aw), np.cos(aw)], 1)
    kp = np.array([2 * j + par + hl * (H - M1) for hl in range(2) for par in range(2) for j in range(M1 // 2)])
    ah = two_pi * ((kp[:, None] * h[None]) % H) / H
    inv_hr = np.concatenate([np.cos(ah), -np.sin(ah)], 0)
    inv_hi = np.concatenate([np.sin(ah), np.cos(ah)], 0)
    cy = np.where(np.arange(M2) == 0, 1.0, 2.0)[:, None] / (H * W)
    inv_w = np.tile(np.concatenate([cy * np.cos(aw.T), -cy * np.sin(aw.T)], 0), (2, 1))
    return dict(
        dft_h=dft_h, dft_wp=dft_wp, dft_wq=dft_wq, inv_hr=inv_hr, inv_hi=inv_hi, inv_w=inv_w,
        avg=np.full((P, P), 1.0 / P))


def weight_layouts(inp):
    f = lambda a: np.ascontiguousarray(a, np.float32)
    c = lambda n: np.asarray(inp["L2_conv_" + n])
    fus = c("fus_w")[:, :, 0, 0]
    out = {}
    out["fusT"] = f(fus.reshape(C, 3, C).transpose(2, 1, 0)).reshape(C, 3 * C)
    dsc = np.stack([c("dscy_w"), c("dscx_w")]).transpose(1, 0, 3, 2)
    out["dsc"] = f(np.tile(dsc, (1, 1, 1, 4))).reshape(C, -1)
    out["convw"] = f(c("conv_w").transpose(0, 3, 2, 1)).reshape(C, -1)
    out["conv_b"] = f(c("conv_b").reshape(C, 1))
    dw = np.stack([c("offx_dw_w")[:, 0], c("offy_dw_w")[:, 0]])
    out["dw"] = f(dw.transpose(2, 1, 0, 3)).reshape(96, 6)
    out["b96"] = f(np.concatenate([c("offx_dw_b"), c("offy_dw_b"), np.zeros(C)])[:, None])
    pw = np.zeros((64, 32))
    pw[0:32, 0:K9] = c("offx_pw_w")[:, :, 0, 0].T
    pw[32:64, K9:2 * K9] = c("offy_pw_w")[:, :, 0, 0].T
    out["pw"] = f(pw)
    pb = np.zeros(32)
    pb[0:K9], pb[K9:2 * K9] = c("offx_pw_b"), c("offy_pw_b")
    out["pb"] = f(np.tile(pb, 4)[:, None])
    out["gbo"] = f(np.stack([np.concatenate([c("offx_bn_g"), c("offy_bn_g")]),
                             np.concatenate([c("offx_bn_b"), c("offy_bn_b")])], 1))
    out["gbf"] = f(np.tile(np.stack([c("fus_bn_g"), c("fus_bn_b")], 1), (4, 1)))
    out["gb1"] = f(np.tile(np.stack([inp["L1_conv_gamma"], inp["L1_conv_beta"]], 1), (4, 1)))
    w1 = np.asarray(inp["L1_conv_conv_w"])[:, :, :, 0]
    out["l1_w"] = f(np.concatenate([w1.transpose(2, 1, 0).reshape(96, C), np.asarray(inp["L1_conv_conv_b"])[None]], 0))
    fr = np.asarray(inp["L3_conv_freq_weight"]).reshape(C, C, 12)
    out["freqT"] = f(np.tile(fr.transpose(2, 0, 1), (1, 1, 4))).reshape(12, -1)
    return out


def shape_constants():
    out = dft_constants()
    p = np.arange(P)
    out["share"] = (p[:, None] % 32 == p[None] % 32) / 4.0
    out["pair"] = ((p[:, None] % 32) // 2 == (p[None] % 32) // 2) / 8.0
    out["eye"] = np.eye(P)
    out["idm"] = (np.arange(96)[:, None] % 32 == np.arange(32)[None]) * 1.0
    sel = np.zeros((97, 2 * K9, P))
    for a in range(2):
        for k in range(K9):
            for part in range(3):
                sel[32 * part + (K9 if a == 0 else 0) + k, K9 * a + k] = 1.0
    sel[96] = -np.arange(P)
    out["select"] = sel.reshape(97, -1)
    grid = np.zeros((4, 32, NCH, 4, W))
    grid[:, 0:K9] = np.arange(W)
    rows = RC * np.arange(NCH)[None, :, None] + 4 * np.arange(4)[:, None, None] + np.arange(4)[None, None, :]
    grid[:, K9:2 * K9] = rows[:, None, :, :, None]
    out["grid"] = grid.reshape(P, -1)
    out["freq_to_taps"] = freq_to_taps()
    return {k: np.ascontiguousarray(v, np.float32) for k, v in out.items()}


def freq_to_taps():
    K = 3
    basis = np.zeros((12, K, 2), complex)
    for f in range(12):
        basis[f, f // 4, (f // 2) % 2] = 1.0 if f % 2 == 0 else 1j
    kern = np.fft.irfft2(basis, s=(K, K), axes=(-2, -1)).astype(np.float32)
    th = np.array([i * np.pi / 4 for i in range(8)], np.float32)[:, None]
    sc = np.array([1.0, 1.25, 1.25 ** 2, 1.25 ** 3], np.float32)[None]
    cos_t, sin_t = (np.cos(th) * sc).reshape(-1), (np.sin(th) * sc).reshape(-1)
    co = ((2 * np.arange(K, dtype=np.float32) + 1) / np.float32(K) - 1).astype(np.float32)
    gy, gx = np.meshgrid(co, co, indexing="ij")
    out = np.zeros((12, K, K))
    for c, s in zip(cos_t, sin_t):
        ix = (((c * gx - s * gy) + 1) * K - 1) * np.float32(0.5)
        iy = (((s * gx + c * gy) + 1) * K - 1) * np.float32(0.5)
        x0, y0 = np.floor(ix).astype(int), np.floor(iy).astype(int)
        wx1, wy1 = ix - x0, iy - y0
        for yy, wy in ((y0, 1 - wy1), (y0 + 1, wy1)):
            for xx, wx in ((x0, 1 - wx1), (x0 + 1, wx1)):
                ok = (xx >= 0) & (xx < K) & (yy >= 0) & (yy < K)
                out += np.where(ok, kern[:, np.clip(yy, 0, K - 1), np.clip(xx, 0, K - 1)], 0) * (wy * wx)
    return (out / len(cos_t)).reshape(12, 9)


def network(nc, x, w, d, out):
    dram = lambda name, shape: nc.dram_tensor(name, shape, F32).ap()
    spec = dram("spec", (M1 // 2, P, 2 * M2 * B))
    gstat = dram("gstat", (B, 1, 4 * B))
    x1, x2, x3 = (dram(f"x_{n}", (B, C, H, W)) for n in (1, 2, 3))
    y1 = dram("y_1", (B, P, NCH, 512))
    hs = dram("branches", (B, 96, PX))
    uy = dram("u_y", (B, C, H, W))
    u = dram("u", (B, 4, C, LINES, W))
    with ExitStack() as sems, Stage(nc, sems, "net") as s:
        with Stage(nc, sems, "l0") as s0:
            F = s0.sb("f", [P, M1 * M2, 2, B])
            spectral_forward(nc, sems, x, d, F)
            spectral_mix(nc, sems, w, F, spec)
        spectral_inverse(nc, sems, x, spec, d, d["l0_bias"], x1, gstat)
        layer_rest(nc, sems, s, d, (spec, gstat, x1, x2, x3, y1, hs, uy, u), out)


def layer_rest(nc, sems, s, d, bufs, out, upto=9):
    spec, gstat, x1, x2, x3, y1, hs, uy, u = bufs
    wt = {n: s.sb(n, sh, dt) for n, sh, dt in (
        ("grid", [P, NCH, 512], F32), ("pw", [64, 32], F32), ("pb", [P, 1], F32), ("share", [P, P], F32),
        ("gb1", [P, 2], F32), ("gbo", [64, 2], F32), ("gbf", [P, 2], F32), ("eye", [P, P], F32),
        ("Z", [P, 2, 32 * K9], F32), ("L2", [96, 3, 96], F32), ("b2", [96, 1], F32), ("L3", [P, 3, 64], F32),
        ("sel", [97, 2 * K9, P], BF16))}
    GS = s.sb("GS", [P, 2, B])
    st1, sto, stf = s.sb("st1", [P, B * NCH, 6]), s.sb("sto", [64, B * NCH * 4, 6]), s.sb("stf", [P, B * 8, 6])
    co1, coo, cof = s.sb("co1", [P, 2]), s.sb("coo", [64, 2]), s.sb("cof", [P, 2])
    mod4 = lambda t: t.rearrange("b c (h q) w -> b q c h w", q=4)
    div4 = lambda t: t.rearrange("b c (q h) w -> b q c h w", q=4)
    load_weights(nc, sems, d, wt)
    graph_conv(nc, sems, x1, gstat, wt, d, y1, st1)
    norm_coefficients(nc, sems, "n1", st1, P, wt["share"][:], wt["gb1"], co1)
    residual_norm(nc, sems, "r1", y1.rearrange("b p j n -> b p (j n)"), co1, mod4(x1), mod4(x2), d["pair"], GS)
    depth_conv(nc, sems, x2, GS, wt["L2"], wt["b2"], hs, sto)
    norm_coefficients(nc, sems, "no", sto, 64, wt["eye"][0:64, 0:64], wt["gbo"], coo)
    deformable(nc, sems, (x2, hs, u), coo, GS, wt, uy, stf)
    norm_coefficients(nc, sems, "nf", stf, P, wt["share"][:], wt["gbf"], cof)
    residual_norm(nc, sems, "r2", u.rearrange("b q o h w -> b (q o) (h w)"), cof, div4(x2), div4(x3), d["pair"], GS)
    last_conv(nc, sems, x3, GS, wt["L3"], out)


def kernel(**inputs):
    import concourse.bacc as _bacc
    from concourse.bass_utils import run_bass_kernel_spmd as _run

    nc = _bacc.Bacc("TRN2", target_bir_lowering=False, num_devices=1)
    arrays = {}

    def given(name, a):
        a = np.ascontiguousarray(a)
        arrays[f"in_{name}"] = a
        return nc.dram_tensor(f"in_{name}", a.shape, mybir.dt.from_np(a.dtype), kind="ExternalInput").ap()

    x = given("x", inputs["x"])
    w = [given(n, inputs["L0_conv_" + n]) for n in ("w1r", "w1i", "w2r", "w2i")]
    d = {n: given(n, a) for n, a in {**weight_layouts(inputs), **shape_constants()}.items()}
    d["l0_bias"] = given("l0_bias", np.asarray(inputs["L0_conv_bias"]).reshape(1, C))
    d["l1_A"] = given("l1_A", inputs["L1_conv_A"])
    out = nc.dram_tensor("out_0", (B, C, H, W), F32, kind="ExternalOutput").ap()
    network(nc, x, w, d, out)
    r = _run(nc, [arrays], core_ids=[0])
    return r.results[0]["out_0"]
```

```python
from contextlib import ExitStack

import numpy as np

import concourse.bass as bass
from concourse import mybir

F32 = mybir.dt.float32
BF16 = mybir.dt.bfloat16
ALU = mybir.AluOpType
ACT = mybir.ActivationFunctionType

B, C, H, W = 8, 32, 128, 128
P = 128
PX = H * W
G = 16
M1, M2 = 32, 32
KX = 2 * M1
K9 = 9
EPS = 1e-5


class Chain:

    def __init__(self, eng, sem, base=0):
        self.eng, self.sem, self.base, self.n = eng, sem, base, 0

    def done(self, ins):
        ins.then_inc(self.sem, 1)
        self.n += 1

    def sync(self):
        self.eng.wait_ge(self.sem, self.base + self.n)


def alone(eng, passed):
    eng.sem_inc(passed, 1)


def one(ap, i):
    dims = "abcdefg"[:len(ap.shape)]
    left = " ".join(dims)
    right = "(" + " ".join(dims[:2]) + ") " + " ".join(dims[2:])
    return ap[(bass.ds(i, 1),) + (slice(None),) * (len(dims) - 1)].rearrange(f"{left} -> {right}")


class Stage:

    def __init__(self, nc, sems, name):
        self.nc, self.sems, self.name, self.ctx = nc, sems, name, ExitStack()

    def __enter__(self):
        return self

    def __exit__(self, *e):
        self.ctx.close()

    def sb(self, name, shape, dt=F32):
        return self.ctx.enter_context(self.nc.sbuf_tensor(f"{self.name}_{name}", shape, dt))

    def ps(self, name, shape):
        return self.ctx.enter_context(self.nc.psum_tensor(f"{self.name}_{name}", shape, F32))

    def sem(self, name):
        return self.sems.enter_context(self.nc.semaphore(f"{self.name}_{name}"))

    def block(self):
        return self.nc.Block()



def spectral_forward(nc, sems, x, consts, F):
    with Stage(nc, sems, "fw") as s:
        X = s.sb("x", [P, 2, C, W])
        rows = s.sb("rows", [P, KX * 3, C])
        dh = s.sb("dh", [P, KX * 3])
        dwp = s.sb("dwp", [P, 2 * M2])
        dwq = s.sb("dwq", [P, 2 * M2])
        avg = s.sb("avg", [P, P])
        st = s.sb("st", [P, G, 6])
        ag = s.sb("ag", [P, G, 2])
        mean = s.sb("mean", [P, G])
        dev = s.sb("dev", [P, G])
        rstd = s.sb("rstd", [P, G])
        ps_s = s.ps("s", [P, 512])
        ps_r = [s.ps(f"r{k}", [P, 512]) for k in range(2)]
        ps_f = [s.ps(f"f{k}", [P, 512]) for k in range(2)]
        c_in, passed = s.sem("c_in"), s.sem("passed")
        x_in = [s.sem(f"x_in{k}") for k in range(2)]
        stats, sums, rooted, normed = s.sem("stats"), s.sem("sums"), s.sem("rooted"), s.sem("normed")
        r_full, r_read, f_full, f_read, r_used = (s.sem(n) for n in ("r_full", "r_read", "f_full", "f_read", "r_used"))
        NR, NF = C // 2, KX // 2 // 8

        with s.block() as block:
            @block.sync
            def _(sp):
                for t, a in ((dh, "dft_h"), (dwp, "dft_wp"), (dwq, "dft_wq"), (avg, "avg")):
                    sp.dma_start(t[:], consts[a]).then_inc(c_in, 16)
                for k in range(2):
                    for c in range(0, C, 8):
                        sp.dma_start(X[:, k, c:c + 8], x[k].rearrange("c h w -> h c w")[:, c:c + 8]).then_inc(x_in[k], 16)
                with sp.Fori(1, B // 2) as i:
                    for k in range(2):
                        sp.wait_ge(r_full, (2 * i + k - 1) * NR)
                        alone(sp, passed)
                        for c in range(0, C, 8):
                            sp.dma_start(X[:, k, c:c + 8], one(x, 2 * i + k).rearrange("c h w -> h c w")[:, c:c + 8]).then_inc(x_in[k], 16)

            @block.vector
            def _(v):
                with v.Fori(0, B // 2) as i:
                    ch = Chain(v, stats, i * (2 * 38))
                    for k in range(2):
                        n = 2 * i + k
                        v.wait_ge(x_in[k], 64 * (i + 1))
                        for g in range(G):
                            ch.done(v.bn_stats(st[:, g], X[:, k, 2 * g:2 * g + 2, :].rearrange("p a w -> p (a w)")))
                        ch.sync()
                        alone(v, passed)
                        for g in range(G):
                            ch.done(v.bn_aggr(ag[:, g], st[:, g]))
                        ch.sync()
                        v.wait_ge(sums, 2 * n + 1)
                        ch.done(v.tensor_copy(mean[:], ps_s[:, 0:G]))
                        ch.sync()
                        ch.done(v.tensor_tensor(dev[:], ag[:, :, 0], mean[:], ALU.subtract))
                        ch.sync()
                        ch.done(v.tensor_tensor(dev[:], dev[:], dev[:], ALU.mult))
                        ch.sync()
                        ch.done(v.tensor_tensor(dev[:], dev[:], ag[:, :, 1], ALU.add))
                        v.wait_ge(sums, 2 * n + 2)
                        ch.done(v.tensor_scalar(rstd[:], ps_s[:, G:2 * G], EPS, None, ALU.add))
                        ch.sync()
                        v.wait_ge(rooted, n + 1)
                        ch.done(v.reciprocal(rstd[:], rstd[:]))
                        ch.sync()
                        for g in range(G):
                            xg = X[:, k, 2 * g:2 * g + 2, :]
                            v.tensor_scalar(xg, xg, mean[:, g:g + 1], rstd[:, g:g + 1],
                                            ALU.subtract, ALU.mult).then_inc(normed, 1)
                    assert ch.n == 2 * 38

            @block.tensor
            def _(pe):
                pe.wait_ge(c_in, 64)
                with pe.Fori(0, B // 2) as i:
                    for k in range(2):
                        n = 2 * i + k
                        pe.wait_ge(stats, 38 * n + 32)
                        pe.matmul(ps_s[:, 0:G], avg[:], ag[:, :, 0], start=True, stop=True).then_inc(sums, 1)
                        pe.wait_ge(stats, 38 * n + 36)
                        pe.matmul(ps_s[:, G:2 * G], avg[:], dev[:], start=True, stop=True).then_inc(sums, 1)
                        for c in range(C):
                            j = c // 2
                            if c % 2 == 0:
                                pe.wait_ge(normed, G * n + j + 1)
                                pe.wait_ge(r_read, NR * n + j + 1)
                            mm = pe.matmul(ps_r[j % 2][:, (c % 2) * KX * 3:(c % 2 + 1) * KX * 3],
                                           X[:, k, c, :], dh[:], start=True, stop=True)
                            if c % 2:
                                mm.then_inc(r_full, 1)
                        for j in range(NF):
                            if j == 0:
                                pe.wait_ge(r_read, NR * (n + 1) + 2)
                            pe.wait_ge(f_read, NF * n + j + 1)
                            for q in range(8):
                                for half in range(2):
                                    kx = (8 * j + q) + M1 * half
                                    out = ps_f[j % 2][64 * half:64 * half + 64, 64 * q:64 * q + 64]
                                    pe.matmul(out, rows[:, 3 * kx + 1:3 * kx + 3, :], dwp[:], start=True, stop=False)
                                    mm = pe.matmul(out, rows[:, 3 * kx:3 * kx + 2, :], dwq[:], start=False, stop=True)
                            mm.then_inc(f_full, 1)

            @block.scalar
            def _(a):
                a.sem_inc(r_read, 2)
                a.sem_inc(f_read, 2)
                with a.Fori(0, B) as n:
                    a.wait_ge(stats, 38 * n + 37)
                    a.activation(rstd[:], rstd[:], ACT.Sqrt).then_inc(rooted, 1)
                    for j in range(NR):
                        a.wait_ge(r_full, NR * n + j + 1)
                        if j == 0:
                            a.wait_ge(f_full, NF * n)
                        a.activation(rows[:, :, 2 * j:2 * j + 2].rearrange("p k c -> p c k"),
                                     ps_r[j % 2][:, 0:2 * KX * 3].rearrange("p (c k) -> p c k", c=2),
                                     ACT.Copy).then_inc(r_read, 1)
                    for j in range(NF):
                        a.wait_ge(f_full, NF * n + j + 1)
                        for r in range(2):
                            ins = a.activation(
                                F[:, 8 * M2 * j:8 * M2 * (j + 1), r, bass.ds(n, 1)].rearrange("p (k y) b -> p k (y b)", k=8),
                                ps_f[j % 2][:].rearrange("p (k r y) -> p k r y", k=8, r=2)[:, :, r, :],
                                ACT.Copy)
                        ins.then_inc(f_read, 1)

def spectral_mix(nc, sems, w, F, spec):
    NP = M1 // 2
    CH = 4
    with Stage(nc, sems, "mx") as s:
        WT = s.sb("w", [P, 2, C, CH * M2])
        FC = s.sb("fc", [P, 2, CH * M2, 2 * B])
        out = s.sb("out", [P, 2, 2, M2, B])
        ps = [s.ps(f"m{k}", [P, 512]) for k in range(2)]
        w_in = [s.sem(f"w_in{k}") for k in range(2)]
        passed, f_in, full, read, sent = s.sem("passed"), s.sem("f_in"), s.sem("full"), s.sem("read"), [s.sem(f"sent{k}") for k in range(2)]
        with s.block() as block:
            @block.sync
            def _(sp):
                def load(n, k):
                    for q in range(4):
                        for x in range(2):
                            src = w[q].rearrange("c o (n x) y -> n c o (x y)", x=CH)
                            sp.dma_start(WT[32 * q:32 * q + 32, k, 16 * x:16 * x + 16],
                                         one(src, n)[:, 16 * x:16 * x + 16]).then_inc(w_in[k], 16)
                for k in range(2):
                    load(k, k)
                with sp.Fori(1, M1 // CH // 2) as i:
                    for k in range(2):
                        sp.wait_ge(full, (2 * i + k - 1) * (CH // 2))
                        alone(sp, passed)
                        load(2 * i + k, k)

            @block.gpsimd
            def _(g):
                for k in range(2):
                    g.tensor_copy(FC[:, k], F[:, k * CH * M2:(k + 1) * CH * M2].rearrange("p m r b -> p m (r b)")).then_inc(f_in, 1)
                with g.Fori(1, M1 // CH // 2) as i:
                    for k in range(2):
                        g.wait_ge(full, (2 * i + k - 1) * (CH // 2))
                        alone(g, passed)
                        g.tensor_copy(FC[:, k], F[:, bass.ds((2 * i + k) * (CH * M2), CH * M2)].rearrange("p m r b -> p m (r b)")).then_inc(f_in, 1)

            @block.tensor
            def _(pe):
                pe.sem_inc(read, 2)
                with pe.Fori(0, M1 // CH // 2) as i:
                    for k in range(2):
                        pe.wait_ge(w_in[k], 128 * (i + 1))
                        pe.wait_ge(f_in, 2 * i + k + 1)
                        for j in range(CH // 2):
                            n = (2 * i + k) * (CH // 2) + j
                            pe.wait_ge(read, n + 1)
                            alone(pe, passed)
                            for par in range(2):
                                for ky in range(M2):
                                    m = (2 * j + par) * M2 + ky
                                    for half in range(2):
                                        r = slice(64 * half, 64 * half + 64)
                                        o = 64 * par + 32 * half
                                        mm = pe.matmul(ps[j % 2][o:o + 32, 16 * ky:16 * ky + 16], WT[r, k, :, m],
                                                       FC[r, k, m, :], start=True, stop=True,
                                                       tile_position=(64 * half, o))
                            mm.then_inc(full, 1)

            @block.vector
            def _(v):
                with v.Fori(0, NP // 2) as i:
                    for k in range(2):
                        n = 2 * i + k
                        v.wait_ge(full, n + 1)
                        v.wait_ge(sent[k], 16 * i)
                        for r in range(2):
                            ins = v.tensor_copy(out[:, k, r], ps[k][:].rearrange("p (y r b) -> p y r b", r=2, b=B)[:, :, r, :])
                        ins.then_inc(read, 1)

            @block.scalar
            def _(a):
                with a.Fori(0, NP // 2) as i:
                    for k in range(2):
                        a.wait_ge(read, 2 * i + k + 3)
                        a.dma_start(one(spec, 2 * i + k), out[:, k].rearrange("p r y b -> p (r y b)")).then_inc(sent[k], 16)
                for k in range(2):
                    a.wait_ge(sent[k], 16 * (NP // 2))


def spectral_inverse(nc, sems, x, spec, consts, bias, x1, gstat):
    OC = 4
    with Stage(nc, sems, "iv") as s:
        Gk = s.sb("g", [P, 2, OC, M2, B])
        X = s.sb("x", [P, 2, B, OC, W])
        Z = s.sb("z", [P, 2, 4, H])
        er, ei, ew = (s.sb(n, [P, P]) for n in ("er", "ei", "ew"))
        avg = s.sb("avg", [P, P])
        bs = s.sb("bs", [P, C])
        NG = 2 * B
        st = s.sb("st", [P, NG, 6])
        ag = s.sb("ag", [P, NG, 2])
        mean, dev = s.sb("mean", [P, NG]), s.sb("dev", [P, NG])
        res = s.sb("res", [P, 2, 2, B])
        ps_z = [s.ps(f"z{k}", [P, 512]) for k in range(2)]
        ps_y = [s.ps(f"y{k}", [P, 512]) for k in range(4)]
        ps_s = s.ps("s", [P, 512])
        c_in, passed = s.sem("c_in"), s.sem("passed")
        in_ = [s.sem(f"in{k}") for k in range(2)]
        z_full, z_done, y_full, y_done, stats, sums, rooted, r_sent = (
            s.sem(n) for n in ("z_full", "z_done", "y_full", "y_done", "stats", "sums", "rooted", "r_sent"))
        sent = [s.sem(f"sent{k}") for k in range(2)]
        NZ = B * OC // 8
        CHN = 2 * NG + 7

        with s.block() as block:
            @block.sync
            def _(sp):
                for t, a in ((er, "inv_hr"), (ei, "inv_hi"), (ew, "inv_w"), (avg, "avg")):
                    sp.dma_start(t[:], consts[a]).then_inc(c_in, 16)
                sp.dma_start(bs[:], bias.partition_broadcast(P)).then_inc(c_in, 16)

                def load(n, k):
                    src = spec.rearrange("j (par hl n o) f -> n par hl j o f", par=2, hl=2, o=OC)
                    for ri in range(2):
                        for hl in range(2):
                            for par in range(2):
                                p0 = 64 * ri + 32 * hl + 16 * par
                                sp.dma_start(Gk[p0:p0 + 16, k].rearrange("p o y b -> p o (y b)"),
                                             one(src, n)[par, hl, :, :, ri * M2 * B:(ri + 1) * M2 * B]).then_inc(in_[k], 16)
                    xs = x.rearrange("b (n o) h w -> n h b o w", o=OC)
                    for b in range(B):
                        sp.dma_start(X[:, k, b], one(xs, n)[:, b]).then_inc(in_[k], 16)
                for k in range(2):
                    load(k, k)
                with sp.Fori(1, C // OC // 2) as i:
                    for k in range(2):
                        sp.wait_ge(sent[k], 16 * B * i)
                        alone(sp, passed)
                        sp.wait_ge(stats, CHN * (2 * i + k - 1))
                        alone(sp, passed)
                        load(2 * i + k, k)

            @block.tensor
            def _(pe):
                pe.wait_ge(c_in, 80)
                pe.sem_inc(z_done, 2)
                pe.sem_inc(y_done, 4)
                with pe.Fori(0, C // OC // 2) as i:
                    for k in range(2):
                        n = 2 * i + k
                        pe.wait_ge(in_[k], 256 * (i + 1))

                        def over_h(j):
                            pe.wait_ge(z_done, NZ * n + j + 1)
                            for m in range(8):
                                b, o = divmod(8 * j + m, OC)
                                for r, e in enumerate((er, ei)):
                                    p0 = 64 * (m % 2) + 32 * r
                                    mm = pe.matmul(ps_z[j % 2][p0:p0 + 32, 128 * (m // 2):128 * (m // 2) + 128],
                                                   Gk[:, k, o, :, b], e[:], start=True, stop=True)
                            mm.then_inc(z_full, 1)

                        def over_w(j):
                            pe.wait_ge(z_done, NZ * n + j + 3)
                            pe.wait_ge(y_done, 2 * NZ * n + 2 * j + 2)
                            for m in range(8):
                                h = slice(64 * (m % 2), 64 * (m % 2) + 64)
                                q = 128 * (m // 2)
                                mm = pe.matmul(ps_y[(2 * j + m % 2) % 4][:, q:q + 128], Z[h, j % 2, m // 2, :],
                                               ew[h, :], start=True, stop=True)
                                if m >= 6:
                                    mm.then_inc(y_full, 1)
                        over_h(0)
                        for j in range(NZ):
                            if j + 1 < NZ:
                                over_h(j + 1)
                            over_w(j)
                        pe.wait_ge(stats, CHN * n + 2 * NG)
                        pe.matmul(ps_s[:, 0:NG], avg[:], ag[:, :, 0], start=True, stop=True).then_inc(sums, 1)
                        pe.wait_ge(stats, CHN * n + 2 * NG + 4)
                        pe.matmul(ps_s[:, NG:2 * NG], avg[:], dev[:], start=True, stop=True).then_inc(sums, 1)

            @block.scalar
            def _(a):
                with a.Fori(0, C // OC) as n:
                    for j in range(NZ):
                        a.wait_ge(z_full, NZ * n + j + 1)
                        if j >= 2:
                            a.wait_ge(y_full, 2 * (NZ * n + j - 1))
                        a.activation(Z[:, j % 2].rearrange("p m h -> p (m h)"), ps_z[j % 2][:], ACT.Copy).then_inc(z_done, 1)
                    a.wait_ge(stats, CHN * (n + 1) - 1)
                    a.activation(res[:, :, 1], res[:, :, 1], ACT.Sqrt).then_inc(rooted, 1)

            @block.vector
            def _(v):
                v.wait_ge(c_in, 80)
                with v.Fori(0, C // OC // 2) as i:
                    ch = Chain(v, stats, i * (2 * CHN))
                    for k in range(2):
                        n = 2 * i + k
                        v.wait_ge(in_[k], 256 * (i + 1))
                        for y in range(2 * NZ):
                            v.wait_ge(y_full, 2 * NZ * n + y + 1)
                            for q in range(4):
                                o = y % 2 + 2 * (q % 2)
                                xo = X[:, k, 2 * (y // 2) + q // 2, o, :]
                                ins = v.scalar_tensor_tensor(out=xo, in0=ps_y[y % 4][:, 128 * q:128 * q + 128],
                                                             scalar=bs[:, bass.ds(n * OC + o, 1)],
                                                             in1=xo, op0=ALU.add, op1=ALU.add)
                            ins.then_inc(y_done, 1)
                        v.wait_ge(y_done, 2 * NZ * (n + 1) + 4)
                        for g in range(NG):
                            ch.done(v.bn_stats(st[:, g], X[:, k, g // 2, 2 * (g % 2):2 * (g % 2) + 2, :].rearrange("p o w -> p (o w)")))
                        ch.sync()
                        alone(v, passed)
                        for g in range(NG):
                            ch.done(v.bn_aggr(ag[:, g], st[:, g]))
                        ch.sync()
                        v.wait_ge(sums, 2 * n + 1)
                        ch.done(v.tensor_copy(mean[:], ps_s[:, 0:NG]))
                        ch.sync()
                        ch.done(v.tensor_tensor(dev[:], ag[:, :, 0], mean[:], ALU.subtract))
                        ch.sync()
                        ch.done(v.tensor_tensor(dev[:], dev[:], dev[:], ALU.mult))
                        ch.sync()
                        ch.done(v.tensor_tensor(dev[:], dev[:], ag[:, :, 1], ALU.add))
                        ch.sync()
                        v.wait_ge(r_sent, 16 * n)
                        ch.done(v.tensor_copy(res[:, :, 0], mean[:].rearrange("p (b q) -> p q b", q=2)))
                        v.wait_ge(sums, 2 * n + 2)
                        ch.done(v.tensor_scalar(res[:, :, 1], ps_s[:, NG:2 * NG].rearrange("p (b q) -> p q b", q=2), EPS, None, ALU.add))
                        v.wait_ge(rooted, n + 1)
                        ch.done(v.reciprocal(res[:, :, 1], res[:, :, 1]))
                    assert ch.n == 2 * CHN

            @block.gpsimd
            def _(g):
                with g.Fori(0, C // OC // 2) as i:
                    for k in range(2):
                        n = 2 * i + k
                        g.wait_ge(y_done, 2 * NZ * (n + 1) + 4)
                        alone(g, passed)
                        for b in range(B):
                            g.dma_start(one(x1.rearrange("b (n o) h w -> n h b o w", o=OC), n)[:, b], X[:, k, b]).then_inc(sent[k], 16)
                        g.wait_ge(stats, CHN * (n + 1))
                        alone(g, passed)
                        g.dma_start(one(gstat, n), res[0:1].rearrange("p q t b -> p (q t b)")).then_inc(r_sent, 16)
                for k in range(2):
                    g.wait_ge(sent[k], 16 * B * (C // OC // 2))
                g.wait_ge(r_sent, 16 * (C // OC))


def norm_coefficients(nc, sems, name, st, parts, share, gb, out):
    n = st.shape[1]
    with Stage(nc, sems, name) as s:
        ag = s.sb("ag", [parts, 2])
        dev = s.sb("dev", [parts, 1])
        cs = s.sb("cs", [parts, 3])
        ps = s.ps("ps", [P, 512])
        steps, sums, rooted = s.sem("steps"), s.sem("sums"), s.sem("rooted")
        with s.block() as block:
            @block.vector
            def _(v):
                ch = Chain(v, steps)
                ch.done(v.bn_aggr(ag[:], st[0:parts].rearrange("p n s -> p (n s)")))
                v.wait_ge(sums, 1)
                ch.done(v.tensor_copy(cs[:, 0:1], ps[0:parts, 0:1]))
                ch.sync()
                ch.done(v.tensor_tensor(dev[:], ag[:, 0:1], cs[:, 0:1], ALU.subtract))
                ch.sync()
                ch.done(v.tensor_tensor(dev[:], dev[:], dev[:], ALU.mult))
                ch.sync()
                ch.done(v.tensor_tensor(dev[:], dev[:], ag[:, 1:2], ALU.add))
                v.wait_ge(sums, 2)
                ch.done(v.tensor_scalar(cs[:, 1:2], ps[0:parts, 1:2], EPS, None, ALU.add))
                v.wait_ge(rooted, 1)
                ch.done(v.reciprocal(cs[:, 1:2], cs[:, 1:2]))
                ch.sync()
                ch.done(v.tensor_tensor(out[:, 0:1], cs[:, 1:2], gb[:, 0:1], ALU.mult))
                ch.sync()
                ch.done(v.tensor_tensor(cs[:, 2:3], cs[:, 0:1], out[:, 0:1], ALU.mult))
                ch.sync()
                v.tensor_tensor(out[:, 1:2], gb[:, 1:2], cs[:, 2:3], ALU.subtract)

            @block.tensor
            def _(pe):
                pe.wait_ge(steps, 1)
                pe.matmul(ps[0:parts, 0:1], share, ag[:, 0:1], start=True, stop=True).then_inc(sums, 1)
                pe.wait_ge(steps, 5)
                pe.matmul(ps[0:parts, 1:2], share, dev[:], start=True, stop=True).then_inc(sums, 1)

            @block.scalar
            def _(a):
                a.wait_ge(steps, 6)
                a.activation(cs[:, 1:2], cs[:, 1:2], ACT.Sqrt).then_inc(rooted, 1)


RC = 16
NCH = H // RC


def load_taps(sp, X, k, src, j, got, pad=0):
    for d in range(3):
        lo, hi = j * RC + d - 1, j * RC + d - 1 + RC
        a, b = max(lo, 0), min(hi, H)
        sp.dma_start(X[32 * d:32 * d + 32, k, a - lo:b - lo, pad:pad + W], src[:, a:b, :]).then_inc(got, 16)


def graph_conv(nc, sems, x1, gstat, wt, wts, y1, st):
    with Stage(nc, sems, "gc") as s:
        X = s.sb("x", [97, 2, RC, W])
        Y = s.sb("y", [P, 2, 512])
        O = s.sb("o", [P, 2, 512])
        GS = s.sb("gs", [96, 2, B])
        cw = s.sb("cw", [97, C])
        A = s.sb("A", [P, P])
        ps_c = [s.ps(f"c{k}", [P, 512]) for k in range(2)]
        ps_a = [s.ps(f"a{k}", [P, 512]) for k in range(2)]
        c_in, g_in, passed = s.sem("c_in"), s.sem("g_in"), s.sem("passed")
        x_in = [s.sem(f"x_in{k}") for k in range(2)]
        set_, normed, edged, conv, y_done, prod, o_done, counted = (
            s.sem(n) for n in ("set", "normed", "edged", "conv", "y_done", "prod", "o_done", "counted"))
        sent = [s.sem(f"sent{k}") for k in range(2)]

        with s.block() as block:
            @block.sync
            def _(sp):
                sp.dma_start(cw[:], wts["l1_w"]).then_inc(c_in, 16)
                sp.dma_start(A[:], wts["l1_A"]).then_inc(c_in, 16)
                for d in range(3):
                    for e in range(2):
                        sp.dma_start(GS[32 * d + e:32 * d + 32:2].rearrange("p t b -> p (t b)"),
                                     gstat.rearrange("n a (q t) -> (n a q) t", q=2)).then_inc(g_in, 16)
                sp.wait_ge(set_, 1)
                with sp.Fori(0, B) as b:
                    for j in range(NCH):
                        k = j % 2
                        sp.wait_ge(conv, b * NCH + j + 1)
                        alone(sp, passed)
                        load_taps(sp, X, k, one(x1, b), j, x_in[k])

            @block.gpsimd
            def _(g):
                g.memset(X[:], 0.0).then_inc(set_, 1)
                g.wait_ge(set_, 1)
                g.memset(X[96:97], 1.0).then_inc(set_, 1)
                with g.Fori(0, B) as b:
                    for j in range(NCH):
                        g.wait_ge(o_done, b * NCH + j + 3)
                        alone(g, passed)
                        g.dma_start(one(y1, b)[:, j], O[:, j % 2]).then_inc(sent[j % 2], 16)
                for k in range(2):
                    g.wait_ge(sent[k], 16 * B * NCH // 2)

            @block.vector
            def _(v):
                v.wait_ge(g_in, 96)
                v.sem_inc(counted, 2)
                with v.Fori(0, B) as b:
                    for j in range(NCH + 1):
                        if j < NCH:
                            k = j % 2
                            v.wait_ge(x_in[k], 48 * (b * (NCH // 2) + j // 2 + 1))
                            xk = X[0:96, k].rearrange("p r w -> p (r w)")
                            v.tensor_scalar(xk, xk, GS[:, 0, bass.ds(b, 1)], GS[:, 1, bass.ds(b, 1)],
                                            ALU.subtract, ALU.mult).then_inc(normed, 1)
                            if j in (0, NCH - 1):
                                v.wait_ge(normed, b * NCH + j + 1)
                                edge = X[0:32, k, 0, :] if j == 0 else X[64:96, k, RC - 1, :]
                                v.memset(edge, 0.0).then_inc(edged, 1)
                        if j:
                            v.wait_ge(o_done, b * NCH + j + 2)
                            v.bn_stats(st[:, bass.ds(b * NCH + j - 1, 1), :].rearrange("p a s -> p (a s)"),
                                       O[:, (j - 1) % 2]).then_inc(counted, 1)

            @block.tensor
            def _(pe):
                pe.wait_ge(c_in, 32)
                pe.wait_ge(set_, 2)
                pe.sem_inc(conv, 2)
                pe.sem_inc(prod, 2)
                with pe.Fori(0, B) as b:
                    for j in range(NCH + 1):
                        n = b * NCH + j
                        if j < NCH:
                            k = j % 2
                            pe.wait_ge(normed, n + 1)
                            if j == 0:
                                pe.wait_ge(edged, 2 * b + 1)
                            if j == NCH - 1:
                                pe.wait_ge(edged, 2 * b + 2)
                            pe.wait_ge(y_done, n + 1)
                            for r in range(RC):
                                mm = pe.matmul(ps_c[k][:, 32 * r:32 * r + 32], X[:, k, r, :], cw[:], start=True, stop=True)
                            mm.then_inc(conv, 1)
                        if j:
                            k = (j - 1) % 2
                            pe.wait_ge(y_done, n + 2)
                            pe.wait_ge(o_done, n)
                            for q in range(4):
                                mm = pe.matmul(ps_a[k][:, 128 * q:128 * q + 128], Y[:, k, 128 * q:128 * q + 128], A[:],
                                               start=True, stop=True)
                            mm.then_inc(prod, 1)

            @block.scalar
            def _(a):
                a.sem_inc(y_done, 2)
                a.sem_inc(o_done, 2)
                with a.Fori(0, B) as b:
                    for j in range(NCH + 1):
                        n = b * NCH + j
                        if j < NCH:
                            a.wait_ge(conv, n + 3)
                            a.wait_ge(prod, n + 1)
                            a.activation(Y[:, j % 2], ps_c[j % 2][:], ACT.Relu).then_inc(y_done, 1)
                        if j:
                            k = (j - 1) % 2
                            a.wait_ge(prod, n + 2)
                            a.wait_ge(sent[k], 16 * (b * (NCH // 2) + (j - 1) // 2))
                            a.wait_ge(counted, n)
                            a.activation(O[:, k], ps_a[k][:], ACT.Copy).then_inc(o_done, 1)


def residual_norm(nc, sems, name, y, coef, x, x_out, pair, GS):
    N = PX // 4
    with Stage(nc, sems, name) as s:
        Y = s.sb("y", [P, 2, N])
        X = s.sb("x", [P, 2, N])
        st = s.sb("st", [P, 8, 6])
        ag = s.sb("ag", [P, 2])
        dev = s.sb("dev", [P, 1])
        pr = s.sb("pr", [P, P])
        ps = s.ps("ps", [P, 512])
        c_in, passed = s.sem("c_in"), s.sem("passed")
        got = [s.sem(f"in{k}") for k in range(2)]
        sent = [s.sem(f"sent{k}") for k in range(2)]
        act, steps, sums, rooted = s.sem("act"), s.sem("steps"), s.sem("sums"), s.sem("rooted")
        ST = 1 + 8 + 1 + 1 + 1 + 1 + 1 + 1 + 1
        with s.block() as block:
            @block.sync
            def _(sp):
                sp.dma_start(pr[:], pair).then_inc(c_in, 16)
                with sp.Fori(0, B // 2) as i:
                    for k in range(2):
                        sp.wait_ge(sent[k], 64 * i)
                        alone(sp, passed)
                        sp.wait_ge(steps, ST * (2 * i + k) + k)
                        alone(sp, passed)
                        sp.dma_start(Y[:, k], one(y, 2 * i + k)).then_inc(got[k], 16)
                        for q in range(4):
                            r = slice(32 * q, 32 * q + 32)
                            xv = X[r, k].rearrange("p (h w) -> p h w", w=W)
                            sp.dma_start(xv, one(x, 2 * i + k)[q]).then_inc(got[k], 16)

            @block.scalar
            def _(a):
                with a.Fori(0, B // 2) as i:
                    for k in range(2):
                        n = 2 * i + k
                        a.wait_ge(got[k], 80 * (i + 1))
                        a.activation(Y[:, k], Y[:, k], ACT.Relu, bias=coef[:, 1:2], scale=coef[:, 0:1]).then_inc(act, 1)
                        a.wait_ge(steps, ST * n + ST - 1 + 2)
                        alone(a, passed)
                        gv = GS[:, 1, bass.ds(n, 1)]
                        a.activation(gv, gv, ACT.Sqrt).then_inc(rooted, 1)

            @block.vector
            def _(v):
                v.sem_inc(steps, 2)
                with v.Fori(0, B // 2) as i:
                    ch = Chain(v, steps, i * (2 * ST) + 2)
                    for k in range(2):
                        n = 2 * i + k
                        v.wait_ge(act, n + 1)
                        ch.done(v.tensor_tensor(X[:, k], X[:, k], Y[:, k], ALU.add))
                        ch.sync()
                        for q in range(8):
                            ch.done(v.bn_stats(st[:, q], X[:, k, 512 * q:512 * q + 512]))
                        ch.sync()
                        alone(v, passed)
                        ch.done(v.bn_aggr(ag[:], st[:].rearrange("p q s -> p (q s)")))
                        v.wait_ge(sums, 2 * n + 1)
                        ch.done(v.tensor_copy(GS[:, 0, bass.ds(n, 1)], ps[:, 0:1]))
                        ch.sync()
                        ch.done(v.tensor_tensor(dev[:], ag[:, 0:1], GS[:, 0, bass.ds(n, 1)], ALU.subtract))
                        ch.sync()
                        ch.done(v.tensor_tensor(dev[:], dev[:], dev[:], ALU.mult))
                        ch.sync()
                        ch.done(v.tensor_tensor(dev[:], dev[:], ag[:, 1:2], ALU.add))
                        v.wait_ge(sums, 2 * n + 2)
                        ch.done(v.tensor_scalar(GS[:, 1, bass.ds(n, 1)], ps[:, 1:2], EPS, None, ALU.add))
                        v.wait_ge(rooted, n + 1)
                        alone(v, passed)
                        ch.done(v.reciprocal(GS[:, 1, bass.ds(n, 1)], GS[:, 1, bass.ds(n, 1)]))
                    assert ch.n == 2 * ST

            @block.tensor
            def _(pe):
                pe.wait_ge(c_in, 16)
                with pe.Fori(0, B) as n:
                    pe.wait_ge(steps, ST * n + 2 + 10)
                    pe.matmul(ps[:, 0:1], pr[:], ag[:, 0:1], start=True, stop=True).then_inc(sums, 1)
                    pe.wait_ge(steps, ST * n + 2 + 14)
                    pe.matmul(ps[:, 1:2], pr[:], dev[:], start=True, stop=True).then_inc(sums, 1)

            @block.gpsimd
            def _(g):
                with g.Fori(0, B // 2) as i:
                    for k in range(2):
                        g.wait_ge(steps, ST * (2 * i + k) + 3)
                        alone(g, passed)
                        for q in range(4):
                            r = slice(32 * q, 32 * q + 32)
                            xv = X[r, k].rearrange("p (h w) -> p h w", w=W)
                            g.dma_start(one(x_out, 2 * i + k)[q], xv).then_inc(sent[k], 16)
                for k in range(2):
                    g.wait_ge(sent[k], 64 * (B // 2))


def depth_conv(nc, sems, x2, GS, LF, fb, hs, xp, st):
    with Stage(nc, sems, "dc") as s:
        X = s.sb("x", [96, 2, RC, W + 2])
        O = s.sb("o", [96, 2, RC * W])
        N = PX // 4
        XI = s.sb("xi", [P, N])
        XH, XM, XL = (s.sb(n, [P, N], BF16) for n in ("xh", "xm", "xl"))
        img_in, img_n, cut, xp_out, xp_free = (s.sem(n) for n in ("img_in", "img_n", "cut", "xp_out", "xp_free"))
        ps = [s.ps(f"c{k}", [P, 512]) for k in range(4)]
        set_, passed = s.sem("set"), s.sem("passed")
        x_in = [s.sem(f"x_in{k}") for k in range(2)]
        sent = [s.sem(f"sent{k}") for k in range(2)]
        normed, edged, conv, o_done, counted = (s.sem(n) for n in ("normed", "edged", "conv", "o_done", "counted"))
        Q = RC // 4
        with s.block() as block:
            @block.sync
            def _(sp):
                sp.wait_ge(set_, 1)
                with sp.Fori(0, B) as b:
                    sp.wait_ge(xp_free, b + 1)
                    alone(sp, passed)
                    for q in range(4):
                        sp.dma_start(XI[32 * q:32 * q + 32], one(x2, b)[:, 32 * q:32 * q + 32, :]).then_inc(img_in, 16)
                    for j in range(NCH):
                        sp.wait_ge(conv, Q * (b * NCH + j + 1))
                        alone(sp, passed)
                        load_taps(sp, X, j % 2, one(x2, b), j, x_in[j % 2], pad=1)

            @block.gpsimd
            def _(g):
                g.memset(X[:], 0.0).then_inc(set_, 1)
                g.sem_inc(xp_free, 1)

                def store(b, t, x):
                    for q in range(4):
                        g.dma_start(one(xp, b)[32 * x:32 * x + 32, N * q:N * q + N], t[32 * q:32 * q + 32]).then_inc(xp_out, 16)

                with g.Fori(0, B) as b:
                    g.wait_ge(img_n, b + 1)
                    alone(g, passed)
                    g.tensor_copy(XH[:], XI[:]).then_inc(cut, 1)
                    g.wait_ge(cut, 4 * b + 1)
                    alone(g, passed)
                    g.tensor_tensor(XI[:], XI[:], XH[:], ALU.subtract).then_inc(cut, 1)
                    store(b, XH, 0)
                    store(b, XH, 3)
                    for j in range(NCH):
                        k = j % 2
                        if j == 2:
                            g.wait_ge(cut, 4 * b + 2)
                            alone(g, passed)
                            g.tensor_copy(XM[:], XI[:]).then_inc(cut, 1)
                        if j == 4:
                            g.wait_ge(cut, 4 * b + 3)
                            alone(g, passed)
                            g.tensor_tensor(XL[:], XI[:], XM[:], ALU.subtract).then_inc(cut, 1)
                            store(b, XM, 1)
                        if j == 6:
                            g.wait_ge(cut, 4 * b + 4)
                            alone(g, passed)
                            store(b, XL, 2)
                        g.wait_ge(o_done, Q * (b * NCH + j + 1) + 4)
                        alone(g, passed)
                        g.dma_start(one(hs, b)[:, j * RC * W:(j + 1) * RC * W], O[:, k]).then_inc(sent[k], 16)
                    g.wait_ge(xp_out, 256 * (b + 1))
                    alone(g, passed)
                    g.sem_inc(xp_free, 1)
                for k in range(2):
                    g.wait_ge(sent[k], 16 * B * NCH // 2)

            @block.vector
            def _(v):
                with v.Fori(0, B) as b:
                    v.wait_ge(img_in, 64 * (b + 1))
                    v.tensor_scalar(XI[:], XI[:], GS[:, 0, bass.ds(b, 1)], GS[:, 1, bass.ds(b, 1)],
                                    ALU.subtract, ALU.mult).then_inc(img_n, 1)
                    for j in range(NCH + 1):
                        if j < NCH:
                            k = j % 2
                            v.wait_ge(x_in[k], 48 * (b * (NCH // 2) + j // 2 + 1))
                            xk = X[0:96, k, :, 1:W + 1]
                            v.tensor_scalar(xk, xk, GS[0:96, 0, bass.ds(b, 1)], GS[0:96, 1, bass.ds(b, 1)],
                                            ALU.subtract, ALU.mult).then_inc(normed, 1)
                            if j in (0, NCH - 1):
                                v.wait_ge(normed, b * NCH + j + 1)
                                edge = X[0:32, k, 0, :] if j == 0 else X[64:96, k, RC - 1, :]
                                v.memset(edge, 0.0).then_inc(edged, 1)
                        if j:
                            for q in range(Q):
                                m = b * (NCH * Q) + (j - 1) * Q + q
                                v.wait_ge(o_done, m + 5)
                                v.bn_stats(st[:, bass.ds(m, 1), :].rearrange("p a s -> p (a s)"),
                                           O[0:64, (j - 1) % 2, 512 * q:512 * q + 512]).then_inc(counted, 1)

            @block.tensor
            def _(pe):
                pe.sem_inc(conv, 2 * Q)
                with pe.Fori(0, B) as b:
                    for j in range(NCH):
                        k = j % 2
                        n = b * NCH + j
                        pe.wait_ge(normed, n + 1)
                        if j == 0:
                            pe.wait_ge(edged, 2 * b + 1)
                        if j == NCH - 1:
                            pe.wait_ge(edged, 2 * b + 2)
                        for q in range(Q):
                            pe.wait_ge(o_done, Q * n + q + 1)
                            alone(pe, passed)
                            for d in range(3):
                                mm = pe.matmul(ps[q][0:96, :], LF[:, d, :], X[:, k, 4 * q:4 * q + 4, d:d + W],
                                               start=(d == 0), stop=(d == 2))
                            mm.then_inc(conv, 1)

            @block.scalar
            def _(a):
                a.sem_inc(o_done, 4)
                with a.Fori(0, B) as b:
                    for j in range(NCH):
                        k = j % 2
                        n = b * NCH + j
                        a.wait_ge(sent[k], 16 * (b * (NCH // 2) + j // 2))
                        if j >= 2:
                            a.wait_ge(counted, Q * (n - 1))
                        for q in range(Q):
                            a.wait_ge(conv, Q * n + q + 1 + 2 * Q)
                            a.activation(O[:, k, 512 * q:512 * q + 512], ps[q][0:96, :], ACT.Identity,
                                         bias=fb[:, 0:1]).then_inc(o_done, 1)


def last_conv(nc, sems, x3, GS, LW, out):
    R2 = RC // 2
    with Stage(nc, sems, "lc") as s:
        X = s.sb("x", [P, 2, R2, W + 2])
        R = s.sb("r", [64, 2, R2, W])
        shift = s.sb("shift", [P, B])
        negated = s.sem("negated")
        ps = [s.ps(f"c{k}", [P, 512]) for k in range(4)]
        set_, passed = s.sem("set"), s.sem("passed")
        x_in = [s.sem(f"x_in{k}") for k in range(2)]
        r_in = [s.sem(f"r_in{k}") for k in range(2)]
        sent = [s.sem(f"sent{k}") for k in range(2)]
        normed, edged, conv, added = (s.sem(n) for n in ("normed", "edged", "conv", "added"))
        Q = R2 // 4
        with s.block() as block:
            @block.sync
            def _(sp):
                sp.wait_ge(set_, 1)
                with sp.Fori(0, B) as b:
                    for j in range(NCH):
                        k = j % 2
                        sp.wait_ge(conv, Q * (b * NCH + j + 1))
                        alone(sp, passed)
                        sp.wait_ge(sent[k], 32 * (b * (NCH // 2) + j // 2))
                        alone(sp, passed)
                        img = one(x3, b)
                        for d in range(4):
                            r0 = j * RC + d - 1
                            a = 1 if r0 < 0 else 0
                            e = R2 - 1 if r0 + 2 * (R2 - 1) >= H else R2
                            sp.dma_start(X[32 * d:32 * d + 32, k, a:e, 1:W + 1],
                                         img[:, r0 + 2 * a:r0 + 2 * (e - 1) + 1:2, :]).then_inc(x_in[k], 16)
                        for p in range(2):
                            sp.dma_start(R[32 * p:32 * p + 32, k], img[:, j * RC + p:(j + 1) * RC:2, :]).then_inc(r_in[k], 16)

            @block.gpsimd
            def _(g):
                g.memset(X[:], 0.0).then_inc(set_, 1)
                with g.Fori(0, B) as b:
                    for j in range(NCH):
                        k = j % 2
                        g.wait_ge(added, Q * (b * NCH + j + 1) + 4)
                        alone(g, passed)
                        for p in range(2):
                            g.dma_start(one(out, b)[:, j * RC + p:(j + 1) * RC:2, :], R[32 * p:32 * p + 32, k]).then_inc(sent[k], 16)
                for k in range(2):
                    g.wait_ge(sent[k], 32 * B * NCH // 2)

            @block.scalar
            def _(a):
                with a.Fori(0, B) as b:
                    for j in range(NCH):
                        k = j % 2
                        a.wait_ge(negated, 1)
                        a.wait_ge(x_in[k], 64 * (b * (NCH // 2) + j // 2 + 1))
                        alone(a, passed)
                        xk = X[:, k, :, 1:W + 1]
                        a.activation(xk, xk, ACT.Identity, bias=shift[:, bass.ds(b, 1)],
                                     scale=GS[:, 1, bass.ds(b, 1)]).then_inc(normed, 1)

            @block.vector
            def _(v):
                v.sem_inc(added, 4)
                v.scalar_tensor_tensor(out=shift[:], in0=GS[:, 0, :], scalar=-1.0, in1=GS[:, 1, :],
                                       op0=ALU.mult, op1=ALU.mult).then_inc(negated, 1)
                with v.Fori(0, B) as b:
                    for j in range(NCH + 1):
                        if j in (0, NCH - 1):
                            v.wait_ge(normed, b * NCH + j + 1)
                            edge = X[0:32, j % 2, 0, :] if j == 0 else X[96:128, j % 2, R2 - 1, :]
                            v.memset(edge, 0.0).then_inc(edged, 1)
                        if j:
                            k = (j - 1) % 2
                            n = b * NCH + j - 1
                            v.wait_ge(r_in[k], 32 * (b * (NCH // 2) + (j - 1) // 2 + 1))
                            for q in range(Q):
                                v.wait_ge(conv, Q * n + q + 1 + 2 * Q)
                                rq = R[:, k, 4 * q:4 * q + 4, :].rearrange("p r w -> p (r w)")
                                v.tensor_tensor(rq, ps[2 * k + q][0:64, :], rq, ALU.add).then_inc(added, 1)

            @block.tensor
            def _(pe):
                pe.sem_inc(conv, 2 * Q)
                with pe.Fori(0, B) as b:
                    for j in range(NCH):
                        k = j % 2
                        n = b * NCH + j
                        pe.wait_ge(normed, n + 1)
                        if j == 0:
                            pe.wait_ge(edged, 2 * b + 1)
                        if j == NCH - 1:
                            pe.wait_ge(edged, 2 * b + 2)
                        for q in range(Q):
                            pe.wait_ge(added, Q * n + q + 1)
                            alone(pe, passed)
                            for d in range(3):
                                mm = pe.matmul(ps[2 * k + q][0:64, :], LW[:, d, :], X[:, k, 4 * q:4 * q + 4, d:d + W],
                                               start=(d == 0), stop=(d == 2))
                            mm.then_inc(conv, 1)


def load_weights(nc, sems, d, wt):
    with Stage(nc, sems, "wt") as s:
        dsc = s.sb("dsc", [C, 2, K9, 4 * C])
        fus = s.sb("fus", [C, 3, C])
        cw = s.sb("cw", [C, 3, 96])
        cb = s.sb("cb", [C, 1])
        fz = s.sb("fz", [C, 96])
        dwv = s.sb("dwv", [96, 2, 3])
        idm = s.sb("idm", [96, C])
        b96 = s.sb("b96", [96, 1])
        fT = s.sb("fT", [12, C, P])
        cm = s.sb("cm", [12, 9])
        sel = s.sb("sel", [97, 2 * K9, P])
        ps = [s.ps(f"p{k}", [P, 512]) for k in range(5)]
        zf, zr = s.sb("zf", [P, 32 * K9]), s.sb("zr", [P, 32 * K9])
        zp = s.sb("zp", [P, 3, 32 * K9], BF16)
        grid = s.sb("grid", [P, NCH, 512])
        c_in, made, zeroed, cut = s.sem("c_in"), s.sem("made"), s.sem("zeroed"), s.sem("cut")
        loads = [(dsc[:].rearrange("m a k c -> m (a k c)"), d["dsc"]), (fus[:].rearrange("m g o -> m (g o)"), d["fusT"]),
                 (cw[:].rearrange("m x c -> m (x c)"), d["convw"]), (cb[:], d["conv_b"]), (fz[:, 64:96], d["fusT"][:, 0:C]),
                 (dwv[:].rearrange("p a x -> p (a x)"), d["dw"]), (idm[:], d["idm"]), (b96[:], d["b96"]),
                 (fT[:].rearrange("f o i -> f (o i)"), d["freqT"]), (cm[:], d["freq_to_taps"]),
                 (sel[:].rearrange("r k p -> r (k p)"), d["select"]),
                 (grid[:].rearrange("p j n -> p (j n)"), d["grid"]), (wt["pw"][:], d["pw"]), (wt["pb"][:], d["pb"]),
                 (wt["share"][:], d["share"]), (wt["gb1"][:], d["gb1"]), (wt["gbo"][:], d["gbo"]), (wt["gbf"][:], d["gbf"]),
                 (wt["eye"][:], d["eye"])]
        with s.block() as block:
            @block.sync
            def _(sp):
                for dst, src in loads:
                    sp.dma_start(dst, src).then_inc(c_in, 16)

            @block.gpsimd
            def _(g):
                g.memset(fz[:, 0:64], 0.0).then_inc(zeroed, 1)
                g.memset(wt["L3"][:], 0.0).then_inc(zeroed, 1)

            @block.tensor
            def _(pe):
                pe.wait_ge(c_in, 16 * len(loads))
                pe.wait_ge(zeroed, 2)
                for a in range(2):
                    for k in range(K9):
                        mm = pe.matmul(ps[a][:, 32 * k:32 * k + 32], dsc[:, a, k, :], fus[:, 2 - a, :], start=True, stop=True)
                for x in range(3):
                    mm = pe.matmul(ps[2][0:96, 32 * x:32 * x + 32], cw[:, x, :], fus[:, 0, :], start=True, stop=True)
                pe.matmul(ps[3][0:96, 0:1], fz[:], cb[:], start=True, stop=True)
                for o in range(C):
                    mm = pe.matmul(ps[4][:, 9 * o:9 * o + 9], fT[:, o, :], cm[:], start=True, stop=True)
                mm.then_inc(made, 1)

            @block.vector
            def _(v):
                v.wait_ge(made, 1)
                ch = Chain(v, cut)
                for a in range(2):
                    n = 32 * K9
                    ch.done(v.tensor_scalar(zf[:], ps[a][:, 0:n], -1.0, None, ALU.mult))
                    ch.sync()
                    ch.done(v.tensor_copy(zp[:, 0], zf[:]))
                    ch.sync()
                    ch.done(v.tensor_tensor(zr[:], zf[:], zp[:, 0], ALU.subtract))
                    ch.sync()
                    ch.done(v.tensor_copy(zp[:, 1], zr[:]))
                    ch.sync()
                    ch.done(v.tensor_tensor(zp[:, 2], zr[:], zp[:, 1], ALU.subtract))
                    ch.sync()
                    for x, part in enumerate((0, 0, 0, 1)):
                        r = slice(32 * x, 32 * x + 32)
                        ch.done(v.tensor_copy(wt["Z"][r, a, 0], zp[r, part]))
                    for x, part in enumerate((2, 1, 1)):
                        r = slice(32 * x, 32 * x + 32)
                        ch.done(v.tensor_copy(wt["Z"][r, a, 1], zp[r, part]))
                    ch.done(v.memset(wt["Z"][96:128, a, 1], 0.0))
                    ch.sync()
                v.tensor_copy(wt["L2"][:, :, 64:96], ps[2][0:96, 0:96].rearrange("p (x o) -> p x o", x=3))
                for x in range(3):
                    for a in range(2):
                        v.tensor_scalar(wt["L2"][:, x, 32 * a:32 * a + 32], idm[:], dwv[:, a, x:x + 1], None, ALU.mult)
                v.tensor_tensor(wt["b2"][:], ps[3][0:96, 0:1], b96[:], ALU.add)
                for q in range(4):
                    for t in range(2):
                        if 0 <= q - t <= 2:
                            dy = q - t
                            src = ps[4][32 * q:32 * q + 32, 0:288].rearrange("i (o y x) -> i y x o", y=3, x=3)[:, dy]
                            v.tensor_copy(wt["L3"][32 * q:32 * q + 32, :, 32 * t:32 * t + 32], src)

            @block.scalar
            def _(a):
                a.wait_ge(c_in, 16 * len(loads))
                a.activation(wt["sel"][:], sel[:], ACT.Copy)
                a.activation(wt["grid"][:], grid[:], ACT.Copy)


LINES = 32
PAIRS = [(0, 1), (2, 3), (4, 5), (6, 7), (8,)]


def deformable(nc, sems, hs, xp, coef, wt, uy, u, st):
    with Stage(nc, sems, "df") as s:
        XP = s.sb("xp", [P, PX], BF16)
        IX = s.sb("ix", [97, PX], BF16)
        HI = s.sb("hi", [64, 2, RC * W])
        t_ix, t_r, t_r2 = (s.sb(n, [P, 512]) for n in ("t_ix", "t_r", "t_r2"))
        parts = s.sb("parts", [P, 2, 3, 512], BF16)
        Zs = s.sb("zs", [P, 2, 4, 32 * K9])
        L = len(PAIRS)
        T = s.sb("t", [P, L, 1024])
        YB = s.sb("yb", [P, C * W])
        U = s.sb("u", [P, LINES, W])
        XO = s.sb("xo", [P, 2, P])
        ps_d = [s.ps(f"d{k}", [P, 1024]) for k in range(2)]
        ps_z = s.ps("z", [P, 512])
        ps_f = s.ps("f", [P, 512])
        ps_o = [s.ps(f"o{k}", [P, 512]) for k in range(2)]
        passed, ones = s.sem("passed"), s.sem("ones")
        h_in, p_out = ([s.sem(f"{n}{k}") for k in range(2)] for n in ("h_in", "p_out"))
        relu, off_full, split, xp_in = s.sem("relu"), s.sem("off_full"), s.sem("split"), s.sem("xp_in")
        z_full, z_read = s.sem("z_full"), s.sem("z_read")
        d_full, d_read = s.sem("d_full"), s.sem("d_read")
        hat, t_used = s.sem("hat"), s.sem("t_used")
        o_read = s.sem("o_read")
        turned, y_read = s.sem("turned"), s.sem("y_read")
        u_in, uy_out, uy_in, u_out = (s.sem(n) for n in ("u_in", "uy_out", "uy_in", "u_out"))
        summed, counted = s.sem("summed"), s.sem("counted")
        S = 2 * LINES
        SC = LINES // NCH
        CHN = 6

        with s.block() as block:
            @block.sync
            def _(sp):
                def load(b, c):
                    sp.wait_ge(off_full, b * NCH + c + 1)
                    alone(sp, passed)
                    sp.dma_start(HI[:, c % 2], one(hs, b)[0:64, c * RC * W:(c + 1) * RC * W]).then_inc(h_in[c % 2], 16)

                def place(b, c, over):
                    k = c % 2
                    if over:
                        sp.wait_ge(d_full, ((b - 1) * S + LINES + SC * (c + 1)) * L)
                        alone(sp, passed)
                    sp.wait_ge(split, CHN * (b * NCH + c + 2))
                    alone(sp, passed)
                    for part in range(3):
                        for q in range(4):
                            px = c * RC * W + 512 * q
                            sp.dma_start(IX[32 * part:32 * part + 32, px:px + 512],
                                         parts[32 * q:32 * q + 32, k, part, :]).then_inc(p_out[k], 16)

                def image(b, over):
                    for c in range(NCH):
                        load(b, c)
                        if c >= 2:
                            place(b, c - 2, over)
                    for c in (NCH - 2, NCH - 1):
                        place(b, c, over)

                sp.wait_ge(ones, 1)
                with sp.Fori(0, 1) as b:
                    image(b, False)
                with sp.Fori(1, B) as b:
                    image(b, True)

            @block.gpsimd
            def _(g):
                def take(b, c):
                    g.dma_start(XP[:, c * RC * W:(c + 1) * RC * W], one(xp, b)[:, c * RC * W:(c + 1) * RC * W]).then_inc(xp_in, 16)

                def finish(b, c):
                    r = slice(SC * c * W, SC * (c + 1) * W)
                    g.wait_ge(o_read, b * S + LINES + SC * (c + 1) + 2)
                    alone(g, passed)
                    g.tensor_tensor(U[:].rearrange("p j w -> p (j w)")[:, r], U[:].rearrange("p j w -> p (j w)")[:, r],
                                    YB[:, r], ALU.add).then_inc(summed, 1)
                    g.wait_ge(summed, b * NCH + c + 1)
                    alone(g, passed)
                    g.dma_start(one(u, b).rearrange("q o j w -> (q o) (j w)")[:, r],
                                U[:].rearrange("p j w -> p (j w)")[:, r]).then_inc(u_out, 16)

                def image(b, more):
                    for q in range(4):
                        r = slice(32 * q, 32 * q + 32)
                        g.dma_start(U[r], one(hs, b)[64:96].rearrange("o (j q w) -> q o j w", q=4, w=W)[q]).then_inc(u_in, 16)
                    g.wait_ge(y_read, (b + 1) * LINES + 2)
                    alone(g, passed)
                    for q in range(4):
                        g.dma_start(one(uy, b).rearrange("o h w -> h o w")[:, 8 * q:8 * q + 8], YB[:, 8 * W * q:8 * W * (q + 1)].rearrange("p (o w) -> p o w", w=W)).then_inc(uy_out, 16)
                    g.wait_ge(uy_out, b * 64 + 64)
                    alone(g, passed)
                    for q in range(4):
                        r = slice(32 * q, 32 * q + 32)
                        g.dma_start(YB[r].rearrange("o (j w) -> o j w", w=W), one(uy, b).rearrange("o (j q) w -> q o j w", q=4)[q]).then_inc(uy_in, 16)
                    for c in range(NCH):
                        if more:
                            g.wait_ge(z_full, 4 * (b * S + LINES + SC * (c + 1)))
                            alone(g, passed)
                            take(b + 1, c)
                        if c == 0:
                            g.wait_ge(uy_in, 64 * (b + 1))
                            alone(g, passed)
                        else:
                            finish(b, c - 1)
                    finish(b, NCH - 1)
                    g.wait_ge(u_out, 16 * NCH * (b + 1))
                    alone(g, passed)
                    g.wait_ge(counted, NCH * (b + 1))
                    alone(g, passed)

                g.memset(IX[96:97], 1.0).then_inc(ones, 1)
                for c in range(NCH):
                    g.dma_start(XP[:, c * RC * W:(c + 1) * RC * W], xp[0][:, c * RC * W:(c + 1) * RC * W]).then_inc(xp_in, 16)
                with g.Fori(0, B - 1) as b:
                    image(b, True)
                with g.Fori(B - 1, B) as b:
                    image(b, False)

            @block.scalar
            def _(act):
                act.sem_inc(d_read, 2)

                def branch(b, c):
                    k = c % 2
                    act.wait_ge(h_in[k], 16 * (b * (NCH // 2) + c // 2 + 1))
                    act.activation(HI[:, k], HI[:, k], ACT.Relu, bias=coef[0:64, 1:2], scale=coef[0:64, 0:1]).then_inc(relu, 1)

                def distances(n, k):
                    for e, pts in enumerate(PAIRS):
                        w = 512 * len(pts)
                        act.wait_ge(d_full, n * L + e + 1)
                        act.wait_ge(t_used, n * L + e + 1)
                        act.activation(T[:, e, 0:w], ps_d[(k * L + e) % 2][:, 0:w], ACT.Abs).then_inc(d_read, 1)

                def image(b, more):
                    with act.Fori(0, LINES // 2) as i:
                        for k in range(2):
                            distances(b * S + 2 * i + k, k)
                    if more:
                        branch(b + 1, 0)
                    for c in range(NCH):
                        for t in range(SC):
                            distances(b * S + LINES + SC * c + t, t % 2)
                            if t == 2 and more and c + 1 < NCH:
                                branch(b + 1, c + 1)

                for c in range(NCH):
                    branch(0, c)
                with act.Fori(0, B - 1) as b:
                    image(b, True)
                with act.Fori(B - 1, B) as b:
                    image(b, False)

            @block.vector
            def _(v):
                v.sem_inc(z_read, 1)
                v.sem_inc(o_read, 2)
                v.sem_inc(y_read, 2)
                v.sem_inc(split, CHN)

                def offsets(b, c):
                    k = c % 2
                    g = b * NCH + c
                    ch = Chain(v, split, CHN * (g + 1))
                    v.wait_ge(off_full, g + 3)
                    ch.done(v.scalar_tensor_tensor(out=t_ix[:], in0=ps_f[:], scalar=wt["pb"][:, 0:1],
                                                   in1=wt["grid"][:, c, :], op0=ALU.add, op1=ALU.add))
                    yield
                    ch.sync()
                    if not (isinstance(b, int) and c < 2):
                        v.wait_ge(p_out[k], 192 * (b * (NCH // 2) + c // 2))
                    ch.done(v.tensor_copy(parts[:, k, 0], t_ix[:]))
                    yield
                    ch.sync()
                    ch.done(v.tensor_tensor(t_r[:], t_ix[:], parts[:, k, 0], ALU.subtract))
                    yield
                    ch.sync()
                    ch.done(v.tensor_copy(parts[:, k, 1], t_r[:]))
                    yield
                    ch.sync()
                    ch.done(v.tensor_tensor(t_r2[:], t_r[:], parts[:, k, 1], ALU.subtract))
                    yield
                    ch.sync()
                    ch.done(v.tensor_copy(parts[:, k, 2], t_r2[:]))
                    yield

                def read_z(n, k, q):
                    v.wait_ge(z_full, 4 * n + q + 1)
                    if q == 0:
                        v.wait_ge(t_used, L * n + 1)
                    v.tensor_copy(Zs[:, k, q], ps_z[:, 0:32 * K9]).then_inc(z_read, 1)

                def read_o(a, n, j, k):
                    v.wait_ge(t_used, L * n + 2 * L)
                    if a == 0:
                        v.tensor_copy(XO[:, k], ps_o[k][:, 0:P]).then_inc(o_read, 1)
                    else:
                        uj = U[:, bass.ds(j, 1), :].rearrange("p j w -> p (j w)")
                        v.tensor_tensor(uj, ps_o[k][:, 0:P], uj, ALU.add).then_inc(o_read, 1)

                def keep_columns(b, j, k):
                    v.wait_ge(turned, b * LINES + j + 1)
                    v.tensor_copy(YB[:].rearrange("h (o q w) -> h q o w", q=4, w=LINES)[:, :, :, bass.ds(j, 1)].rearrange("h q o w -> h q (o w)"),
                                  ps_o[k][:, P:2 * P].rearrange("h (q o) -> h q o", q=4)).then_inc(y_read, 1)

                def step(b, a, j, k, first=False, last=False, side=None):
                    n = b * S + a * LINES + j
                    pa, pj = (0, LINES - 1) if a == 1 and first else (a, j - 1)
                    behind = not (a == 0 and first)
                    for e, pts in enumerate(PAIRS):
                        w = 512 * len(pts)
                        v.wait_ge(d_read, n * L + e + 3)
                        v.tensor_scalar(T[:, e, 0:w], T[:, e, 0:w], 1.0, 1.0, ALU.min, ALU.subtract).then_inc(hat, 1)
                        if e == 0 and behind:
                            read_o(pa, n - 1, pj, 1 - k)
                        if e >= 1 and not (a == 1 and last):
                            read_z(n + 1, 1 - k, e - 1)
                        if e == 3 and behind and pa == 0:
                            keep_columns(b, pj, 1 - k)
                        if e in (2, 4) and side:
                            next(side, None)

                def stats(b, c):
                    v.wait_ge(summed, b * NCH + c + 1)
                    v.bn_stats(st[:, bass.ds(b * NCH + c, 1), :].rearrange("p a s -> p (a s)"),
                               U[:, SC * c:SC * (c + 1), :].rearrange("p j w -> p (j w)")).then_inc(counted, 1)

                def image(b, more):
                    for q in range(4):
                        read_z(b * S, 0, q)
                    step(b, 0, 0, 0, first=True)
                    step(b, 0, 1, 1)
                    with v.Fori(1, LINES // 2 - 1) as i:
                        for k in range(2):
                            step(b, 0, 2 * i + k, k)
                    step(b, 0, LINES - 2, 0)
                    step(b, 0, LINES - 1, 1, last=True)
                    v.wait_ge(u_in, 64 * (b + 1))
                    for c in range(NCH):
                        side = offsets(b + 1, c) if more else None
                        for t in range(SC):
                            j = SC * c + t
                            step(b, 1, j, t % 2, first=(j == 0), last=(j == LINES - 1), side=side if t else None)
                        if c:
                            stats(b, c - 1)
                    read_o(1, b * S + S - 1, LINES - 1, 1)
                    stats(b, NCH - 1)

                for c in range(NCH):
                    for _ in offsets(0, c):
                        pass
                with v.Fori(0, B - 1) as b:
                    image(b, True)
                with v.Fori(B - 1, B) as b:
                    image(b, False)

            @block.tensor
            def _(pe):
                pe.sem_inc(off_full, 2)
                pe.sem_inc(t_used, L)
                pe.wait_ge(ones, 1)

                def branch(b, c):
                    g = b * NCH + c
                    pe.wait_ge(relu, g + 1)
                    pe.wait_ge(split, CHN * g + 1)
                    alone(pe, passed)
                    for q in range(4):
                        mm = pe.matmul(ps_f[32 * q:32 * q + 32, :], wt["pw"][:], HI[:, c % 2, 512 * q:512 * q + 512],
                                       start=True, stop=True)
                    mm.then_inc(off_full, 1)

                def spread(a, n, j, k, e):
                    pe.wait_ge(d_read, n * L + e + 1)
                    if a == 0:
                        ix = IX[:].rearrange("r (h q w) -> r q h w", q=4, w=LINES)[:, :, :, bass.ds(j, 1)].rearrange("r q h w -> r q (h w)")
                    else:
                        ix = IX[:, bass.ds(j * (4 * W), 4 * W)]
                    for x, pt in enumerate(PAIRS[e]):
                        mm = pe.matmul(ps_d[(k * L + e) % 2][:, 512 * x:512 * x + 512], wt["sel"][:, K9 * a + pt, :], ix,
                                       start=True, stop=True)
                    mm.then_inc(d_full, 1)

                def make_z(a, n, j, q):
                    pe.wait_ge(z_read, 4 * n + q + 1)
                    alone(pe, passed)
                    if a == 0:
                        line = XP[:].rearrange("c (h w) -> c h w", w=W)[:, :, bass.ds(j + LINES * q, 1)].rearrange("c h w -> c (h w)")
                    else:
                        line = XP[:, bass.ds((j * 4 + q) * W, W)]
                    for x in range(2):
                        mm = pe.matmul(ps_z[:, 0:32 * K9], line, wt["Z"][:, a, x, :], start=(x == 0), stop=(x == 1))
                    mm.then_inc(z_full, 1)

                def apply(a, b, n, j, k, e, first):
                    pe.wait_ge(hat, n * L + e + 1)
                    if e == 0:
                        pe.wait_ge(z_read, 4 * n + 5)
                        pe.wait_ge(o_read, n + 1)
                        if a == 0:
                            pe.wait_ge(y_read, b * LINES + j + 1)
                        elif first:
                            pe.wait_ge(y_read, (b + 1) * LINES + j + 1)
                    for x, pt in enumerate(PAIRS[e]):
                        for q in range(4):
                            c = 512 * x + 128 * q
                            mm = pe.matmul(ps_o[k][32 * q:32 * q + 32, 0:P], Zs[:, k, q, 32 * pt:32 * pt + 32], T[:, e, c:c + 128],
                                           start=(pt == 0), stop=(pt == K9 - 1))
                    mm.then_inc(t_used, 1)

                def turn(n, k):
                    pe.wait_ge(o_read, n + 3)
                    alone(pe, passed)
                    pe.transpose(ps_o[k][:, P:2 * P], XO[:, k], wt["eye"][:]).then_inc(turned, 1)

                def step(b, a, j, k, first=False, last=False, head=False):
                    n = b * S + a * LINES + j
                    nxt = (a, j + 1) if not last else (1, 0) if a == 0 else None
                    for e in range(L):
                        if e + 2 < L:
                            spread(a, n, j, k, e + 2)
                        elif nxt:
                            spread(nxt[0], n + 1, nxt[1], 1 - k, e + 2 - L)
                        apply(a, b, n, j, k, e, head)
                        if e < 4 and nxt:
                            make_z(nxt[0], n + 1, nxt[1], e)
                        if e == 1 and (first if a else not first):
                            turn(n - 1, 1 - k)

                def image(b, more):
                    pe.wait_ge(xp_in, 16 * NCH * (b + 1))
                    alone(pe, passed)
                    for q in range(4):
                        make_z(0, b * S, 0, q)
                    for k in range(2):
                        pe.wait_ge(p_out[k], 192 * (NCH // 2) * (b + 1))
                    alone(pe, passed)
                    for e in range(2):
                        spread(0, b * S, 0, 0, e)
                    step(b, 0, 0, 0, first=True)
                    step(b, 0, 1, 1)
                    with pe.Fori(1, LINES // 2 - 1) as i:
                        for k in range(2):
                            step(b, 0, 2 * i + k, k)
                    step(b, 0, LINES - 2, 0)
                    step(b, 0, LINES - 1, 1, last=True)
                    for c in range(NCH):
                        for t in range(SC):
                            j = SC * c + t
                            step(b, 1, j, t % 2, first=(j == 0), last=(j == LINES - 1), head=(j < 2))
                            if t == 0 and more:
                                branch(b + 1, c)

                for c in range(NCH):
                    branch(0, c)
                with pe.Fori(0, B - 1) as b:
                    image(b, True)
                with pe.Fori(B - 1, B) as b:
                    image(b, False)


def dft_constants():
    two_pi = 2 * np.pi
    kx = np.concatenate([np.arange(M1), np.arange(H - M1, H)])
    h = np.arange(H)
    ang = two_pi * ((h[:, None] * kx[None]) % H) / H
    dft_h = np.stack([-np.sin(ang), np.cos(ang), np.sin(ang)], 2).reshape(H, -1)
    aw = two_pi * ((np.arange(W)[:, None] * np.arange(M2)[None]) % W) / W
    dft_wp = np.concatenate([np.cos(aw), -np.sin(aw)], 1)
    dft_wq = np.concatenate([np.sin(aw), np.cos(aw)], 1)
    kp = np.array([2 * j + par + hl * (H - M1) for hl in range(2) for par in range(2) for j in range(M1 // 2)])
    ah = two_pi * ((kp[:, None] * h[None]) % H) / H
    inv_hr = np.concatenate([np.cos(ah), -np.sin(ah)], 0)
    inv_hi = np.concatenate([np.sin(ah), np.cos(ah)], 0)
    cy = np.where(np.arange(M2) == 0, 1.0, 2.0)[:, None] / (H * W)
    inv_w = np.tile(np.concatenate([cy * np.cos(aw.T), -cy * np.sin(aw.T)], 0), (2, 1))
    return dict(
        dft_h=dft_h, dft_wp=dft_wp, dft_wq=dft_wq, inv_hr=inv_hr, inv_hi=inv_hi, inv_w=inv_w,
        avg=np.full((P, P), 1.0 / P))


def weight_layouts(inp):
    f = lambda a: np.ascontiguousarray(a, np.float32)
    c = lambda n: np.asarray(inp["L2_conv_" + n])
    fus = c("fus_w")[:, :, 0, 0]
    out = {}
    out["fusT"] = f(fus.reshape(C, 3, C).transpose(2, 1, 0)).reshape(C, 3 * C)
    dsc = np.stack([c("dscy_w"), c("dscx_w")]).transpose(1, 0, 3, 2)
    out["dsc"] = f(np.tile(dsc, (1, 1, 1, 4))).reshape(C, -1)
    out["convw"] = f(c("conv_w").transpose(0, 3, 2, 1)).reshape(C, -1)
    out["conv_b"] = f(c("conv_b").reshape(C, 1))
    dw = np.stack([c("offx_dw_w")[:, 0], c("offy_dw_w")[:, 0]])
    out["dw"] = f(dw.transpose(2, 1, 0, 3)).reshape(96, 6)
    out["b96"] = f(np.concatenate([c("offx_dw_b"), c("offy_dw_b"), np.zeros(C)])[:, None])
    pw = np.zeros((64, 32))
    pw[0:32, 0:K9] = c("offx_pw_w")[:, :, 0, 0].T
    pw[32:64, K9:2 * K9] = c("offy_pw_w")[:, :, 0, 0].T
    out["pw"] = f(pw)
    pb = np.zeros(32)
    pb[0:K9], pb[K9:2 * K9] = c("offx_pw_b"), c("offy_pw_b")
    out["pb"] = f(np.tile(pb, 4)[:, None])
    out["gbo"] = f(np.stack([np.concatenate([c("offx_bn_g"), c("offy_bn_g")]),
                             np.concatenate([c("offx_bn_b"), c("offy_bn_b")])], 1))
    out["gbf"] = f(np.tile(np.stack([c("fus_bn_g"), c("fus_bn_b")], 1), (4, 1)))
    out["gb1"] = f(np.tile(np.stack([inp["L1_conv_gamma"], inp["L1_conv_beta"]], 1), (4, 1)))
    w1 = np.asarray(inp["L1_conv_conv_w"])[:, :, :, 0]
    out["l1_w"] = f(np.concatenate([w1.transpose(2, 1, 0).reshape(96, C), np.asarray(inp["L1_conv_conv_b"])[None]], 0))
    fr = np.asarray(inp["L3_conv_freq_weight"]).reshape(C, C, 12)
    out["freqT"] = f(np.tile(fr.transpose(2, 0, 1), (1, 1, 4))).reshape(12, -1)
    return out


def shape_constants():
    out = dft_constants()
    p = np.arange(P)
    out["share"] = (p[:, None] % 32 == p[None] % 32) / 4.0
    out["pair"] = ((p[:, None] % 32) // 2 == (p[None] % 32) // 2) / 8.0
    out["eye"] = np.eye(P)
    out["idm"] = (np.arange(96)[:, None] % 32 == np.arange(32)[None]) * 1.0
    sel = np.zeros((97, 2 * K9, P))
    for a in range(2):
        for k in range(K9):
            for part in range(3):
                sel[32 * part + (K9 if a == 0 else 0) + k, K9 * a + k] = 1.0
    sel[96] = -np.arange(P)
    out["select"] = sel.reshape(97, -1)
    grid = np.zeros((4, 32, NCH, 4, W))
    grid[:, 0:K9] = np.arange(W)
    rows = RC * np.arange(NCH)[None, :, None] + 4 * np.arange(4)[:, None, None] + np.arange(4)[None, None, :]
    grid[:, K9:2 * K9] = rows[:, None, :, :, None]
    out["grid"] = grid.reshape(P, -1)
    out["freq_to_taps"] = freq_to_taps()
    return {k: np.ascontiguousarray(v, np.float32) for k, v in out.items()}


def freq_to_taps():
    K = 3
    basis = np.zeros((12, K, 2), complex)
    for f in range(12):
        basis[f, f // 4, (f // 2) % 2] = 1.0 if f % 2 == 0 else 1j
    kern = np.fft.irfft2(basis, s=(K, K), axes=(-2, -1)).astype(np.float32)
    th = np.array([i * np.pi / 4 for i in range(8)], np.float32)[:, None]
    sc = np.array([1.0, 1.25, 1.25 ** 2, 1.25 ** 3], np.float32)[None]
    cos_t, sin_t = (np.cos(th) * sc).reshape(-1), (np.sin(th) * sc).reshape(-1)
    co = ((2 * np.arange(K, dtype=np.float32) + 1) / np.float32(K) - 1).astype(np.float32)
    gy, gx = np.meshgrid(co, co, indexing="ij")
    out = np.zeros((12, K, K))
    for c, s in zip(cos_t, sin_t):
        ix = (((c * gx - s * gy) + 1) * K - 1) * np.float32(0.5)
        iy = (((s * gx + c * gy) + 1) * K - 1) * np.float32(0.5)
        x0, y0 = np.floor(ix).astype(int), np.floor(iy).astype(int)
        wx1, wy1 = ix - x0, iy - y0
        for yy, wy in ((y0, 1 - wy1), (y0 + 1, wy1)):
            for xx, wx in ((x0, 1 - wx1), (x0 + 1, wx1)):
                ok = (xx >= 0) & (xx < K) & (yy >= 0) & (yy < K)
                out += np.where(ok, kern[:, np.clip(yy, 0, K - 1), np.clip(xx, 0, K - 1)], 0) * (wy * wx)
    return (out / len(cos_t)).reshape(12, 9)


def network(nc, x, w, d, out):
    dram = lambda name, shape: nc.dram_tensor(name, shape, F32).ap()
    spec = dram("spec", (M1 // 2, P, 2 * M2 * B))
    gstat = dram("gstat", (B, 1, 4 * B))
    x1, x2, x3 = (dram(f"x_{n}", (B, C, H, W)) for n in (1, 2, 3))
    y1 = dram("y_1", (B, P, NCH, 512))
    hs = dram("branches", (B, 96, PX))
    xp = nc.dram_tensor("parts", (B, P, PX), BF16).ap()
    uy = dram("u_y", (B, C, H, W))
    u = dram("u", (B, 4, C, LINES, W))
    with ExitStack() as sems, Stage(nc, sems, "net") as s:
        with Stage(nc, sems, "l0") as s0:
            F = s0.sb("f", [P, M1 * M2, 2, B])
            spectral_forward(nc, sems, x, d, F)
            spectral_mix(nc, sems, w, F, spec)
        spectral_inverse(nc, sems, x, spec, d, d["l0_bias"], x1, gstat)
        layer_rest(nc, sems, s, d, (spec, gstat, x1, x2, x3, y1, hs, xp, uy, u), out)


def layer_rest(nc, sems, s, d, bufs, out, upto=9):
    spec, gstat, x1, x2, x3, y1, hs, xp, uy, u = bufs
    wt = {n: s.sb(n, sh, dt) for n, sh, dt in (
        ("grid", [P, NCH, 512], BF16), ("pw", [64, 32], F32), ("pb", [P, 1], F32), ("share", [P, P], F32),
        ("gb1", [P, 2], F32), ("gbo", [64, 2], F32), ("gbf", [P, 2], F32), ("eye", [P, P], F32),
        ("Z", [P, 2, 2, 32 * K9], BF16), ("L2", [96, 3, 96], F32), ("b2", [96, 1], F32), ("L3", [P, 3, 64], F32),
        ("sel", [97, 2 * K9, P], BF16))}
    GS = s.sb("GS", [P, 2, B])
    st1, sto, stf = s.sb("st1", [P, B * NCH, 6]), s.sb("sto", [64, B * NCH * 4, 6]), s.sb("stf", [P, B * 8, 6])
    co1, coo, cof = s.sb("co1", [P, 2]), s.sb("coo", [64, 2]), s.sb("cof", [P, 2])
    mod4 = lambda t: t.rearrange("b c (h q) w -> b q c h w", q=4)
    load_weights(nc, sems, d, wt)
    graph_conv(nc, sems, x1, gstat, wt, d, y1, st1)
    norm_coefficients(nc, sems, "n1", st1, P, wt["share"][:], wt["gb1"], co1)
    residual_norm(nc, sems, "r1", y1.rearrange("b p j n -> b p (j n)"), co1, mod4(x1), mod4(x2), d["pair"], GS)
    depth_conv(nc, sems, x2, GS, wt["L2"], wt["b2"], hs, xp, sto)
    norm_coefficients(nc, sems, "no", sto, 64, wt["eye"][0:64, 0:64], wt["gbo"], coo)
    deformable(nc, sems, hs, xp, coo, wt, uy, u, stf)
    norm_coefficients(nc, sems, "nf", stf, P, wt["share"][:], wt["gbf"], cof)
    residual_norm(nc, sems, "r2", u.rearrange("b q o h w -> b (q o) (h w)"), cof, mod4(x2), mod4(x3), d["pair"], GS)
    last_conv(nc, sems, x3, GS, wt["L3"], out)


def kernel(**inputs):
    import concourse.bacc as _bacc
    from concourse.bass_utils import run_bass_kernel_spmd as _run

    nc = _bacc.Bacc("TRN2", target_bir_lowering=False, num_devices=1)
    arrays = {}

    def given(name, a):
        a = np.ascontiguousarray(a)
        arrays[f"in_{name}"] = a
        return nc.dram_tensor(f"in_{name}", a.shape, mybir.dt.from_np(a.dtype), kind="ExternalInput").ap()

    x = given("x", inputs["x"])
    w = [given(n, inputs["L0_conv_" + n]) for n in ("w1r", "w1i", "w2r", "w2i")]
    d = {n: given(n, a) for n, a in {**weight_layouts(inputs), **shape_constants()}.items()}
    d["l0_bias"] = given("l0_bias", np.asarray(inputs["L0_conv_bias"]).reshape(1, C))
    d["l1_A"] = given("l1_A", inputs["L1_conv_A"])
    out = nc.dram_tensor("out_0", (B, C, H, W), F32, kind="ExternalOutput").ap()
    network(nc, x, w, d, out)
    r = _run(nc, [arrays], core_ids=[0])
    return r.results[0]["out_0"]
```

```python
from contextlib import ExitStack

import numpy as np

import concourse.bass as bass
from concourse import mybir

F32 = mybir.dt.float32
BF16 = mybir.dt.bfloat16
ALU = mybir.AluOpType
ACT = mybir.ActivationFunctionType

B, C, H, W = 8, 32, 128, 128
P = 128
PX = H * W
G = 16
M1, M2 = 32, 32
KX = 2 * M1
K9 = 9
EPS = 1e-5


class Chain:

    def __init__(self, eng, sem, base=0):
        self.eng, self.sem, self.base, self.n = eng, sem, base, 0

    def done(self, ins):
        ins.then_inc(self.sem, 1)
        self.n += 1

    def sync(self):
        self.eng.wait_ge(self.sem, self.base + self.n)


def alone(eng, passed):
    eng.sem_inc(passed, 1)


def one(ap, i):
    dims = "abcdefg"[:len(ap.shape)]
    left = " ".join(dims)
    right = "(" + " ".join(dims[:2]) + ") " + " ".join(dims[2:])
    return ap[(bass.ds(i, 1),) + (slice(None),) * (len(dims) - 1)].rearrange(f"{left} -> {right}")


class Stage:

    def __init__(self, nc, sems, name):
        self.nc, self.sems, self.name, self.ctx = nc, sems, name, ExitStack()

    def __enter__(self):
        return self

    def __exit__(self, *e):
        self.ctx.close()

    def sb(self, name, shape, dt=F32):
        return self.ctx.enter_context(self.nc.sbuf_tensor(f"{self.name}_{name}", shape, dt))

    def ps(self, name, shape):
        return self.ctx.enter_context(self.nc.psum_tensor(f"{self.name}_{name}", shape, F32))

    def sem(self, name):
        return self.sems.enter_context(self.nc.semaphore(f"{self.name}_{name}"))

    def block(self):
        return self.nc.Block()



def spectral_forward(nc, sems, x, consts, F):
    with Stage(nc, sems, "fw") as s:
        X = s.sb("x", [P, 2, C, W])
        rows = s.sb("rows", [P, KX * 3, C])
        dh = s.sb("dh", [P, KX * 3])
        dwp = s.sb("dwp", [P, 2 * M2])
        dwq = s.sb("dwq", [P, 2 * M2])
        avg = s.sb("avg", [P, P])
        st = s.sb("st", [P, G, 6])
        ag = s.sb("ag", [P, G, 2])
        mean = s.sb("mean", [P, G])
        dev = s.sb("dev", [P, G])
        rstd = s.sb("rstd", [P, G])
        ps_s = s.ps("s", [P, 512])
        ps_r = [s.ps(f"r{k}", [P, 512]) for k in range(2)]
        ps_f = [s.ps(f"f{k}", [P, 512]) for k in range(2)]
        c_in, passed = s.sem("c_in"), s.sem("passed")
        x_in = [s.sem(f"x_in{k}") for k in range(2)]
        stats, sums, rooted, normed = s.sem("stats"), s.sem("sums"), s.sem("rooted"), s.sem("normed")
        r_full, r_read, f_full, f_read, r_used = (s.sem(n) for n in ("r_full", "r_read", "f_full", "f_read", "r_used"))
        NR, NF = C // 2, KX // 2 // 8

        with s.block() as block:
            @block.sync
            def _(sp):
                for t, a in ((dh, "dft_h"), (dwp, "dft_wp"), (dwq, "dft_wq"), (avg, "avg")):
                    sp.dma_start(t[:], consts[a]).then_inc(c_in, 16)
                for k in range(2):
                    for c in range(0, C, 8):
                        sp.dma_start(X[:, k, c:c + 8], x[k].rearrange("c h w -> h c w")[:, c:c + 8]).then_inc(x_in[k], 16)
                with sp.Fori(1, B // 2) as i:
                    for k in range(2):
                        sp.wait_ge(r_full, (2 * i + k - 1) * NR)
                        alone(sp, passed)
                        for c in range(0, C, 8):
                            sp.dma_start(X[:, k, c:c + 8], one(x, 2 * i + k).rearrange("c h w -> h c w")[:, c:c + 8]).then_inc(x_in[k], 16)

            @block.vector
            def _(v):
                with v.Fori(0, B // 2) as i:
                    ch = Chain(v, stats, i * (2 * 38))
                    for k in range(2):
                        n = 2 * i + k
                        v.wait_ge(x_in[k], 64 * (i + 1))
                        for g in range(G):
                            ch.done(v.bn_stats(st[:, g], X[:, k, 2 * g:2 * g + 2, :].rearrange("p a w -> p (a w)")))
                        ch.sync()
                        alone(v, passed)
                        for g in range(G):
                            ch.done(v.bn_aggr(ag[:, g], st[:, g]))
                        ch.sync()
                        v.wait_ge(sums, 2 * n + 1)
                        ch.done(v.tensor_copy(mean[:], ps_s[:, 0:G]))
                        ch.sync()
                        ch.done(v.tensor_tensor(dev[:], ag[:, :, 0], mean[:], ALU.subtract))
                        ch.sync()
                        ch.done(v.tensor_tensor(dev[:], dev[:], dev[:], ALU.mult))
                        ch.sync()
                        ch.done(v.tensor_tensor(dev[:], dev[:], ag[:, :, 1], ALU.add))
                        v.wait_ge(sums, 2 * n + 2)
                        ch.done(v.tensor_scalar(rstd[:], ps_s[:, G:2 * G], EPS, None, ALU.add))
                        ch.sync()
                        v.wait_ge(rooted, n + 1)
                        ch.done(v.reciprocal(rstd[:], rstd[:]))
                        ch.sync()
                        for g in range(G):
                            xg = X[:, k, 2 * g:2 * g + 2, :]
                            v.tensor_scalar(xg, xg, mean[:, g:g + 1], rstd[:, g:g + 1],
                                            ALU.subtract, ALU.mult).then_inc(normed, 1)
                    assert ch.n == 2 * 38

            @block.tensor
            def _(pe):
                pe.wait_ge(c_in, 64)
                pe.sem_inc(f_full, 1)

                def means(n):
                    pe.wait_ge(stats, 38 * n + 32)
                    pe.matmul(ps_s[:, 0:G], avg[:], ag[:, :, 0], start=True, stop=True).then_inc(sums, 1)

                def variances(n):
                    pe.wait_ge(stats, 38 * n + 36)
                    pe.matmul(ps_s[:, G:2 * G], avg[:], dev[:], start=True, stop=True).then_inc(sums, 1)

                def image(n, k, more):
                    for c in range(C):
                        j = c // 2
                        if c % 2 == 0:
                            pe.wait_ge(normed, G * n + j + 1)
                            pe.wait_ge(r_read, NR * n + j + 1)
                        mm = pe.matmul(ps_r[j % 2][:, (c % 2) * KX * 3:(c % 2 + 1) * KX * 3],
                                       X[:, k, c, :], dh[:], start=True, stop=True)
                        if c % 2:
                            mm.then_inc(r_full, 1)
                    for j in range(NF):
                        if j == 0:
                            pe.wait_ge(r_read, NR * (n + 1) + 2)
                        if more and j == 1:
                            means(n + 1)
                        if more and j == 2:
                            variances(n + 1)
                        pe.wait_ge(f_read, NF * n + j + 1)
                        for q in range(8):
                            for half in range(2):
                                kx = (8 * j + q) + M1 * half
                                out = ps_f[j % 2][64 * half:64 * half + 64, 64 * q:64 * q + 64]
                                pe.matmul(out, rows[:, 3 * kx + 1:3 * kx + 3, :], dwp[:], start=True, stop=False)
                                mm = pe.matmul(out, rows[:, 3 * kx:3 * kx + 2, :], dwq[:], start=False, stop=True)
                        mm.then_inc(f_full, 1)

                means(0)
                variances(0)
                with pe.Fori(0, B // 2 - 1) as i:
                    for k in range(2):
                        image(2 * i + k, k, True)
                image(B - 2, 0, True)
                image(B - 1, 1, False)

            @block.scalar
            def _(a):
                a.sem_inc(r_read, 2)
                a.sem_inc(f_read, 2)

                def root(n):
                    a.wait_ge(stats, 38 * n + 37)
                    a.activation(rstd[:], rstd[:], ACT.Sqrt).then_inc(rooted, 1)

                def image(n, more):
                    for j in range(NR):
                        a.wait_ge(r_full, NR * n + j + 1)
                        if j == 0:
                            a.wait_ge(f_full, NF * n + 1)
                        a.activation(rows[:, :, 2 * j:2 * j + 2].rearrange("p k c -> p c k"),
                                     ps_r[j % 2][:, 0:2 * KX * 3].rearrange("p (c k) -> p c k", c=2),
                                     ACT.Copy).then_inc(r_read, 1)
                    for j in range(NF):
                        a.wait_ge(f_full, NF * n + j + 2)
                        for r in range(2):
                            ins = a.activation(
                                F[:, 8 * M2 * j:8 * M2 * (j + 1), r, bass.ds(n, 1)].rearrange("p (k y) b -> p k (y b)", k=8),
                                ps_f[j % 2][:].rearrange("p (k r y) -> p k r y", k=8, r=2)[:, :, r, :],
                                ACT.Copy)
                        ins.then_inc(f_read, 1)
                        if more and j == 1:
                            root(n + 1)

                root(0)
                with a.Fori(0, B - 1) as n:
                    image(n, True)
                with a.Fori(B - 1, B) as n:
                    image(n, False)


def spectral_mix(nc, sems, w, F, spec):
    NP = M1 // 2
    CH = 4
    with Stage(nc, sems, "mx") as s:
        WT = s.sb("w", [P, 2, C, CH * M2])
        FC = s.sb("fc", [P, 2, CH * M2, 2 * B])
        out = s.sb("out", [P, 2, 2, M2, B])
        ps = [s.ps(f"m{k}", [P, 512]) for k in range(2)]
        w_in = [s.sem(f"w_in{k}") for k in range(2)]
        passed, f_in, full, read, sent = s.sem("passed"), s.sem("f_in"), s.sem("full"), s.sem("read"), [s.sem(f"sent{k}") for k in range(2)]
        with s.block() as block:
            @block.sync
            def _(sp):
                def load(n, k):
                    for q in range(4):
                        for x in range(2):
                            src = w[q].rearrange("c o (n x) y -> n c o (x y)", x=CH)
                            sp.dma_start(WT[32 * q:32 * q + 32, k, 16 * x:16 * x + 16],
                                         one(src, n)[:, 16 * x:16 * x + 16]).then_inc(w_in[k], 16)
                for k in range(2):
                    load(k, k)
                with sp.Fori(1, M1 // CH // 2) as i:
                    for k in range(2):
                        sp.wait_ge(full, (2 * i + k - 1) * (CH // 2))
                        alone(sp, passed)
                        load(2 * i + k, k)

            @block.gpsimd
            def _(g):
                for k in range(2):
                    g.tensor_copy(FC[:, k], F[:, k * CH * M2:(k + 1) * CH * M2].rearrange("p m r b -> p m (r b)")).then_inc(f_in, 1)
                with g.Fori(1, M1 // CH // 2) as i:
                    for k in range(2):
                        g.wait_ge(full, (2 * i + k - 1) * (CH // 2))
                        alone(g, passed)
                        g.tensor_copy(FC[:, k], F[:, bass.ds((2 * i + k) * (CH * M2), CH * M2)].rearrange("p m r b -> p m (r b)")).then_inc(f_in, 1)

            @block.tensor
            def _(pe):
                pe.sem_inc(read, 2)
                with pe.Fori(0, M1 // CH // 2) as i:
                    for k in range(2):
                        pe.wait_ge(w_in[k], 128 * (i + 1))
                        pe.wait_ge(f_in, 2 * i + k + 1)
                        for j in range(CH // 2):
                            n = (2 * i + k) * (CH // 2) + j
                            pe.wait_ge(read, n + 1)
                            alone(pe, passed)
                            for par in range(2):
                                for ky in range(M2):
                                    m = (2 * j + par) * M2 + ky
                                    for half in range(2):
                                        r = slice(64 * half, 64 * half + 64)
                                        o = 64 * par + 32 * half
                                        mm = pe.matmul(ps[j % 2][o:o + 32, 16 * ky:16 * ky + 16], WT[r, k, :, m],
                                                       FC[r, k, m, :], start=True, stop=True,
                                                       tile_position=(64 * half, o))
                            mm.then_inc(full, 1)

            @block.vector
            def _(v):
                with v.Fori(0, NP // 2) as i:
                    for k in range(2):
                        n = 2 * i + k
                        v.wait_ge(full, n + 1)
                        v.wait_ge(sent[k], 16 * (i + 1))
                        for r in range(2):
                            ins = v.tensor_copy(out[:, k, r], ps[k][:].rearrange("p (y r b) -> p y r b", r=2, b=B)[:, :, r, :])
                        ins.then_inc(read, 1)

            @block.scalar
            def _(a):
                for k in range(2):
                    a.sem_inc(sent[k], 16)
                with a.Fori(0, NP // 2) as i:
                    for k in range(2):
                        a.wait_ge(read, 2 * i + k + 3)
                        a.dma_start(one(spec, 2 * i + k), out[:, k].rearrange("p r y b -> p (r y b)")).then_inc(sent[k], 16)
                for k in range(2):
                    a.wait_ge(sent[k], 16 + 16 * (NP // 2))


def spectral_inverse(nc, sems, x, spec, consts, bias, x1, gstat):
    OC = 4
    with Stage(nc, sems, "iv") as s:
        Gk = s.sb("g", [P, 2, OC, M2, B])
        X = s.sb("x", [P, 2, B, OC, W])
        Z = s.sb("z", [P, 2, 4, H])
        er, ei, ew = (s.sb(n, [P, P]) for n in ("er", "ei", "ew"))
        avg = s.sb("avg", [P, P])
        bs = s.sb("bs", [P, C])
        NG = 2 * B
        st = s.sb("st", [P, NG, 6])
        ag = s.sb("ag", [P, NG, 2])
        mean, dev = s.sb("mean", [P, NG]), s.sb("dev", [P, NG])
        res = s.sb("res", [P, 2, 2, B])
        ps_z = [s.ps(f"z{k}", [P, 512]) for k in range(2)]
        ps_y = [s.ps(f"y{k}", [P, 512]) for k in range(4)]
        ps_s = s.ps("s", [P, 512])
        c_in, passed = s.sem("c_in"), s.sem("passed")
        in_ = [s.sem(f"in{k}") for k in range(2)]
        z_full, z_done, y_full, y_done, stats, sums, rooted, r_sent = (
            s.sem(n) for n in ("z_full", "z_done", "y_full", "y_done", "stats", "sums", "rooted", "r_sent"))
        sent = [s.sem(f"sent{k}") for k in range(2)]
        r_free = s.sem("r_free")
        NZ = B * OC // 8
        CHN = 2 * NG + 7

        with s.block() as block:
            @block.sync
            def _(sp):
                for t, a in ((er, "inv_hr"), (ei, "inv_hi"), (ew, "inv_w"), (avg, "avg")):
                    sp.dma_start(t[:], consts[a]).then_inc(c_in, 16)
                sp.dma_start(bs[:], bias.partition_broadcast(P)).then_inc(c_in, 16)

                def load(n, k):
                    src = spec.rearrange("j (par hl n o) f -> n par hl j o f", par=2, hl=2, o=OC)
                    for ri in range(2):
                        for hl in range(2):
                            for par in range(2):
                                p0 = 64 * ri + 32 * hl + 16 * par
                                sp.dma_start(Gk[p0:p0 + 16, k].rearrange("p o y b -> p o (y b)"),
                                             one(src, n)[par, hl, :, :, ri * M2 * B:(ri + 1) * M2 * B]).then_inc(in_[k], 16)
                    xs = x.rearrange("b (n o) h w -> n h b o w", o=OC)
                    for b in range(B):
                        sp.dma_start(X[:, k, b], one(xs, n)[:, b]).then_inc(in_[k], 16)
                for k in range(2):
                    load(k, k)
                with sp.Fori(1, C // OC // 2) as i:
                    for k in range(2):
                        sp.wait_ge(sent[k], 16 * B * i)
                        alone(sp, passed)
                        sp.wait_ge(stats, CHN * (2 * i + k - 1))
                        alone(sp, passed)
                        load(2 * i + k, k)

            @block.tensor
            def _(pe):
                pe.wait_ge(c_in, 80)
                pe.sem_inc(z_done, 2)
                pe.sem_inc(y_done, 4)

                def means(n):
                    pe.wait_ge(stats, CHN * n + 2 * NG)
                    pe.matmul(ps_s[:, 0:NG], avg[:], ag[:, :, 0], start=True, stop=True).then_inc(sums, 1)

                def variances(n):
                    pe.wait_ge(stats, CHN * n + 2 * NG + 4)
                    pe.matmul(ps_s[:, NG:2 * NG], avg[:], dev[:], start=True, stop=True).then_inc(sums, 1)

                def chunk(i, k, behind):
                    n = 2 * i + k
                    pe.wait_ge(in_[k], 256 * (i + 1))

                    def over_h(j):
                        pe.wait_ge(z_done, NZ * n + j + 1)
                        for m in range(8):
                            b, o = divmod(8 * j + m, OC)
                            for r, e in enumerate((er, ei)):
                                p0 = 64 * (m % 2) + 32 * r
                                mm = pe.matmul(ps_z[j % 2][p0:p0 + 32, 128 * (m // 2):128 * (m // 2) + 128],
                                               Gk[:, k, o, :, b], e[:], start=True, stop=True)
                        mm.then_inc(z_full, 1)

                    def over_w(j):
                        pe.wait_ge(z_done, NZ * n + j + 3)
                        pe.wait_ge(y_done, 2 * NZ * n + 2 * j + 2)
                        for m in range(8):
                            h = slice(64 * (m % 2), 64 * (m % 2) + 64)
                            q = 128 * (m // 2)
                            mm = pe.matmul(ps_y[(2 * j + m % 2) % 4][:, q:q + 128], Z[h, j % 2, m // 2, :],
                                           ew[h, :], start=True, stop=True)
                            if m >= 6:
                                mm.then_inc(y_full, 1)
                    over_h(0)
                    for j in range(NZ):
                        if j + 1 < NZ:
                            over_h(j + 1)
                        over_w(j)
                        if behind and j < 2:
                            (means, variances)[j](n - 1)

                for k in range(2):
                    chunk(0, k, k == 1)
                with pe.Fori(1, C // OC // 2) as i:
                    for k in range(2):
                        chunk(i, k, True)
                means(C // OC - 1)
                variances(C // OC - 1)

            @block.scalar
            def _(a):
                def root(n):
                    a.wait_ge(stats, CHN * (n + 1) - 1)
                    a.activation(res[:, :, 1], res[:, :, 1], ACT.Sqrt).then_inc(rooted, 1)

                def chunk(n, behind):
                    for j in range(NZ):
                        a.wait_ge(z_full, NZ * n + j + 1)
                        if j >= 2:
                            a.wait_ge(y_full, 2 * (NZ * n + j - 1))
                        a.activation(Z[:, j % 2].rearrange("p m h -> p (m h)"), ps_z[j % 2][:], ACT.Copy).then_inc(z_done, 1)
                        if behind and j == 2:
                            root(n - 1)

                chunk(0, False)
                with a.Fori(1, C // OC) as n:
                    chunk(n, True)
                root(C // OC - 1)

            @block.vector
            def _(v):
                v.wait_ge(c_in, 80)
                with v.Fori(0, C // OC // 2) as i:
                    ch = Chain(v, stats, i * (2 * CHN))
                    for k in range(2):
                        n = 2 * i + k
                        v.wait_ge(in_[k], 256 * (i + 1))
                        for y in range(2 * NZ):
                            v.wait_ge(y_full, 2 * NZ * n + y + 1)
                            for q in range(4):
                                o = y % 2 + 2 * (q % 2)
                                xo = X[:, k, 2 * (y // 2) + q // 2, o, :]
                                ins = v.scalar_tensor_tensor(out=xo, in0=ps_y[y % 4][:, 128 * q:128 * q + 128],
                                                             scalar=bs[:, bass.ds(n * OC + o, 1)],
                                                             in1=xo, op0=ALU.add, op1=ALU.add)
                            ins.then_inc(y_done, 1)
                        v.wait_ge(y_done, 2 * NZ * (n + 1) + 4)
                        for g in range(NG):
                            ch.done(v.bn_stats(st[:, g], X[:, k, g // 2, 2 * (g % 2):2 * (g % 2) + 2, :].rearrange("p o w -> p (o w)")))
                        ch.sync()
                        alone(v, passed)
                        for g in range(NG):
                            ch.done(v.bn_aggr(ag[:, g], st[:, g]))
                        ch.sync()
                        v.wait_ge(sums, 2 * n + 1)
                        ch.done(v.tensor_copy(mean[:], ps_s[:, 0:NG]))
                        ch.sync()
                        ch.done(v.tensor_tensor(dev[:], ag[:, :, 0], mean[:], ALU.subtract))
                        ch.sync()
                        ch.done(v.tensor_tensor(dev[:], dev[:], dev[:], ALU.mult))
                        ch.sync()
                        ch.done(v.tensor_tensor(dev[:], dev[:], ag[:, :, 1], ALU.add))
                        ch.sync()
                        v.wait_ge(r_free, n + 1)
                        ch.done(v.tensor_copy(res[:, :, 0], mean[:].rearrange("p (b q) -> p q b", q=2)))
                        v.wait_ge(sums, 2 * n + 2)
                        ch.done(v.tensor_scalar(res[:, :, 1], ps_s[:, NG:2 * NG].rearrange("p (b q) -> p q b", q=2), EPS, None, ALU.add))
                        v.wait_ge(rooted, n + 1)
                        ch.done(v.reciprocal(res[:, :, 1], res[:, :, 1]))
                    assert ch.n == 2 * CHN

            @block.gpsimd
            def _(g):
                g.sem_inc(r_free, 1)
                with g.Fori(0, C // OC // 2) as i:
                    for k in range(2):
                        n = 2 * i + k
                        g.wait_ge(y_done, 2 * NZ * (n + 1) + 4)
                        alone(g, passed)
                        for b in range(B):
                            g.dma_start(one(x1.rearrange("b (n o) h w -> n h b o w", o=OC), n)[:, b], X[:, k, b]).then_inc(sent[k], 16)
                        g.wait_ge(stats, CHN * (n + 1))
                        alone(g, passed)
                        g.dma_start(one(gstat, n), res[0:1].rearrange("p q t b -> p (q t b)")).then_inc(r_sent, 16)
                        g.wait_ge(r_sent, 16 * (n + 1))
                        alone(g, passed)
                        g.sem_inc(r_free, 1)
                for k in range(2):
                    g.wait_ge(sent[k], 16 * B * (C // OC // 2))
                g.wait_ge(r_sent, 16 * (C // OC))


def norm_coefficients(nc, sems, name, st, parts, share, gb, out):
    n = st.shape[1]
    with Stage(nc, sems, name) as s:
        ag = s.sb("ag", [parts, 2])
        dev = s.sb("dev", [parts, 1])
        cs = s.sb("cs", [parts, 3])
        ps = s.ps("ps", [P, 512])
        steps, sums, rooted = s.sem("steps"), s.sem("sums"), s.sem("rooted")
        with s.block() as block:
            @block.vector
            def _(v):
                ch = Chain(v, steps)
                ch.done(v.bn_aggr(ag[:], st[0:parts].rearrange("p n s -> p (n s)")))
                v.wait_ge(sums, 1)
                ch.done(v.tensor_copy(cs[:, 0:1], ps[0:parts, 0:1]))
                ch.sync()
                ch.done(v.tensor_tensor(dev[:], ag[:, 0:1], cs[:, 0:1], ALU.subtract))
                ch.sync()
                ch.done(v.tensor_tensor(dev[:], dev[:], dev[:], ALU.mult))
                ch.sync()
                ch.done(v.tensor_tensor(dev[:], dev[:], ag[:, 1:2], ALU.add))
                v.wait_ge(sums, 2)
                ch.done(v.tensor_scalar(cs[:, 1:2], ps[0:parts, 1:2], EPS, None, ALU.add))
                v.wait_ge(rooted, 1)
                ch.done(v.reciprocal(cs[:, 1:2], cs[:, 1:2]))
                ch.sync()
                ch.done(v.tensor_tensor(out[:, 0:1], cs[:, 1:2], gb[:, 0:1], ALU.mult))
                ch.sync()
                ch.done(v.tensor_tensor(cs[:, 2:3], cs[:, 0:1], out[:, 0:1], ALU.mult))
                ch.sync()
                v.tensor_tensor(out[:, 1:2], gb[:, 1:2], cs[:, 2:3], ALU.subtract)

            @block.tensor
            def _(pe):
                pe.wait_ge(steps, 1)
                pe.matmul(ps[0:parts, 0:1], share, ag[:, 0:1], start=True, stop=True).then_inc(sums, 1)
                pe.wait_ge(steps, 5)
                pe.matmul(ps[0:parts, 1:2], share, dev[:], start=True, stop=True).then_inc(sums, 1)

            @block.scalar
            def _(a):
                a.wait_ge(steps, 6)
                a.activation(cs[:, 1:2], cs[:, 1:2], ACT.Sqrt).then_inc(rooted, 1)


RC = 16
NCH = H // RC


def load_row_pairs(sp, X, k, img, j, got, pad=0, rows=RC):
    R2 = rows // 2
    for d in range(4):
        r0 = j * rows + d - 1
        a = 1 if r0 < 0 else 0
        e = R2 - 1 if r0 + 2 * (R2 - 1) >= H else R2
        sp.dma_start(X[32 * d:32 * d + 32, k, a:e, pad:pad + W], img[:, r0 + 2 * a:r0 + 2 * (e - 1) + 1:2, :]).then_inc(got, 16)


def graph_conv(nc, sems, x1, gstat, wt, wts, y1, st):
    R2 = RC // 2
    NX = 4
    with Stage(nc, sems, "gc") as s:
        X = s.sb("x", [P, NX, R2, W])
        Y, YT = s.sb("y", [P, 2, 512]), s.sb("yt", [P, 2, 512])
        O = s.sb("o", [P, NX, 512])
        GS = s.sb("gs", [P, 2, B])
        cw, cb = s.sb("cw", [P, 2 * C]), s.sb("cb", [P, 1])
        A = s.sb("A", [P, P])
        ps_c, ps_t, ps_a = ([s.ps(f"{n}{k}", [P, 512]) for k in range(2)] for n in "cta")
        c_in, g_in, passed, set_ = s.sem("c_in"), s.sem("g_in"), s.sem("passed"), s.sem("set")
        x_in, sent = ([s.sem(f"{n}{k}") for k in range(NX)] for n in ("x_in", "sent"))
        normed, edged = s.sem("normed"), s.sem("edged")
        conv, counted = s.sem("conv"), s.sem("counted")
        y_done, turned, t_done, prod, o_done = (s.sem(n) for n in ("y_done", "turned", "t_done", "prod", "o_done"))

        with s.block() as block:
            @block.sync
            def _(sp):
                sp.dma_start(cw[:], wts["l1_w"]).then_inc(c_in, 16)
                sp.dma_start(cb[:], wts["l1_b"]).then_inc(c_in, 16)
                sp.dma_start(A[:], wts["l1_A"]).then_inc(c_in, 16)
                for d in range(4):
                    for e in range(2):
                        sp.dma_start(GS[32 * d + e:32 * d + 32:2].rearrange("p t b -> p (t b)"),
                                     gstat.rearrange("n a (q t) -> (n a q) t", q=2)).then_inc(g_in, 16)
                sp.wait_ge(set_, 1)
                with sp.Fori(0, B) as b:
                    for j in range(NCH):
                        sp.wait_ge(conv, b * NCH + j + 1)
                        alone(sp, passed)
                        load_row_pairs(sp, X, j % NX, one(x1, b), j, x_in[j % NX])

            @block.gpsimd
            def _(g):
                g.memset(X[:], 0.0).then_inc(set_, 1)

            @block.vector
            def _(v):
                v.wait_ge(g_in, 128)
                v.sem_inc(counted, NX)
                v.sem_inc(t_done, 2)

                def normalise(b, j):
                    k = j % NX
                    v.wait_ge(x_in[k], 64 * (b * (NCH // NX) + j // NX + 1))
                    xk = X[:, k].rearrange("p r w -> p (r w)")
                    v.tensor_scalar(xk, xk, GS[:, 0, bass.ds(b, 1)], GS[:, 1, bass.ds(b, 1)],
                                    ALU.subtract, ALU.mult).then_inc(normed, 1)
                    if j in (0, NCH - 1):
                        v.wait_ge(normed, b * NCH + j + 1)
                        edge = X[0:32, k, 0, :] if j == 0 else X[96:128, k, R2 - 1, :]
                        v.memset(edge, 0.0).then_inc(edged, 1)

                with v.Fori(0, B) as b:
                    n = b * NCH
                    normalise(b, 0)
                    for j in range(NCH + 3):
                        if j + 1 < NCH:
                            normalise(b, j + 1)
                        if 1 <= j <= NCH:
                            v.wait_ge(turned, n + j - 1 + 3)
                            v.wait_ge(prod, n + j - 1 + 1)
                            v.tensor_copy(YT[:, (j - 1) % 2], ps_t[(j - 1) % 2][:]).then_inc(t_done, 1)
                        if j >= 3:
                            v.wait_ge(o_done, n + j - 3 + 3)
                            v.bn_stats(st[:, bass.ds(n + j - 3, 1), :].rearrange("p a s -> p (a s)"),
                                       O[:, (j - 3) % NX]).then_inc(counted, 1)

            @block.tensor
            def _(pe):
                pe.wait_ge(c_in, 48)
                pe.wait_ge(set_, 1)
                pe.sem_inc(conv, NX)
                pe.sem_inc(turned, 2)
                pe.sem_inc(prod, 2)
                with pe.Fori(0, B) as b:
                    n = b * NCH
                    for j in range(NCH + 2):
                        if j < NCH:
                            pe.wait_ge(normed, n + j + 1)
                            if j == 0:
                                pe.wait_ge(edged, 2 * b + 1)
                            if j == NCH - 1:
                                pe.wait_ge(edged, 2 * b + 2)
                            pe.wait_ge(y_done, n + j + 1)
                            alone(pe, passed)
                            for t in range(2):
                                mm = pe.matmul(ps_c[j % 2][64 * t:64 * t + 64, :], cw[:], X[:, j % NX, t:R2:2, :],
                                               start=True, stop=True)
                            mm.then_inc(conv, 1)
                        if 1 <= j <= NCH:
                            k = (j - 1) % 2
                            pe.wait_ge(y_done, n + j - 1 + 3)
                            pe.wait_ge(t_done, n + j - 1 + 1)
                            alone(pe, passed)
                            for r in range(4):
                                c = slice(P * r, P * r + P)
                                mm = pe.transpose(ps_t[k][:, c], Y[:, k, c], wt["eye"][:])
                            mm.then_inc(turned, 1)
                        if j >= 2:
                            k = (j - 2) % 2
                            pe.wait_ge(t_done, n + j - 2 + 3)
                            pe.wait_ge(o_done, n + j - 2 + 1)
                            alone(pe, passed)
                            for r in range(4):
                                c = slice(P * r, P * r + P)
                                mm = pe.matmul(ps_a[k][:, c], YT[:, k, c], A[:], start=True, stop=True)
                            mm.then_inc(prod, 1)

            @block.scalar
            def _(a):
                a.sem_inc(y_done, 2)
                a.sem_inc(o_done, 2)
                for k in range(NX):
                    a.sem_inc(sent[k], 16)
                a.wait_ge(c_in, 48)

                def store(b, j):
                    a.wait_ge(o_done, b * NCH + j + 3)
                    alone(a, passed)
                    a.dma_start(one(y1, b)[:, j], O[:, j % NX]).then_inc(sent[j % NX], 16)

                with a.Fori(0, B) as b:
                    n = b * NCH
                    for j in range(NCH + 2):
                        if j < NCH:
                            a.wait_ge(conv, n + j + NX + 1)
                            a.wait_ge(turned, n + j + 1)
                            a.activation(Y[:, j % 2], ps_c[j % 2][:], ACT.Relu, bias=cb[:, 0:1]).then_inc(y_done, 1)
                        if j >= 3:
                            store(b, j - 3)
                        if j >= 2:
                            m = j - 2
                            a.wait_ge(prod, n + m + 3)
                            a.wait_ge(sent[m % NX], 16 * (b * (NCH // NX) + m // NX + 1))
                            a.wait_ge(counted, n + m + 1)
                            a.activation(O[:, m % NX], ps_a[m % 2][:], ACT.Copy).then_inc(o_done, 1)
                    store(b, NCH - 1)
                for k in range(NX):
                    a.wait_ge(sent[k], 16 + 16 * B * NCH // NX)


def residual_norm(nc, sems, name, y, coef, x, x_out, pair, GS):
    N = PX // 4
    with Stage(nc, sems, name) as s:
        NS = 4
        Y = s.sb("y", [P, NS, N])
        X = s.sb("x", [P, NS, N])
        st = s.sb("st", [P, 8, 6])
        ag = s.sb("ag", [P, 2])
        dev = s.sb("dev", [P, 1])
        pr = s.sb("pr", [P, P])
        ps = s.ps("ps", [P, 512])
        c_in, passed = s.sem("c_in"), s.sem("passed")
        got, sent = ([s.sem(f"{n}{k}") for k in range(NS)] for n in ("in", "sent"))
        act, steps, sums, rooted = s.sem("act"), s.sem("steps"), s.sem("sums"), s.sem("rooted")
        ST = 1 + 8 + 1 + 1 + 1 + 1 + 1 + 1 + 1
        with s.block() as block:
            @block.sync
            def _(sp):
                sp.dma_start(pr[:], pair).then_inc(c_in, 16)
                with sp.Fori(0, B // NS) as i:
                    for k in range(NS):
                        sp.wait_ge(sent[k], 64 * (i + 1))
                        alone(sp, passed)
                        sp.wait_ge(rooted, NS * i + k + 1)
                        alone(sp, passed)
                        sp.dma_start(Y[:, k], one(y, NS * i + k)).then_inc(got[k], 16)
                        for q in range(4):
                            r = slice(32 * q, 32 * q + 32)
                            xv = X[r, k].rearrange("p (h w) -> p h w", w=W)
                            sp.dma_start(xv, one(x, NS * i + k)[q]).then_inc(got[k], 16)

            @block.scalar
            def _(a):
                a.sem_inc(rooted, NS)
                for k in range(NS):
                    a.sem_inc(sent[k], 64)

                def finish(i, k):
                    n = NS * i + k
                    a.wait_ge(steps, ST * n + 3)
                    alone(a, passed)
                    for q in range(4):
                        r = slice(32 * q, 32 * q + 32)
                        xv = X[r, k].rearrange("p (h w) -> p h w", w=W)
                        a.dma_start(one(x_out, n)[q], xv).then_inc(sent[k], 16)
                    a.wait_ge(steps, ST * n + ST - 1 + 2)
                    alone(a, passed)
                    gv = GS[:, 1, bass.ds(n, 1)]
                    a.activation(gv, gv, ACT.Sqrt).then_inc(rooted, 1)

                with a.Fori(0, B // NS) as i:
                    for k in range(NS):
                        a.wait_ge(got[k], 80 * (i + 1))
                        a.activation(Y[:, k], Y[:, k], ACT.Relu, bias=coef[:, 1:2], scale=coef[:, 0:1]).then_inc(act, 1)
                        if k:
                            finish(i, k - 1)
                    finish(i, NS - 1)
                for k in range(NS):
                    a.wait_ge(sent[k], 64 * (B // NS + 1))

            @block.vector
            def _(v):
                v.sem_inc(steps, 2)
                with v.Fori(0, B // NS) as i:
                    ch = Chain(v, steps, i * (NS * ST) + 2)
                    for k in range(NS):
                        n = NS * i + k
                        v.wait_ge(act, n + 1)
                        ch.done(v.tensor_tensor(X[:, k], X[:, k], Y[:, k], ALU.add))
                        ch.sync()
                        for q in range(8):
                            ch.done(v.bn_stats(st[:, q], X[:, k, 512 * q:512 * q + 512]))
                        ch.sync()
                        alone(v, passed)
                        ch.done(v.bn_aggr(ag[:], st[:].rearrange("p q s -> p (q s)")))
                        v.wait_ge(sums, 2 * n + 1)
                        ch.done(v.tensor_copy(GS[:, 0, bass.ds(n, 1)], ps[:, 0:1]))
                        ch.sync()
                        ch.done(v.tensor_tensor(dev[:], ag[:, 0:1], GS[:, 0, bass.ds(n, 1)], ALU.subtract))
                        ch.sync()
                        ch.done(v.tensor_tensor(dev[:], dev[:], dev[:], ALU.mult))
                        ch.sync()
                        ch.done(v.tensor_tensor(dev[:], dev[:], ag[:, 1:2], ALU.add))
                        v.wait_ge(sums, 2 * n + 2)
                        ch.done(v.tensor_scalar(GS[:, 1, bass.ds(n, 1)], ps[:, 1:2], EPS, None, ALU.add))
                        v.wait_ge(rooted, n + 1 + NS)
                        alone(v, passed)
                        ch.done(v.reciprocal(GS[:, 1, bass.ds(n, 1)], GS[:, 1, bass.ds(n, 1)]))
                    assert ch.n == NS * ST

            @block.tensor
            def _(pe):
                pe.wait_ge(c_in, 16)
                with pe.Fori(0, B) as n:
                    pe.wait_ge(steps, ST * n + 2 + 10)
                    pe.matmul(ps[:, 0:1], pr[:], ag[:, 0:1], start=True, stop=True).then_inc(sums, 1)
                    pe.wait_ge(steps, ST * n + 2 + 14)
                    pe.matmul(ps[:, 1:2], pr[:], dev[:], start=True, stop=True).then_inc(sums, 1)


def depth_conv(nc, sems, x2, GS, wt, hs, up, xp, st):
    R2 = RC // 2
    NX = 4
    with Stage(nc, sems, "dc") as s:
        X = s.sb("x", [P, NX, R2, W + 2])
        O = s.sb("o", [P, 2, 3 * 512])
        N = PX // 4
        XI = s.sb("xi", [P, N])
        XH, XM, XL = (s.sb(n, [P, N], BF16) for n in ("xh", "xm", "xl"))
        img_in, img_n, cut, xp_out, xp_free = (s.sem(n) for n in ("img_in", "img_n", "cut", "xp_out", "xp_free"))
        ps = [s.ps(f"c{k}", [P, 512]) for k in range(6)]
        set_, passed = s.sem("set"), s.sem("passed")
        x_in = [s.sem(f"x_in{k}") for k in range(NX)]
        sent = [s.sem(f"sent{k}") for k in range(2)]
        normed, edged = s.sem("normed"), s.sem("edged")
        conv, o_done, counted = s.sem("conv"), s.sem("o_done"), s.sem("counted")
        with s.block() as block:
            @block.sync
            def _(sp):
                sp.wait_ge(set_, 1)
                with sp.Fori(0, B) as b:
                    for j in range(NCH):
                        sp.wait_ge(conv, 3 * (b * NCH + j + 1))
                        alone(sp, passed)
                        load_row_pairs(sp, X, j % NX, one(x2, b), j, x_in[j % NX], pad=1)
                        if j == 1:
                            sp.wait_ge(xp_free, b + 1)
                            alone(sp, passed)
                            for q in range(4):
                                sp.dma_start(XI[32 * q:32 * q + 32], one(x2, b)[:, 32 * q:32 * q + 32, :]).then_inc(img_in, 16)

            @block.gpsimd
            def _(g):
                g.memset(X[:], 0.0).then_inc(set_, 1)
                g.sem_inc(xp_free, 1)

                def store(b, t, x):
                    for q in range(4):
                        g.dma_start(one(xp, b)[32 * x:32 * x + 32, N * q:N * q + N], t[32 * q:32 * q + 32]).then_inc(xp_out, 16)

                with g.Fori(0, B) as b:
                    g.wait_ge(img_n, b + 1)
                    alone(g, passed)
                    g.tensor_copy(XH[:], XI[:]).then_inc(cut, 1)
                    g.wait_ge(cut, 4 * b + 1)
                    alone(g, passed)
                    g.tensor_tensor(XI[:], XI[:], XH[:], ALU.subtract).then_inc(cut, 1)
                    store(b, XH, 0)
                    store(b, XH, 3)
                    g.wait_ge(cut, 4 * b + 2)
                    alone(g, passed)
                    g.tensor_copy(XM[:], XI[:]).then_inc(cut, 1)
                    g.wait_ge(cut, 4 * b + 3)
                    alone(g, passed)
                    store(b, XM, 1)
                    g.tensor_tensor(XL[:], XI[:], XM[:], ALU.subtract).then_inc(cut, 1)
                    g.wait_ge(cut, 4 * b + 4)
                    alone(g, passed)
                    store(b, XL, 2)
                    g.wait_ge(xp_out, 256 * (b + 1))
                    alone(g, passed)
                    g.sem_inc(xp_free, 1)

            @block.vector
            def _(v):
                v.sem_inc(counted, 4)
                with v.Fori(0, B) as b:
                    for j in range(NCH + 1):
                        if j < NCH:
                            k = j % NX
                            v.wait_ge(x_in[k], 64 * (b * (NCH // NX) + j // NX + 1))
                            xk = X[:, k, :, 1:W + 1]
                            v.tensor_scalar(xk, xk, GS[:, 0, bass.ds(b, 1)], GS[:, 1, bass.ds(b, 1)],
                                            ALU.subtract, ALU.mult).then_inc(normed, 1)
                            if j in (0, NCH - 1):
                                v.wait_ge(normed, b * NCH + j + 1)
                                edge = X[0:32, k, 0, :] if j == 0 else X[96:128, k, R2 - 1, :]
                                v.memset(edge, 0.0).then_inc(edged, 1)
                        if j == 2:
                            v.wait_ge(img_in, 64 * (b + 1))
                            v.tensor_scalar(XI[:], XI[:], GS[:, 0, bass.ds(b, 1)], GS[:, 1, bass.ds(b, 1)],
                                            ALU.subtract, ALU.mult).then_inc(img_n, 1)
                        if j:
                            n = b * NCH + j - 1
                            for m in range(2):
                                v.wait_ge(o_done, 3 * n + m + 7)
                                v.bn_stats(st[:, bass.ds(2 * n + m, 1), :].rearrange("p a s -> p (a s)"),
                                           O[:, (j - 1) % 2, 512 * m:512 * m + 512]).then_inc(counted, 1)

            @block.tensor
            def _(pe):
                pe.sem_inc(conv, 3 * NX)
                with pe.Fori(0, B) as b:
                    for j in range(NCH):
                        k = j % NX
                        n = b * NCH + j
                        pe.wait_ge(normed, n + 1)
                        if j == 0:
                            pe.wait_ge(edged, 2 * b + 1)
                        if j == NCH - 1:
                            pe.wait_ge(edged, 2 * b + 2)
                        for m in range(3):
                            bank = ps[3 * (j % 2) + m]
                            pe.wait_ge(o_done, 3 * n + m + 1)
                            alone(pe, passed)
                            for d in range(3):
                                if m < 2:
                                    mm = pe.matmul(bank[:], wt["LD"][:, d, :], X[:, k, 4 * m:4 * m + 4, d:d + W],
                                                   start=(d == 0), stop=(d == 2))
                                else:
                                    for t in range(2):
                                        mm = pe.matmul(bank[64 * t:64 * t + 64, :], wt["LP"][:, d, :], X[:, k, t:R2:2, d:d + W],
                                                       start=(d == 0), stop=(d == 2))
                            mm.then_inc(conv, 1)

            @block.scalar
            def _(a):
                a.sem_inc(o_done, 6)
                for k in range(2):
                    a.sem_inc(sent[k], 32)
                with a.Fori(0, B) as b:
                    for j in range(NCH):
                        k = j % 2
                        n = b * NCH + j
                        a.wait_ge(sent[k], 32 * (b * (NCH // 2) + j // 2 + 1))
                        a.wait_ge(counted, 2 * n + 2)
                        for m in range(3):
                            a.wait_ge(conv, 3 * n + m + 1 + 3 * NX)
                            a.activation(O[:, k, 512 * m:512 * m + 512], ps[3 * k + m][:], ACT.Identity,
                                         bias=wt["bp" if m == 2 else "bd"][:, 0:1]).then_inc(o_done, 1)
                        a.wait_ge(o_done, 3 * n + 9)
                        alone(a, passed)
                        a.dma_start(one(hs, b)[:, j * R2 * W:(j + 1) * R2 * W], O[:, k, 0:1024]).then_inc(sent[k], 16)
                        a.dma_start(one(up, b)[:, j * 512:(j + 1) * 512], O[:, k, 1024:1536]).then_inc(sent[k], 16)
                for k in range(2):
                    a.wait_ge(sent[k], 32 + 32 * B * NCH // 2)
                a.wait_ge(xp_out, 256 * B)


def last_conv(nc, sems, x3, GS, LW, pick, out):
    RL = 2 * RC
    R2, NL, NX = RL // 2, H // RL, 2
    with Stage(nc, sems, "lc") as s:
        X = s.sb("x", [P, NX, R2, W])
        XN = s.sb("xn", [P, NX, R2, W + 2])
        O = s.sb("o", [P, NX, R2 * W // 2])
        ps = [s.ps(f"c{k}", [P, 512]) for k in range(4)]
        Q = R2 // 8
        set_, passed = s.sem("set"), s.sem("passed")
        x_in, sent = ([s.sem(f"{n}{k}") for k in range(NX)] for n in ("x_in", "sent"))
        normed, edged = s.sem("normed"), s.sem("edged")
        conv, o_done = s.sem("conv"), s.sem("o_done")
        with s.block() as block:
            @block.sync
            def _(sp):
                sp.wait_ge(set_, 2)
                with sp.Fori(0, B) as b:
                    for j in range(NL):
                        sp.wait_ge(conv, Q * (b * NL + j + 1))
                        alone(sp, passed)
                        load_row_pairs(sp, X, j % NX, one(x3, b), j, x_in[j % NX], rows=RL)

            @block.gpsimd
            def _(g):
                g.memset(X[:], 0.0).then_inc(set_, 1)
                g.memset(XN[:], 0.0).then_inc(set_, 1)

            @block.vector
            def _(v):
                with v.Fori(0, B) as b:
                    for j in range(NL):
                        k = j % NX
                        n = b * NL + j
                        v.wait_ge(x_in[k], 64 * (b * (NL // NX) + j // NX + 1))
                        v.wait_ge(conv, Q * (n + 1))
                        alone(v, passed)
                        v.tensor_scalar(XN[:, k, :, 1:W + 1], X[:, k], GS[:, 0, bass.ds(b, 1)], GS[:, 1, bass.ds(b, 1)],
                                        ALU.subtract, ALU.mult).then_inc(normed, 1)
                        if j in (0, NL - 1):
                            v.wait_ge(normed, n + 1)
                            r = slice(0, 32) if j == 0 else slice(96, 128)
                            i = 0 if j == 0 else R2 - 1
                            v.memset(XN[r, k, i, :], 0.0).then_inc(edged, 1)
                            v.memset(X[r, k, i, :], 0.0).then_inc(edged, 1)

            @block.tensor
            def _(pe):
                pe.sem_inc(conv, NX * Q)
                with pe.Fori(0, B) as b:
                    for j in range(NL):
                        k = j % NX
                        n = b * NL + j
                        pe.wait_ge(normed, n + 1)
                        if j == 0:
                            pe.wait_ge(edged, 4 * b + 2)
                        if j == NL - 1:
                            pe.wait_ge(edged, 4 * b + 4)
                        for m in range(Q):
                            bank = ps[Q * k + m]
                            pe.wait_ge(o_done, Q * n + m + 1)
                            alone(pe, passed)
                            for d in range(4):
                                for t in range(2):
                                    pairs = slice(8 * m + t, 8 * m + 8, 2)
                                    line = XN[:, k, pairs, d:d + W] if d < 3 else X[:, k, pairs, :]
                                    w = LW[:, d, :] if d < 3 else pick
                                    mm = pe.matmul(bank[64 * t:64 * t + 64, :], w, line, start=(d == 0), stop=(d == 3))
                            mm.then_inc(conv, 1)

            @block.scalar
            def _(a):
                a.sem_inc(o_done, 2 * Q)
                for k in range(NX):
                    a.sem_inc(sent[k], 64)
                with a.Fori(0, B) as b:
                    for j in range(NL):
                        k = j % NX
                        n = b * NL + j
                        a.wait_ge(sent[k], 64 * (b * (NL // NX) + j // NX + 1))
                        for m in range(Q):
                            a.wait_ge(conv, Q * n + m + 1 + NX * Q)
                            a.activation(O[:, k, 512 * m:512 * m + 512], ps[Q * k + m][:], ACT.Copy).then_inc(o_done, 1)
                        a.wait_ge(o_done, Q * (n + 1) + 2 * Q)
                        alone(a, passed)
                        for q in range(4):
                            a.dma_start(one(out, b)[:, j * RL + q:(j + 1) * RL:4, :],
                                        O[32 * q:32 * q + 32, k].rearrange("o (r w) -> o r w", w=W)).then_inc(sent[k], 16)
                for k in range(NX):
                    a.wait_ge(sent[k], 64 + 64 * B * NL // NX)


def load_weights(nc, sems, d, wt):
    with Stage(nc, sems, "wt") as s:
        dsc = s.sb("dsc", [C, 2, K9, 4 * C])
        fus = s.sb("fus", [C, 3, C])
        cw = s.sb("cw", [C, 2, 3, P])
        cb = s.sb("cb", [C, 1])
        fz = s.sb("fz", [C, 4, C])
        dwv = s.sb("dwv", [P, 4, 3])
        idm = s.sb("idm", [P, C])
        fT = s.sb("fT", [12, C, P])
        cm = s.sb("cm", [12, 9])
        sel = s.sb("sel", [97, 2 * K9, P])
        ps = [s.ps(f"p{k}", [P, 512]) for k in range(5)]
        zf, zr = s.sb("zf", [P, 32 * K9]), s.sb("zr", [P, 32 * K9])
        zp = s.sb("zp", [P, 3, 32 * K9], BF16)
        grid = s.sb("grid", [P, NCH, 512])
        c_in, made, zeroed, cut = s.sem("c_in"), s.sem("made"), s.sem("zeroed"), s.sem("cut")
        multiplied = [(dsc[:].rearrange("m a k c -> m (a k c)"), d["dsc"]), (fus[:].rearrange("m g o -> m (g o)"), d["fusT"]),
                      (cw[:].rearrange("m p x c -> m (p x c)"), d["convw"]), (cb[:], d["conv_b"]),
                      *((fz[:, q, :], d["fusT"][:, 0:C]) for q in range(4)),
                      (fT[:].rearrange("f o i -> f (o i)"), d["freqT"]), (cm[:], d["freq_to_taps"])]
        others = [(sel[:].rearrange("r k p -> r (k p)"), d["select"]), (grid[:].rearrange("p j n -> p (j n)"), d["grid"]),
                  (dwv[:].rearrange("p a x -> p (a x)"), d["dw"]), (idm[:], d["idm"])]
        kept = [(wt[n][:], d[n]) for n in ("bd", "share2", "pw", "pb", "share", "gb1", "gbo", "gbf", "eye", "pick")]
        m_in = s.sem("m_in")
        with s.block() as block:
            @block.sync
            def _(sp):
                for dst, src in multiplied:
                    sp.dma_start(dst, src).then_inc(m_in, 16)
                for dst, src in others:
                    sp.dma_start(dst, src).then_inc(c_in, 16)

            @block.gpsimd
            def _(g):
                g.memset(wt["L3"][:], 0.0).then_inc(zeroed, 1)

            @block.tensor
            def _(pe):
                pe.wait_ge(m_in, 16 * len(multiplied))
                pe.wait_ge(zeroed, 1)
                for a in range(2):
                    for k in range(K9):
                        mm = pe.matmul(ps[a][:, 32 * k:32 * k + 32], dsc[:, a, k, :], fus[:, 2 - a, :], start=True, stop=True)
                for x in range(3):
                    for p in range(2):
                        pe.matmul(ps[2][:, 64 * x + 32 * p:64 * x + 32 * p + 32], cw[:, p, x, :], fus[:, 0, :], start=True, stop=True)
                pe.matmul(ps[3][:, 0:1], fz[:].rearrange("m q o -> m (q o)"), cb[:], start=True, stop=True)
                for o in range(C):
                    mm = pe.matmul(ps[4][:, 9 * o:9 * o + 9], fT[:, o, :], cm[:], start=True, stop=True)
                mm.then_inc(made, 1)

            @block.vector
            def _(v):
                v.wait_ge(made, 1)
                ch = Chain(v, cut)
                for a in range(2):
                    n = 32 * K9
                    ch.done(v.tensor_scalar(zf[:], ps[a][:, 0:n], -1.0, None, ALU.mult))
                    ch.sync()
                    ch.done(v.tensor_copy(zp[:, 0], zf[:]))
                    ch.sync()
                    ch.done(v.tensor_tensor(zr[:], zf[:], zp[:, 0], ALU.subtract))
                    ch.sync()
                    ch.done(v.tensor_copy(zp[:, 1], zr[:]))
                    ch.sync()
                    ch.done(v.tensor_tensor(zp[:, 2], zr[:], zp[:, 1], ALU.subtract))
                    ch.sync()
                    for x, part in enumerate((0, 0, 0, 1)):
                        r = slice(32 * x, 32 * x + 32)
                        ch.done(v.tensor_copy(wt["Z"][r, a, 0], zp[r, part]))
                    for x, part in enumerate((2, 1, 1)):
                        r = slice(32 * x, 32 * x + 32)
                        ch.done(v.tensor_copy(wt["Z"][r, a, 1], zp[r, part]))
                    ch.done(v.memset(wt["Z"][96:128, a, 1], 0.0))
                    ch.sync()
                v.wait_ge(c_in, 16 * len(others + kept))
                v.tensor_copy(wt["LP"][:].rearrange("p x o -> p (x o)"), ps[2][:, 0:192])
                for x in range(3):
                    for pa in range(4):
                        v.tensor_scalar(wt["LD"][:, x, 32 * pa:32 * pa + 32], idm[:], dwv[:, pa, x:x + 1], None, ALU.mult)
                v.tensor_copy(wt["bp"][:], ps[3][:, 0:1])
                for q in range(4):
                    for t in range(2):
                        if 0 <= q - t <= 2:
                            dy = q - t
                            src = ps[4][32 * q:32 * q + 32, 0:288].rearrange("i (o y x) -> i y x o", y=3, x=3)[:, dy]
                            v.tensor_copy(wt["L3"][32 * q:32 * q + 32, :, 32 * t:32 * t + 32], src)

            @block.scalar
            def _(a):
                for dst, src in kept:
                    a.dma_start(dst, src).then_inc(c_in, 16)
                a.wait_ge(c_in, 16 * len(others + kept))
                a.activation(wt["sel"][:], sel[:], ACT.Copy)
                a.activation(wt["grid"][:], grid[:], ACT.Copy)


LINES = 32
PAIRS = [(0, 1), (2, 3), (4, 5), (6, 7), (8,)]


def deformable(nc, sems, hs, up, xp, coef, wt, uy, u, st):
    with Stage(nc, sems, "df") as s:
        XP = s.sb("xp", [P, PX], BF16)
        IX = s.sb("ix", [97, PX], BF16)
        HI = s.sb("hi", [64, 2, RC * W])
        t_ix, t_r, t_r2 = (s.sb(n, [P, 512]) for n in ("t_ix", "t_r", "t_r2"))
        parts = s.sb("parts", [P, 2, 3, 512], BF16)
        Zs = s.sb("zs", [P, 2, 4, 32 * K9])
        L = len(PAIRS)
        T = s.sb("t", [P, L, 1024])
        YB = s.sb("yb", [P, C * W])
        U = s.sb("u", [P, LINES, W])
        XO = s.sb("xo", [P, 2, P])
        ps_d = [s.ps(f"d{k}", [P, 1024]) for k in range(2)]
        ps_z = s.ps("z", [P, 512])
        ps_f = s.ps("f", [P, 512])
        ps_o = [s.ps(f"o{k}", [P, 512]) for k in range(2)]
        passed, ones = s.sem("passed"), s.sem("ones")
        h_in, p_out = ([s.sem(f"{n}{k}") for k in range(2)] for n in ("h_in", "p_out"))
        relu, off_full, split, xp_in = s.sem("relu"), s.sem("off_full"), s.sem("split"), s.sem("xp_in")
        z_full, z_read = s.sem("z_full"), s.sem("z_read")
        d_full, d_read = s.sem("d_full"), s.sem("d_read")
        hat, t_used = s.sem("hat"), s.sem("t_used")
        o_read = s.sem("o_read")
        turned, y_read = s.sem("turned"), s.sem("y_read")
        u_in, uy_out, uy_in, u_out = (s.sem(n) for n in ("u_in", "uy_out", "uy_in", "u_out"))
        summed, counted = s.sem("summed"), s.sem("counted")
        S = 2 * LINES
        SC = LINES // NCH
        CHN = 6

        with s.block() as block:
            @block.sync
            def _(sp):
                def load(b, c):
                    sp.wait_ge(off_full, b * NCH + c + 1)
                    alone(sp, passed)
                    for p in range(2):
                        sp.dma_start(HI[:, c % 2].rearrange("c (i p w) -> c i p w", p=2, w=W)[:, :, p, :],
                                     one(hs, b)[64 * p:64 * p + 64, c * RC // 2 * W:(c + 1) * RC // 2 * W]
                                     .rearrange("c (i w) -> c i w", w=W)).then_inc(h_in[c % 2], 16)

                def place(b, c, over):
                    k = c % 2
                    if over:
                        sp.wait_ge(d_full, ((b - 1) * S + LINES + SC * (c + 1)) * L)
                        alone(sp, passed)
                    sp.wait_ge(split, CHN * (b * NCH + c + 2))
                    alone(sp, passed)
                    for part in range(3):
                        for q in range(4):
                            px = c * RC * W + 512 * q
                            sp.dma_start(IX[32 * part:32 * part + 32, px:px + 512],
                                         parts[32 * q:32 * q + 32, k, part, :]).then_inc(p_out[k], 16)

                def image(b, over):
                    for c in range(NCH):
                        load(b, c)
                        if c >= 2:
                            place(b, c - 2, over)
                    for c in (NCH - 2, NCH - 1):
                        place(b, c, over)

                sp.wait_ge(ones, 1)
                with sp.Fori(0, 1) as b:
                    image(b, False)
                with sp.Fori(1, B) as b:
                    image(b, True)

            @block.gpsimd
            def _(g):
                def take(b, c):
                    g.dma_start(XP[:, c * RC * W:(c + 1) * RC * W], one(xp, b)[:, c * RC * W:(c + 1) * RC * W]).then_inc(xp_in, 16)

                def finish(b, c):
                    r = slice(SC * c * W, SC * (c + 1) * W)
                    g.wait_ge(o_read, b * S + LINES + SC * (c + 1) + 2)
                    alone(g, passed)
                    g.tensor_tensor(U[:].rearrange("p j w -> p (j w)")[:, r], U[:].rearrange("p j w -> p (j w)")[:, r],
                                    YB[:, r], ALU.add).then_inc(summed, 1)
                    g.wait_ge(summed, b * NCH + c + 1)
                    alone(g, passed)
                    g.dma_start(one(u, b).rearrange("q o j w -> (q o) (j w)")[:, r],
                                U[:].rearrange("p j w -> p (j w)")[:, r]).then_inc(u_out, 16)

                def image(b, more):
                    g.dma_start(U[:].rearrange("p j w -> p (j w)"), one(up, b)).then_inc(u_in, 16)
                    g.wait_ge(y_read, (b + 1) * LINES + 2)
                    alone(g, passed)
                    for q in range(4):
                        g.dma_start(one(uy, b).rearrange("o h w -> h o w")[:, 8 * q:8 * q + 8], YB[:, 8 * W * q:8 * W * (q + 1)].rearrange("p (o w) -> p o w", w=W)).then_inc(uy_out, 16)
                    g.wait_ge(uy_out, b * 64 + 64)
                    alone(g, passed)
                    for q in range(4):
                        r = slice(32 * q, 32 * q + 32)
                        g.dma_start(YB[r].rearrange("o (j w) -> o j w", w=W), one(uy, b).rearrange("o (j q) w -> q o j w", q=4)[q]).then_inc(uy_in, 16)
                    for c in range(NCH):
                        if more:
                            g.wait_ge(z_full, 4 * (b * S + LINES + SC * (c + 1)))
                            alone(g, passed)
                            take(b + 1, c)
                        if c == 0:
                            g.wait_ge(uy_in, 64 * (b + 1))
                            alone(g, passed)
                        else:
                            finish(b, c - 1)
                    finish(b, NCH - 1)
                    g.wait_ge(u_out, 16 * NCH * (b + 1))
                    alone(g, passed)
                    g.wait_ge(counted, NCH * (b + 1))
                    alone(g, passed)

                g.memset(IX[96:97], 1.0).then_inc(ones, 1)
                for c in range(NCH):
                    g.wait_ge(relu, c + 1)
                    g.dma_start(XP[:, c * RC * W:(c + 1) * RC * W], xp[0][:, c * RC * W:(c + 1) * RC * W]).then_inc(xp_in, 16)
                with g.Fori(0, B - 1) as b:
                    image(b, True)
                with g.Fori(B - 1, B) as b:
                    image(b, False)

            @block.scalar
            def _(act):
                act.sem_inc(d_read, 2)

                def branch(b, c):
                    k = c % 2
                    act.wait_ge(h_in[k], 32 * (b * (NCH // 2) + c // 2 + 1))
                    act.activation(HI[:, k], HI[:, k], ACT.Relu, bias=coef[0:64, 1:2], scale=coef[0:64, 0:1]).then_inc(relu, 1)

                def distances(n, k):
                    for e, pts in enumerate(PAIRS):
                        w = 512 * len(pts)
                        act.wait_ge(t_used, n * L + e + 1)
                        act.wait_ge(d_full, n * L + e + 1)
                        act.activation(T[:, e, 0:w], ps_d[(k * L + e) % 2][:, 0:w], ACT.Abs).then_inc(d_read, 1)

                def image(b, more):
                    with act.Fori(0, LINES // 2) as i:
                        for k in range(2):
                            distances(b * S + 2 * i + k, k)
                    if more:
                        branch(b + 1, 0)
                    for c in range(NCH):
                        for t in range(SC):
                            distances(b * S + LINES + SC * c + t, t % 2)
                            if t == 2 and more and c + 1 < NCH:
                                branch(b + 1, c + 1)

                for c in range(NCH):
                    branch(0, c)
                with act.Fori(0, B - 1) as b:
                    image(b, True)
                with act.Fori(B - 1, B) as b:
                    image(b, False)

            @block.vector
            def _(v):
                v.sem_inc(z_read, 1)
                v.sem_inc(o_read, 2)
                v.sem_inc(y_read, 2)
                v.sem_inc(split, CHN)

                def offsets(b, c):
                    k = c % 2
                    g = b * NCH + c
                    ch = Chain(v, split, CHN * (g + 1))
                    v.wait_ge(off_full, g + 3)
                    ch.done(v.scalar_tensor_tensor(out=t_ix[:], in0=ps_f[:], scalar=wt["pb"][:, 0:1],
                                                   in1=wt["grid"][:, c, :], op0=ALU.add, op1=ALU.add))
                    yield
                    ch.sync()
                    if not (isinstance(b, int) and c < 2):
                        v.wait_ge(p_out[k], 192 * (b * (NCH // 2) + c // 2))
                    ch.done(v.tensor_copy(parts[:, k, 0], t_ix[:]))
                    yield
                    ch.sync()
                    ch.done(v.tensor_tensor(t_r[:], t_ix[:], parts[:, k, 0], ALU.subtract))
                    yield
                    ch.sync()
                    ch.done(v.tensor_copy(parts[:, k, 1], t_r[:]))
                    yield
                    ch.sync()
                    ch.done(v.tensor_tensor(t_r2[:], t_r[:], parts[:, k, 1], ALU.subtract))
                    yield
                    ch.sync()
                    ch.done(v.tensor_copy(parts[:, k, 2], t_r2[:]))
                    yield

                def read_z(n, k, q):
                    if q == 0:
                        v.wait_ge(t_used, L * n + 1)
                    v.wait_ge(z_full, 4 * n + q + 1)
                    v.tensor_copy(Zs[:, k, q], ps_z[:, 0:32 * K9]).then_inc(z_read, 1)

                def read_o(a, n, j, k):
                    v.wait_ge(t_used, L * n + 2 * L)
                    if a == 0:
                        v.tensor_copy(XO[:, k], ps_o[k][:, 0:P]).then_inc(o_read, 1)
                    else:
                        uj = U[:, bass.ds(j, 1), :].rearrange("p j w -> p (j w)")
                        v.tensor_tensor(uj, ps_o[k][:, 0:P], uj, ALU.add).then_inc(o_read, 1)

                def keep_columns(b, j, k):
                    v.wait_ge(turned, b * LINES + j + 1)
                    v.tensor_copy(YB[:].rearrange("h (o q w) -> h q o w", q=4, w=LINES)[:, :, :, bass.ds(j, 1)].rearrange("h q o w -> h q (o w)"),
                                  ps_o[k][:, P:2 * P].rearrange("h (q o) -> h q o", q=4)).then_inc(y_read, 1)

                def step(b, a, j, k, first=False, last=False, side=None, counts=None):
                    n = b * S + a * LINES + j
                    pa, pj = (0, LINES - 1) if a == 1 and first else (a, j - 1)
                    behind = not (a == 0 and first)
                    for e, pts in enumerate(PAIRS):
                        w = 512 * len(pts)
                        v.wait_ge(d_read, n * L + e + 3)
                        v.tensor_scalar(T[:, e, 0:w], T[:, e, 0:w], 1.0, 1.0, ALU.min, ALU.subtract).then_inc(hat, 1)
                        if e == 0 and behind:
                            read_o(pa, n - 1, pj, 1 - k)
                        if e >= 1 and not (a == 1 and last):
                            read_z(n + 1, 1 - k, e - 1)
                        if e == 3 and counts is not None:
                            stats(b, counts)
                        if e == 3 and behind and pa == 0:
                            keep_columns(b, pj, 1 - k)
                        if e in (2, 4) and side:
                            next(side, None)

                def stats(b, c):
                    v.wait_ge(summed, b * NCH + c + 1)
                    v.bn_stats(st[:, bass.ds(b * NCH + c, 1), :].rearrange("p a s -> p (a s)"),
                               U[:, SC * c:SC * (c + 1), :].rearrange("p j w -> p (j w)")).then_inc(counted, 1)

                def image(b, more):
                    for q in range(4):
                        read_z(b * S, 0, q)
                    step(b, 0, 0, 0, first=True)
                    step(b, 0, 1, 1)
                    with v.Fori(1, LINES // 2 - 1) as i:
                        for k in range(2):
                            step(b, 0, 2 * i + k, k)
                    step(b, 0, LINES - 2, 0)
                    step(b, 0, LINES - 1, 1, last=True)
                    v.wait_ge(u_in, 16 * (b + 1))
                    for c in range(NCH):
                        side = offsets(b + 1, c) if more else None
                        for t in range(SC):
                            j = SC * c + t
                            step(b, 1, j, t % 2, first=(j == 0), last=(j == LINES - 1), side=side if t else None,
                                 counts=c - 2 if c >= 2 and t == 2 else None)
                    read_o(1, b * S + S - 1, LINES - 1, 1)
                    stats(b, NCH - 2)
                    stats(b, NCH - 1)

                for c in range(NCH):
                    for _ in offsets(0, c):
                        pass
                with v.Fori(0, B - 1) as b:
                    image(b, True)
                with v.Fori(B - 1, B) as b:
                    image(b, False)

            @block.tensor
            def _(pe):
                pe.sem_inc(off_full, 2)
                pe.sem_inc(t_used, L)
                pe.wait_ge(ones, 1)

                def branch(b, c):
                    g = b * NCH + c
                    pe.wait_ge(relu, g + 1)
                    pe.wait_ge(split, CHN * g + 1)
                    alone(pe, passed)
                    for q in range(4):
                        mm = pe.matmul(ps_f[32 * q:32 * q + 32, :], wt["pw"][:], HI[:, c % 2, 512 * q:512 * q + 512],
                                       start=True, stop=True)
                    mm.then_inc(off_full, 1)

                def spread(a, n, j, k, e):
                    pe.wait_ge(d_read, n * L + e + 1)
                    if a == 0:
                        ix = IX[:].rearrange("r (h q w) -> r q h w", q=4, w=LINES)[:, :, :, bass.ds(j, 1)].rearrange("r q h w -> r q (h w)")
                    else:
                        ix = IX[:, bass.ds(j * (4 * W), 4 * W)]
                    for x, pt in enumerate(PAIRS[e]):
                        mm = pe.matmul(ps_d[(k * L + e) % 2][:, 512 * x:512 * x + 512], wt["sel"][:, K9 * a + pt, :], ix,
                                       start=True, stop=True)
                    mm.then_inc(d_full, 1)

                def make_z(a, n, j, q):
                    pe.wait_ge(z_read, 4 * n + q + 1)
                    alone(pe, passed)
                    if a == 0:
                        line = XP[:].rearrange("c (h w) -> c h w", w=W)[:, :, bass.ds(j + LINES * q, 1)].rearrange("c h w -> c (h w)")
                    else:
                        line = XP[:, bass.ds((j * 4 + q) * W, W)]
                    for x in range(2):
                        mm = pe.matmul(ps_z[:, 0:32 * K9], line, wt["Z"][:, a, x, :], start=(x == 0), stop=(x == 1))
                    mm.then_inc(z_full, 1)

                def apply(a, b, n, j, k, e, first):
                    if e == 0:
                        pe.wait_ge(z_read, 4 * n + 5)
                        pe.wait_ge(o_read, n + 1)
                        if a == 0:
                            pe.wait_ge(y_read, b * LINES + j + 1)
                        elif first:
                            pe.wait_ge(y_read, (b + 1) * LINES + j + 1)
                    pe.wait_ge(hat, n * L + e + 1)
                    for x, pt in enumerate(PAIRS[e]):
                        for q in range(4):
                            c = 512 * x + 128 * q
                            mm = pe.matmul(ps_o[k][32 * q:32 * q + 32, 0:P], Zs[:, k, q, 32 * pt:32 * pt + 32], T[:, e, c:c + 128],
                                           start=(pt == 0), stop=(pt == K9 - 1))
                    mm.then_inc(t_used, 1)

                def turn(n, k):
                    pe.wait_ge(o_read, n + 3)
                    alone(pe, passed)
                    pe.transpose(ps_o[k][:, P:2 * P], XO[:, k], wt["eye"][:]).then_inc(turned, 1)

                def step(b, a, j, k, first=False, last=False, head=False):
                    n = b * S + a * LINES + j
                    nxt = (a, j + 1) if not last else (1, 0) if a == 0 else None
                    for e in range(L):
                        if e + 2 < L:
                            spread(a, n, j, k, e + 2)
                        elif nxt:
                            spread(nxt[0], n + 1, nxt[1], 1 - k, e + 2 - L)
                        apply(a, b, n, j, k, e, head)
                        if e < 4 and nxt:
                            make_z(nxt[0], n + 1, nxt[1], e)
                        if e == 1 and (first if a else not first):
                            turn(n - 1, 1 - k)

                def image(b, more):
                    pe.wait_ge(xp_in, 16 * NCH * (b + 1))
                    alone(pe, passed)
                    for q in range(4):
                        make_z(0, b * S, 0, q)
                    for k in range(2):
                        pe.wait_ge(p_out[k], 192 * (NCH // 2) * (b + 1))
                    alone(pe, passed)
                    for e in range(2):
                        spread(0, b * S, 0, 0, e)
                    step(b, 0, 0, 0, first=True)
                    step(b, 0, 1, 1)
                    with pe.Fori(1, LINES // 2 - 1) as i:
                        for k in range(2):
                            step(b, 0, 2 * i + k, k)
                    step(b, 0, LINES - 2, 0)
                    step(b, 0, LINES - 1, 1, last=True)
                    for c in range(NCH):
                        for t in range(SC):
                            j = SC * c + t
                            step(b, 1, j, t % 2, first=(j == 0), last=(j == LINES - 1), head=(j < 2))
                            if t == 0 and more:
                                branch(b + 1, c)

                for c in range(NCH):
                    branch(0, c)
                with pe.Fori(0, B - 1) as b:
                    image(b, True)
                with pe.Fori(B - 1, B) as b:
                    image(b, False)


def dft_constants():
    two_pi = 2 * np.pi
    kx = np.concatenate([np.arange(M1), np.arange(H - M1, H)])
    h = np.arange(H)
    ang = two_pi * ((h[:, None] * kx[None]) % H) / H
    dft_h = np.stack([-np.sin(ang), np.cos(ang), np.sin(ang)], 2).reshape(H, -1)
    aw = two_pi * ((np.arange(W)[:, None] * np.arange(M2)[None]) % W) / W
    dft_wp = np.concatenate([np.cos(aw), -np.sin(aw)], 1)
    dft_wq = np.concatenate([np.sin(aw), np.cos(aw)], 1)
    kp = np.array([2 * j + par + hl * (H - M1) for hl in range(2) for par in range(2) for j in range(M1 // 2)])
    ah = two_pi * ((kp[:, None] * h[None]) % H) / H
    inv_hr = np.concatenate([np.cos(ah), -np.sin(ah)], 0)
    inv_hi = np.concatenate([np.sin(ah), np.cos(ah)], 0)
    cy = np.where(np.arange(M2) == 0, 1.0, 2.0)[:, None] / (H * W)
    inv_w = np.tile(np.concatenate([cy * np.cos(aw.T), -cy * np.sin(aw.T)], 0), (2, 1))
    return dict(
        dft_h=dft_h, dft_wp=dft_wp, dft_wq=dft_wq, inv_hr=inv_hr, inv_hi=inv_hi, inv_w=inv_w,
        avg=np.full((P, P), 1.0 / P))


def weight_layouts(inp):
    f = lambda a: np.ascontiguousarray(a, np.float32)
    c = lambda n: np.asarray(inp["L2_conv_" + n])
    fus = c("fus_w")[:, :, 0, 0]
    out = {}
    out["fusT"] = f(fus.reshape(C, 3, C).transpose(2, 1, 0)).reshape(C, 3 * C)
    dsc = np.stack([c("dscy_w"), c("dscx_w")]).transpose(1, 0, 3, 2)
    out["dsc"] = f(np.tile(dsc, (1, 1, 1, 4))).reshape(C, -1)
    cw = np.zeros((C, 2, 3, 4, C))
    dw = np.stack([c("offx_dw_w")[:, 0], c("offy_dw_w")[:, 0]])
    dwp = np.zeros((4, C, 2, 2, 3))
    for p in range(2):
        cw[:, p, :, p:p + 3] = c("conv_w").transpose(0, 3, 2, 1)
        dwp[p:p + 3, :, p] = dw.transpose(2, 1, 0, 3)
    out["convw"], out["dw"] = f(cw.reshape(C, -1)), f(dwp.reshape(P, 12))
    out["conv_b"] = f(c("conv_b").reshape(C, 1))
    out["bd"] = f(np.tile(np.concatenate([c("offx_dw_b"), c("offy_dw_b")]), 2)[:, None])
    pw = np.zeros((64, 32))
    pw[0:32, 0:K9] = c("offx_pw_w")[:, :, 0, 0].T
    pw[32:64, K9:2 * K9] = c("offy_pw_w")[:, :, 0, 0].T
    out["pw"] = f(pw)
    pb = np.zeros(32)
    pb[0:K9], pb[K9:2 * K9] = c("offx_pw_b"), c("offy_pw_b")
    out["pb"] = f(np.tile(pb, 4)[:, None])
    out["gbo"] = f(np.tile(np.stack([np.concatenate([c("offx_bn_g"), c("offy_bn_g")]),
                                     np.concatenate([c("offx_bn_b"), c("offy_bn_b")])], 1), (2, 1)))
    out["gbf"] = f(np.tile(np.stack([c("fus_bn_g"), c("fus_bn_b")], 1), (4, 1)))
    out["gb1"] = f(np.tile(np.stack([inp["L1_conv_gamma"], inp["L1_conv_beta"]], 1), (4, 1)))
    w1 = np.asarray(inp["L1_conv_conv_w"])[:, :, :, 0]
    l1 = np.zeros((4, C, 2, C))
    for t in range(2):
        l1[t:t + 3, :, t] = w1.transpose(2, 1, 0)
    out["l1_w"] = f(l1.reshape(P, 2 * C))
    out["l1_b"] = f(np.tile(inp["L1_conv_conv_b"], 4)[:, None])
    fr = np.asarray(inp["L3_conv_freq_weight"]).reshape(C, C, 12)
    out["freqT"] = f(np.tile(fr.transpose(2, 0, 1), (1, 1, 4))).reshape(12, -1)
    return out


def shape_constants():
    out = dft_constants()
    p = np.arange(P)
    out["share"] = (p[:, None] % 32 == p[None] % 32) / 4.0
    out["pair"] = ((p[:, None] % 32) // 2 == (p[None] % 32) // 2) / 8.0
    out["eye"] = np.eye(P)
    out["pick"] = np.eye(P)[:, C:3 * C]
    out["share2"] = (p[:, None] % 64 == p[None] % 64) / 2.0
    out["idm"] = (np.arange(P)[:, None] % 32 == np.arange(32)[None]) * 1.0
    sel = np.zeros((97, 2 * K9, P))
    for a in range(2):
        for k in range(K9):
            for part in range(3):
                sel[32 * part + (K9 if a == 0 else 0) + k, K9 * a + k] = 1.0
    sel[96] = -np.arange(P)
    out["select"] = sel.reshape(97, -1)
    grid = np.zeros((4, 32, NCH, 4, W))
    grid[:, 0:K9] = np.arange(W)
    rows = RC * np.arange(NCH)[None, :, None] + 4 * np.arange(4)[:, None, None] + np.arange(4)[None, None, :]
    grid[:, K9:2 * K9] = rows[:, None, :, :, None]
    out["grid"] = grid.reshape(P, -1)
    out["freq_to_taps"] = freq_to_taps()
    return {k: np.ascontiguousarray(v, np.float32) for k, v in out.items()}


def freq_to_taps():
    K = 3
    basis = np.zeros((12, K, 2), complex)
    for f in range(12):
        basis[f, f // 4, (f // 2) % 2] = 1.0 if f % 2 == 0 else 1j
    kern = np.fft.irfft2(basis, s=(K, K), axes=(-2, -1)).astype(np.float32)
    th = np.array([i * np.pi / 4 for i in range(8)], np.float32)[:, None]
    sc = np.array([1.0, 1.25, 1.25 ** 2, 1.25 ** 3], np.float32)[None]
    cos_t, sin_t = (np.cos(th) * sc).reshape(-1), (np.sin(th) * sc).reshape(-1)
    co = ((2 * np.arange(K, dtype=np.float32) + 1) / np.float32(K) - 1).astype(np.float32)
    gy, gx = np.meshgrid(co, co, indexing="ij")
    out = np.zeros((12, K, K))
    for c, s in zip(cos_t, sin_t):
        ix = (((c * gx - s * gy) + 1) * K - 1) * np.float32(0.5)
        iy = (((s * gx + c * gy) + 1) * K - 1) * np.float32(0.5)
        x0, y0 = np.floor(ix).astype(int), np.floor(iy).astype(int)
        wx1, wy1 = ix - x0, iy - y0
        for yy, wy in ((y0, 1 - wy1), (y0 + 1, wy1)):
            for xx, wx in ((x0, 1 - wx1), (x0 + 1, wx1)):
                ok = (xx >= 0) & (xx < K) & (yy >= 0) & (yy < K)
                out += np.where(ok, kern[:, np.clip(yy, 0, K - 1), np.clip(xx, 0, K - 1)], 0) * (wy * wx)
    return (out / len(cos_t)).reshape(12, 9)


def network(nc, x, w, d, out):
    dram = lambda name, shape: nc.dram_tensor(name, shape, F32).ap()
    spec = dram("spec", (M1 // 2, P, 2 * M2 * B))
    gstat = dram("gstat", (B, 1, 4 * B))
    x1, x2, x3 = (dram(f"x_{n}", (B, C, H, W)) for n in (1, 2, 3))
    y1 = dram("y_1", (B, P, NCH, 512))
    hs = dram("branches", (B, P, PX // 2))
    up = dram("plain", (B, P, PX // 4))
    xp = nc.dram_tensor("parts", (B, P, PX), BF16).ap()
    uy = dram("u_y", (B, C, H, W))
    u = dram("u", (B, 4, C, LINES, W))
    with ExitStack() as sems, Stage(nc, sems, "net") as s:
        with Stage(nc, sems, "l0") as s0:
            F = s0.sb("f", [P, M1 * M2, 2, B])
            spectral_forward(nc, sems, x, d, F)
            spectral_mix(nc, sems, w, F, spec)
        spectral_inverse(nc, sems, x, spec, d, d["l0_bias"], x1, gstat)
        layer_rest(nc, sems, s, d, (spec, gstat, x1, x2, x3, y1, hs, up, xp, uy, u), out)


def layer_rest(nc, sems, s, d, bufs, out):
    spec, gstat, x1, x2, x3, y1, hs, up, xp, uy, u = bufs
    wt = {n: s.sb(n, sh, dt) for n, sh, dt in (
        ("grid", [P, NCH, 512], BF16), ("pw", [64, 32], F32), ("pb", [P, 1], F32), ("share", [P, P], F32),
        ("gb1", [P, 2], F32), ("gbo", [P, 2], F32), ("share2", [P, P], F32), ("gbf", [P, 2], F32), ("eye", [P, P], F32), ("pick", [P, 2 * C], F32),
        ("Z", [P, 2, 2, 32 * K9], BF16), ("LD", [P, 3, P], F32), ("LP", [P, 3, 2 * C], F32), ("bd", [P, 1], F32), ("bp", [P, 1], F32), ("L3", [P, 3, 64], F32),
        ("sel", [97, 2 * K9, P], BF16))}
    GS = s.sb("GS", [P, 2, B])
    st1, sto, stf = s.sb("st1", [P, B * NCH, 6]), s.sb("sto", [P, B * NCH * 2, 6]), s.sb("stf", [P, B * 8, 6])
    co1, coo, cof = s.sb("co1", [P, 2]), s.sb("coo", [P, 2]), s.sb("cof", [P, 2])
    mod4 = lambda t: t.rearrange("b c (h q) w -> b q c h w", q=4)
    load_weights(nc, sems, d, wt)
    graph_conv(nc, sems, x1, gstat, wt, d, y1, st1)
    norm_coefficients(nc, sems, "n1", st1, P, wt["share"][:], wt["gb1"], co1)
    residual_norm(nc, sems, "r1", y1.rearrange("b p j n -> b p (j n)"), co1, mod4(x1), mod4(x2), d["pair"], GS)
    depth_conv(nc, sems, x2, GS, wt, hs, up, xp, sto)
    norm_coefficients(nc, sems, "no", sto, P, wt["share2"][:], wt["gbo"], coo)
    deformable(nc, sems, hs, up, xp, coo, wt, uy, u, stf)
    norm_coefficients(nc, sems, "nf", stf, P, wt["share"][:], wt["gbf"], cof)
    residual_norm(nc, sems, "r2", u.rearrange("b q o h w -> b (q o) (h w)"), cof, mod4(x2), mod4(x3), d["pair"], GS)
    last_conv(nc, sems, x3, GS, wt["L3"], wt["pick"][:], out)


def kernel(**inputs):
    import concourse.bacc as _bacc
    from concourse.bass_utils import run_bass_kernel_spmd as _run

    nc = _bacc.Bacc("TRN2", target_bir_lowering=False, num_devices=1)
    arrays = {}

    def given(name, a):
        a = np.ascontiguousarray(a)
        arrays[f"in_{name}"] = a
        return nc.dram_tensor(f"in_{name}", a.shape, mybir.dt.from_np(a.dtype), kind="ExternalInput").ap()

    x = given("x", inputs["x"])
    w = [given(n, inputs["L0_conv_" + n]) for n in ("w1r", "w1i", "w2r", "w2i")]
    d = {n: given(n, a) for n, a in {**weight_layouts(inputs), **shape_constants()}.items()}
    d["l0_bias"] = given("l0_bias", np.asarray(inputs["L0_conv_bias"]).reshape(1, C))
    d["l1_A"] = given("l1_A", inputs["L1_conv_A"])
    out = nc.dram_tensor("out_0", (B, C, H, W), F32, kind="ExternalOutput").ap()
    network(nc, x, w, d, out)
    r = _run(nc, [arrays], core_ids=[0])
    return r.results[0]["out_0"]
```
